# Optimizing a Trainium2 kernel written in Bass

```python
import numpy as np
import jax
import jax.numpy as jnp

def _softmax(x, axis=-1):
    return jax.nn.softmax(x, axis=axis)

def _gelu(x):
    return jax.nn.gelu(x, approximate=True)

def _silu(x):
    return jax.nn.silu(x)

def _sigmoid(x):
    return jax.nn.sigmoid(x)

def _layernorm(x, axis=-1, eps=1e-05):
    m = jnp.mean(x, axis=axis, keepdims=True)
    v = jnp.var(x, axis=axis, keepdims=True)
    return (x - m) / jnp.sqrt(v + eps)

def _scatter_add(tgt, idx, src, axis=0):
    return tgt.at[idx].add(src)

def _segment_sum(src, seg, n):
    return jax.ops.segment_sum(src, seg, n)
kernel_name = 'mk_flamingo_gated_d1_seqx_r8_f0e491'

def setup_inputs(seed: int=0):
    np.random.seed(seed)
    _w = jnp.asarray

    def _rec_inputs():
        import jax
        import jax.numpy as jnp
        _rk = jax.random.key(seed)
        x = 7.22e-05 + 1 * jax.random.normal(jax.random.fold_in(_rk, 1), (4, 256, 256), jnp.float32)
        _lenS = 256 - jax.random.randint(jax.random.fold_in(_rk, 7), (4,), 0, max(1, 256 // 4) + 1, jnp.int32)
        _lenS2 = 256 - jax.random.randint(jax.random.fold_in(_rk, 8), (4,), 0, max(1, 256 // 4) + 1, jnp.int32)
        _ctx_512P = jax.random.normal(jax.random.fold_in(_rk, 11), (4, 16, 64), jnp.float32)
        _ctx_512c = jax.random.dirichlet(jax.random.fold_in(_rk, 511), 0.3 * jnp.ones((16,), jnp.float32), (4, 256))
        _ctx_512t = jnp.einsum('bsk,bkd->bsd', _ctx_512c, _ctx_512P)
        _ctx_512t = _ctx_512t * jax.lax.rsqrt(jnp.mean(jnp.square(_ctx_512t)) + 1e-12) * 0.953939
        ctx_512 = -0.000514642 + 1.00011 * (_ctx_512t + 0.3 * jax.random.normal(jax.random.fold_in(_rk, 611), (4, 256, 64), jnp.float32))
        _g = jax.random.normal(jax.random.fold_in(_rk, 9001), (2, 1), jnp.float32)
        _g = jnp.sign(_g) * jnp.maximum(jnp.abs(_g), 1.0) + (_g == 0) * 1.0
        g_xattn = _g[0]
        g_ffn = _g[1]
        return (x, ctx_512, g_xattn, g_ffn)
    x, ctx_512, g_xattn, g_ffn = _rec_inputs()

    def _L0_xattn_setup():
        import jax, jax.numpy as jnp
        import numpy as np
        N_HEADS = 16
        N_KV_HEADS = 4
        ROPE_THETA = 10000.0
        EPS = 1e-05

        def _rms_norm(x, w):
            var = jnp.mean(x * x, axis=-1, keepdims=True)
            return x * jax.lax.rsqrt(var + EPS) * w

        def _rope_sin_cos(T, head_dim, dtype):
            inv_freq = 1.0 / ROPE_THETA ** (jnp.arange(0, head_dim, 2, dtype=jnp.float32) / head_dim)
            t = jnp.arange(T, dtype=jnp.float32)
            freqs = jnp.outer(t, inv_freq)
            emb = jnp.concatenate([freqs, freqs], -1)
            return (jnp.sin(emb).astype(dtype)[None, None], jnp.cos(emb).astype(dtype)[None, None])

        def _rotate_half(x):
            h = x.shape[-1] // 2
            x1, x2 = (x[..., :h], x[..., h:])
            return jnp.concatenate([-x2, x1], axis=-1)
        key = jax.random.key(seed)
        ks = jax.random.split(key, 6)
        B, T, C = (2, 256, 256)
        Ckv = C // N_HEADS * N_KV_HEADS
        return {'q': jax.random.normal(ks[0], (B, T, C), jnp.float32), 'k': jax.random.normal(ks[1], (B, T, Ckv), jnp.float32), 'v': jax.random.normal(ks[2], (B, T, Ckv), jnp.float32), 'q_norm_w': jnp.ones((C,), jnp.float32), 'k_norm_w': jnp.ones((Ckv,), jnp.float32), 'w_out': jax.random.normal(ks[3], (C, C), jnp.float32) * C ** (-0.5)}
    _L0_xattn_all = _L0_xattn_setup()
    _L0_xattn_in = {k: v for k, v in _L0_xattn_all.items() if k in ('q_norm_w', 'k_norm_w', 'w_out')}
    del _L0_xattn_all

    def _L0_ffn_setup():
        import jax, jax.numpy as jnp
        import numpy as np
        import math
        B, S, D = (2, 256, 256)
        H, HD = (16, 128)
        E, I = (4, 256)
        TOP_K = 2
        ROPE_THETA = 10000.0

        def _layernorm(x, w, b):
            mu = jnp.mean(x, axis=-1, keepdims=True)
            var = jnp.mean(jnp.square(x - mu), axis=-1, keepdims=True)
            return (x - mu) * jax.lax.rsqrt(var + 1e-05) * w + b

        def _rotate_half(x):
            x1, x2 = jnp.split(x, 2, axis=-1)
            return jnp.concatenate((-x2, x1), axis=-1)

        def _attention(h, wq, bq, wk, bk, wv, bv, wo, bo):
            b, s, _ = h.shape
            q = (h @ wq + bq).reshape(b, s, H, HD).transpose(0, 2, 1, 3)
            k = (h @ wk + bk).reshape(b, s, H, HD).transpose(0, 2, 1, 3)
            v = (h @ wv + bv).reshape(b, s, H, HD).transpose(0, 2, 1, 3)
            inv_freq = 1.0 / ROPE_THETA ** (jnp.arange(0, HD, 2, dtype=jnp.float32) / HD)
            freqs = jnp.arange(s, dtype=jnp.float32)[:, None] * inv_freq[None, :]
            emb = jnp.concatenate((freqs, freqs), axis=-1)
            cos = jnp.cos(emb)[None, None]
            sin = jnp.sin(emb)[None, None]
            q = q * cos + _rotate_half(q) * sin
            k = k * cos + _rotate_half(k) * sin
            scores = jnp.einsum('bhqd,bhkd->bhqk', q, k) / math.sqrt(HD)
            causal = jnp.tril(jnp.ones((s, s), bool))
            scores = jnp.where(causal[None, None], scores, jnp.finfo(jnp.float32).min)
            probs = jax.nn.softmax(scores.astype(jnp.float32), axis=-1).astype(q.dtype)
            out = jnp.einsum('bhqk,bhkd->bhqd', probs, v)
            out = out.transpose(0, 2, 1, 3).reshape(b, s, H * HD)
            return out @ wo + bo

        def _moe(h, w_gate, we1, be1, we2, be2):
            b, s, d = h.shape
            x = h.reshape(-1, d)
            t = x.shape[0]
            raw = jax.nn.softmax(x @ w_gate, axis=-1)
            top_vals, top_idx = jax.lax.top_k(raw, TOP_K)
            w = jax.nn.softmax(top_vals, axis=-1)
            comb = jnp.zeros((t, E), x.dtype).at[jnp.arange(t)[:, None], top_idx].add(w)
            hmid = jax.nn.gelu(jnp.einsum('td,edi->tei', x, we1) + be1[None], approximate=False)
            eout = jnp.einsum('tei,eid->ted', hmid, we2) + be2[None]
            out = jnp.einsum('te,ted->td', comb, eout)
            return out.reshape(b, s, d)
        key = jax.random.key(seed)
        ks = jax.random.split(key, 20)
        s = 0.02
        p = {'hidden_states': jax.random.normal(ks[0], (B, S, D), jnp.float32), 'wq': jax.random.normal(ks[1], (D, H * HD), jnp.float32) * s, 'bq': jnp.zeros((H * HD,), jnp.float32), 'wk': jax.random.normal(ks[2], (D, H * HD), jnp.float32) * s, 'bk': jnp.zeros((H * HD,), jnp.float32), 'wv': jax.random.normal(ks[3], (D, H * HD), jnp.float32) * s, 'bv': jnp.zeros((H * HD,), jnp.float32), 'wo': jax.random.normal(ks[4], (H * HD, D), jnp.float32) * s, 'bo': jnp.zeros((D,), jnp.float32), 'ln1_w': jnp.ones((D,), jnp.float32), 'ln1_b': jnp.zeros((D,), jnp.float32), 'ln2_w': jnp.ones((D,), jnp.float32), 'ln2_b': jnp.zeros((D,), jnp.float32), 'w_gate': jax.random.normal(ks[5], (D, E), jnp.float32) * s, 'we1': jax.random.normal(ks[6], (E, D, I), jnp.float32) * s, 'be1': jnp.zeros((E, I), jnp.float32), 'we2': jax.random.normal(ks[7], (E, I, D), jnp.float32) * s, 'be2': jnp.zeros((E, D), jnp.float32)}
        return p
    _L0_ffn_all = _L0_ffn_setup()
    _L0_ffn_in = {k: v for k, v in _L0_ffn_all.items() if k in ('wq', 'bq', 'wk', 'bk', 'wv', 'bv', 'wo', 'bo', 'ln1_w', 'ln1_b', 'ln2_w', 'ln2_b', 'w_gate', 'we1', 'be1', 'we2', 'be2')}
    del _L0_ffn_all
    return {'x': x, 'ctx_512': ctx_512, 'g_xattn': g_xattn, 'g_ffn': g_ffn, 'L0_xattn_q_norm_w': _L0_xattn_in['q_norm_w'], 'L0_xattn_k_norm_w': _L0_xattn_in['k_norm_w'], 'L0_xattn_w_out': _L0_xattn_in['w_out'], 'L0_ffn_wq': _L0_ffn_in['wq'], 'L0_ffn_bq': _L0_ffn_in['bq'], 'L0_ffn_wk': _L0_ffn_in['wk'], 'L0_ffn_bk': _L0_ffn_in['bk'], 'L0_ffn_wv': _L0_ffn_in['wv'], 'L0_ffn_bv': _L0_ffn_in['bv'], 'L0_ffn_wo': _L0_ffn_in['wo'], 'L0_ffn_bo': _L0_ffn_in['bo'], 'L0_ffn_ln1_w': _L0_ffn_in['ln1_w'], 'L0_ffn_ln1_b': _L0_ffn_in['ln1_b'], 'L0_ffn_ln2_w': _L0_ffn_in['ln2_w'], 'L0_ffn_ln2_b': _L0_ffn_in['ln2_b'], 'L0_ffn_w_gate': _L0_ffn_in['w_gate'], 'L0_ffn_we1': _L0_ffn_in['we1'], 'L0_ffn_be1': _L0_ffn_in['be1'], 'L0_ffn_we2': _L0_ffn_in['we2'], 'L0_ffn_be2': _L0_ffn_in['be2']}

def reference(x, ctx_512, g_xattn, g_ffn, L0_xattn_q_norm_w, L0_xattn_k_norm_w, L0_xattn_w_out, L0_ffn_wq, L0_ffn_bq, L0_ffn_wk, L0_ffn_bk, L0_ffn_wv, L0_ffn_bv, L0_ffn_wo, L0_ffn_bo, L0_ffn_ln1_w, L0_ffn_ln1_b, L0_ffn_ln2_w, L0_ffn_ln2_b, L0_ffn_w_gate, L0_ffn_we1, L0_ffn_be1, L0_ffn_we2, L0_ffn_be2):
    import jax
    import jax.numpy as jnp

    def _L0_xattn_ref(q, k, v, q_norm_w, k_norm_w, w_out):
        import jax, jax.numpy as jnp
        import numpy as np
        N_HEADS = 16
        N_KV_HEADS = 4
        ROPE_THETA = 10000.0
        EPS = 1e-05

        def _rms_norm(x, w):
            var = jnp.mean(x * x, axis=-1, keepdims=True)
            return x * jax.lax.rsqrt(var + EPS) * w

        def _rope_sin_cos(T, head_dim, dtype):
            inv_freq = 1.0 / ROPE_THETA ** (jnp.arange(0, head_dim, 2, dtype=jnp.float32) / head_dim)
            t = jnp.arange(T, dtype=jnp.float32)
            freqs = jnp.outer(t, inv_freq)
            emb = jnp.concatenate([freqs, freqs], -1)
            return (jnp.sin(emb).astype(dtype)[None, None], jnp.cos(emb).astype(dtype)[None, None])

        def _rotate_half(x):
            h = x.shape[-1] // 2
            x1, x2 = (x[..., :h], x[..., h:])
            return jnp.concatenate([-x2, x1], axis=-1)
        B, T, C = q.shape
        hd = C // N_HEADS
        g = N_HEADS // N_KV_HEADS
        q = _rms_norm(q, q_norm_w)
        k = _rms_norm(k, k_norm_w)
        q = q.reshape(B, T, N_HEADS, hd).transpose(0, 2, 1, 3)
        k = k.reshape(B, T, N_KV_HEADS, hd).transpose(0, 2, 1, 3)
        v = v.reshape(B, T, N_KV_HEADS, hd).transpose(0, 2, 1, 3)
        sin, cos = _rope_sin_cos(T, hd, q.dtype)
        q = q * cos + _rotate_half(q) * sin
        k = k * cos + _rotate_half(k) * sin
        qg = q.reshape(B, N_KV_HEADS, g, T, hd)
        scale = 1.0 / jnp.sqrt(jnp.asarray(hd, q.dtype))
        scores = jnp.einsum('bgnqd,bgkd->bgnqk', qg, k) * scale
        causal = jnp.tril(jnp.ones((T, T), bool))
        scores = jnp.where(causal, scores, jnp.asarray(-1e+30, scores.dtype))
        attn = jax.nn.softmax(scores, axis=-1)
        out = jnp.einsum('bgnqk,bgkd->bgnqd', attn, v)
        out = out.reshape(B, N_HEADS, T, hd).transpose(0, 2, 1, 3).reshape(B, T, C)
        return out @ w_out.T

    def _L0_ffn_ref(hidden_states, wq, bq, wk, bk, wv, bv, wo, bo, ln1_w, ln1_b, ln2_w, ln2_b, w_gate, we1, be1, we2, be2):
        import jax, jax.numpy as jnp
        import numpy as np
        import math
        B, S, D = (2, 256, 256)
        H, HD = (16, 128)
        E, I = (4, 256)
        TOP_K = 2
        ROPE_THETA = 10000.0

        def _layernorm(x, w, b):
            mu = jnp.mean(x, axis=-1, keepdims=True)
            var = jnp.mean(jnp.square(x - mu), axis=-1, keepdims=True)
            return (x - mu) * jax.lax.rsqrt(var + 1e-05) * w + b

        def _rotate_half(x):
            x1, x2 = jnp.split(x, 2, axis=-1)
            return jnp.concatenate((-x2, x1), axis=-1)

        def _attention(h, wq, bq, wk, bk, wv, bv, wo, bo):
            b, s, _ = h.shape
            q = (h @ wq + bq).reshape(b, s, H, HD).transpose(0, 2, 1, 3)
            k = (h @ wk + bk).reshape(b, s, H, HD).transpose(0, 2, 1, 3)
            v = (h @ wv + bv).reshape(b, s, H, HD).transpose(0, 2, 1, 3)
            inv_freq = 1.0 / ROPE_THETA ** (jnp.arange(0, HD, 2, dtype=jnp.float32) / HD)
            freqs = jnp.arange(s, dtype=jnp.float32)[:, None] * inv_freq[None, :]
            emb = jnp.concatenate((freqs, freqs), axis=-1)
            cos = jnp.cos(emb)[None, None]
            sin = jnp.sin(emb)[None, None]
            q = q * cos + _rotate_half(q) * sin
            k = k * cos + _rotate_half(k) * sin
            scores = jnp.einsum('bhqd,bhkd->bhqk', q, k) / math.sqrt(HD)
            causal = jnp.tril(jnp.ones((s, s), bool))
            scores = jnp.where(causal[None, None], scores, jnp.finfo(jnp.float32).min)
            probs = jax.nn.softmax(scores.astype(jnp.float32), axis=-1).astype(q.dtype)
            out = jnp.einsum('bhqk,bhkd->bhqd', probs, v)
            out = out.transpose(0, 2, 1, 3).reshape(b, s, H * HD)
            return out @ wo + bo

        def _moe(h, w_gate, we1, be1, we2, be2):
            b, s, d = h.shape
            x = h.reshape(-1, d)
            t = x.shape[0]
            raw = jax.nn.softmax(x @ w_gate, axis=-1)
            top_vals, top_idx = jax.lax.top_k(raw, TOP_K)
            w = jax.nn.softmax(top_vals, axis=-1)
            comb = jnp.zeros((t, E), x.dtype).at[jnp.arange(t)[:, None], top_idx].add(w)
            hmid = jax.nn.gelu(jnp.einsum('td,edi->tei', x, we1) + be1[None], approximate=False)
            eout = jnp.einsum('tei,eid->ted', hmid, we2) + be2[None]
            out = jnp.einsum('te,ted->td', comb, eout)
            return out.reshape(b, s, d)
        a = _attention(_layernorm(hidden_states, ln1_w, ln1_b), wq, bq, wk, bk, wv, bv, wo, bo)
        h = hidden_states + a
        m = _moe(_layernorm(h, ln2_w, ln2_b), w_gate, we1, be1, we2, be2)
        return h + m
    x = x + jnp.tanh(g_xattn[0]) * _L0_xattn_ref(_layernorm(x, axis=-1), ctx_512, ctx_512, L0_xattn_q_norm_w, L0_xattn_k_norm_w, L0_xattn_w_out)
    x = x + jnp.tanh(g_ffn[0]) * _L0_ffn_ref(_layernorm(x, axis=-1), L0_ffn_wq, L0_ffn_bq, L0_ffn_wk, L0_ffn_bk, L0_ffn_wv, L0_ffn_bv, L0_ffn_wo, L0_ffn_bo, L0_ffn_ln1_w, L0_ffn_ln1_b, L0_ffn_ln2_w, L0_ffn_ln2_b, L0_ffn_w_gate, L0_ffn_we1, L0_ffn_be1, L0_ffn_we2, L0_ffn_be2)
    return x

_drawn_inputs = setup_inputs


def setup_inputs(seed=0):
    import zlib

    import numpy as np

    out = dict(_drawn_inputs(seed))
    spreads = {'L0_xattn_q_norm_w': (1.0, 0.2),
     'L0_xattn_k_norm_w': (1.0, 0.2),
     'L0_ffn_bq': (0.0, 0.469),
     'L0_ffn_bk': (0.0, 0.602),
     'L0_ffn_bv': (0.0, 0.1),
     'L0_ffn_bo': (0.0, 0.1),
     'L0_ffn_ln1_w': (1.0, 0.2),
     'L0_ffn_ln1_b': (0.0, 0.1),
     'L0_ffn_ln2_w': (1.0, 0.2),
     'L0_ffn_ln2_b': (0.0, 0.1),
     'L0_ffn_be1': (0.0, 0.1),
     'L0_ffn_be2': (0.0, 0.1)}
    factors = {}
    for name, (base, spread) in spreads.items():
        noise = np.random.default_rng([zlib.crc32(name.encode()), seed]).standard_normal(out[name].shape)
        drawn = base * np.exp(spread * noise) if base else spread * noise
        out[name] = jnp.asarray(drawn.astype(out[name].dtype))
    for name, factor in factors.items():
        out[name] = (out[name] * factor).astype(out[name].dtype)
    return out
```

```python
from contextlib import ExitStack

import numpy as np

import concourse.bass as bass
from concourse import mybir

F32 = mybir.dt.float32
F32R = mybir.dt.float32r
BF16 = mybir.dt.bfloat16
I32 = mybir.dt.int32
ALU = mybir.AluOpType
ACT = mybir.ActivationFunctionType
AX = mybir.AxisListType

P = 128
B, S, D = 4, 256, 256
NT = B * S // P
KT = D // P
XH, XG, XD = 16, 4, 16
XS = 8
XP = 12
VW = XD + 1
H, HD = 16, 128
NP = H // 2
U = 2 * B
NU = NP * U
LEAD = 6
E, I, IT = 4, 256, 2
NE = E * IT
BIG = 1e30
EPS = 1e-5
RSQRT_SEED = 1597463007.0

C_ID, C_MASK, C_XCOS, C_XSIN, C_RCOSQ, C_RSINQ, C_RCOSK, C_RSINK, C_TIE = 0, 128, 384, 416, 448, 704, 960, 1216, 1472
C_END = 1488
B_BQ, B_BK, B_L1W, B_L1B, B_L2W, B_L2B, B_BE1, B_END = 0, 16, 32, 34, 36, 38, 40, 48
R_QW, R_KW, R_BO, R_GX, R_GF, R_END = 0, 256, 320, 576, 577, 578
W_Q, W_K, W_V = 0, 1, 2


def build_kernel(nc, x, ctx_in, cst, cols, rows, bv, wqkv, wo, w_out_t, w_gate, be2, we1, we2, out):
    with ExitStack() as stack:
        def sb(name, shape, dt=F32):
            return stack.enter_context(nc.sbuf_tensor(name, shape, dt))

        def ps(name, shape=(P, 512), dt=F32):
            return stack.enter_context(nc.psum_tensor(name, list(shape), dt))

        def sem(name):
            return stack.enter_context(nc.semaphore(name))

        x_sb = sb("x_sb", [P, NT, D])
        ctx_sb = sb("ctx_sb", [P, NT, 64])
        cst_sb = sb("cst_sb", [P, C_END])
        bf_sb = sb("bf_sb", [P, 256], BF16)
        cols_sb = sb("cols_sb", [P, B_END])
        rows_sb = sb("rows_sb", [P, R_END])
        bv_sb = sb("bv_sb", [P, H * HD])
        w_out_sb = sb("w_out_sb", [P, KT, D])
        w_gate_sb = sb("w_gate_sb", [P, KT, E])
        be2_sb = sb("be2_sb", [E, D])
        yacc = sb("yacc", [P, NT, D])
        hH = sb("hH", [P, KT, NT * P], F32R)
        hL = sb("hL", [P, KT, NT * P], F32R)
        mv = sb("mv", [P, NT, 2])
        bnst = sb("bnst", [P, NT, 6])
        small = sb("small", [P, 160])
        stg = sb("stg", [P, 3, KT, 256])
        stgo = sb("stgo", [P, 2, D])
        qk_parts = sb("qk_parts", [P, 2, 4 * KT * HD], F32R)
        wqkH = qk_parts[:, 0, :].rearrange("p (c k n) -> p c k n", c=4, k=KT)
        wqkL = qk_parts[:, 1, :].rearrange("p (c k n) -> p c k n", c=4, k=KT)
        wvH = sb("wvH", [P, KT, 256], F32R)
        wvL = sb("wvL", [P, KT, 256], F32R)
        woH = sb("woH", [P, 2, D], F32R)
        woL = sb("woL", [P, 2, D], F32R)
        qk_bias = sb("qk_bias", [P, 4])
        qk_room = sb("qk_room", [P, 4, 512])
        qk_f = qk_room[:, 0:2, :]
        qk_sw = qk_room[:, 2:4, :]
        QT = sb("QT", [P, 4, NT * P])
        V = sb("V", [P, NT, 256])
        sm = sb("sm", [P, 2, 384])
        nm = sb("nm", [P, 2, 2])
        rs = sb("rs", [P, 2, 2])
        PR = sb("PR", [P, 2, 512])
        PTs = sb("PTs", [P, 2, 512])
        o_parts = sb("o_parts", [P, 2, 1024], F32R)
        oH = o_parts[:, 0, :].rearrange("p (m r n) -> p m r n", m=2, r=2)
        oL = o_parts[:, 1, :].rearrange("p (m r n) -> p m r n", m=2, r=2)
        weH = sb("weH", [P, 4096], F32R)
        weL = sb("weL", [P, 4096], F32R)
        we1H = weH[:, 0:2048].rearrange("p (k n) -> p k n", k=KT)
        we1L = weL[:, 0:2048].rearrange("p (k n) -> p k n", k=KT)
        we2H = weH[:, 2048:4096].rearrange("p (e n) -> p e n", e=NE)
        we2L = weL[:, 2048:4096].rearrange("p (e n) -> p e n", e=NE)
        G = sb("G", [P, 2, 512])
        GH = o_parts[:, :, :].rearrange("p m (k n) -> p m k n", k=IT)
        GL = qk_parts[:, :, :].rearrange("p m (k n) -> p m k n", k=IT)
        gate = sb("gate", [P, 512])
        combT = sb("combT", [E, NT, P])
        qn = sb("qn", [P, 2, D])
        kpack = V[:, :, :].rearrange("p t n -> p (t n)").bitcast(BF16).rearrange("p (n s d) -> p n s d", s=XS, d=XD)
        qpack = sb("qpack", [P, 2, 2, 8, XS, XD], BF16)
        kT = sb("kT", [P, B, XG, 256], BF16)
        qT = qk_room[:, :, :].rearrange("p a n -> p (a n)").bitcast(BF16).rearrange("p (x t h n) -> p x t h n", x=2, t=2, h=8)
        vA = sb("vA", [P, NT, XG, VW])
        WC = sb("WC", [P, 2, 2, P])
        WS = sb("WS", [P, 2, 2, P])
        qf = sb("qf", [P, 256])
        qf2 = sb("qf2", [P, 256])
        qr = sb("qr", [P, 256])
        on = sb("on", [P, 2, D])
        onT = sb("onT", [P, KT, 2, P])
        nxm = sb("nxm", [P, 2, 4])
        rden = sb("rden", [P, 2, XH])
        WKC = sb("WKC", [P, 2, 64])
        WKS = sb("WKS", [P, 2, 64])
        kf = yacc[:, 0:2, :].rearrange("p t n -> p (t n)").rearrange("p (t n) -> p t n", t=NT)
        kf2 = yacc[:, 2:4, :].rearrange("p t n -> p (t n)").rearrange("p (t n) -> p t n", t=NT)
        kr = yacc[:, 4:6, :].rearrange("p t n -> p (t n)").rearrange("p (t n) -> p t n", t=NT)

        nh = sb("nh", [P, 2, D])
        hT = sm[:, :, :].rearrange("p a n -> p (a n)")[:, 0:512].rearrange("p (k n) -> p k n", k=KT)

        bank = [ps(f"bank{n}") for n in range(8)]
        S_B = bank[0:2]
        PT_B = bank[2:4]
        O_B = bank[4:6]
        M_B = bank[6:8]

        ident = cst_sb[:, C_ID:C_ID + P]
        ident_bf = bf_sb[:, 0:P]
        mask_bf = bf_sb[:, P:2 * P]

        names = """d_x0 d_x1 d_x2 d_x3 d_ctx d_cst d_cols d_rows d_bv d_wout d_small d_wqkv d_wo d_we d_sw0 d_sw1 d_out
        bf_ready dve_seq pool_seq ssk_done wtab_ready va_ready qn_ready q_parts qpack_ready kpack_ready
        m6_pe m7_pe m6_free m7_free s_pe s_max s_exp pt_pe pt_copy_act pt_copy_dve pv_pe on_ready tanh_done
        nh_ready yacc_init hT_ready hH_ready h_ready we_ready
        wqk_ready wqk_half wqk_bias wv_ready wv_half wo_ready wo_half b_recip c_gmax c_gexp c_gdiff chunk_pe chunk_f chunk_cos chunk_sw rope_done
        b_s b_max b_exp b_norm b_pt b_ptcopy b_pv b_oH b_oL b_wo b_yadd v_pe v_ready
        c_nh c_tr c_hT c_hH c_h c_logit c_comb c_combT_pe c_combT c_be c_init c_mid c_gelu c_gH c_gL c_exp_pe c_acc c_fin"""
        s = {n: sem(n) for n in names.split()}

        def wait(eng, name, value):
            eng.wait_ge(s[name], value)

        x_v = x.rearrange("b (t p) d -> p (b t) d", p=P)
        ctx_v = ctx_in.rearrange("b (t p) d -> p (b t) d", p=P)
        out_v = out.rearrange("b (t p) d -> p (b t) d", p=P)

        def piece(k):
            g, j = divmod(k, 3)
            return (g, 0, [4 * g + n for n in range(4)]) if j == 0 else (g, 1, [4 * g + 2 * (j - 1) + n for n in range(2)])

        M6, M7 = [("Q", 0, 0, 0), ("Q", 0, 0, 1)], [("K", b) for b in range(B)]
        for b in range(B):
            M6 += [("Q", b, 1, 0), ("Q", b, 1, 1)] + ([("OT", b - 1)] if b else [])
            M6 += [("Q", b + 1, 0, 0), ("Q", b + 1, 0, 1)] if b + 1 < B else []
            M7 += [("PJ", b), ("NT", b)]
        M6 += [("OT", B - 1)]
        m6 = {e: n for n, e in enumerate(M6)}
        m7 = {e: n for n, e in enumerate(M7)}
        NPX = XP * B

        def copier(p):
            by_act = [n % 3 == 2 for n in range(p + 1)]
            return ("pt_copy_act", sum(by_act)) if by_act[p] else ("pt_copy_dve", p + 1 - sum(by_act))

        def steps(eng, step, peeled=1):
            for j in range(U):
                step(0, j)
            with eng.Fori(1, NP - peeled) as i:
                for j in range(U):
                    step(i, j)
            for i in range(NP - peeled, NP):
                for j in range(U):
                    step(i, j)
            for j in range(4):
                step(NP, j)

        def unit(i, j, lag):
            if not isinstance(i, int):
                return True
            return 0 <= U * i + j - lag < NU

        def chunk_at(j):
            return (j + LEAD) % 4, (j + LEAD) // 4 % 2

        def v_event(i, j):
            return j % 2 == 1 and (not isinstance(i, int) or (i < NP and B * i + (j + 3) // 2 < B * NP))

        def pt_copy(eng, p):
            eng.wait_ge(s["pt_pe"], p + 1)
            if p >= 2:
                eng.wait_ge(s["pv_pe"], p - 1)
            copy = eng.tensor_copy if eng is nc.vector else eng.copy
            copy(PTs[:, p % 2, :], PT_B[p % 2][:, :]).then_inc(s[copier(p)[0]], 1)

        h2T = QT[:, 0:2, :]
        bank_bf = [bank[n][:, :].bitcast(BF16) for n in (6, 7)]
        block = stack.enter_context(nc.Block())

        @block.sync
        def _(sp):
            sp.dma_start(cst_sb[:, :], cst).then_inc(s["d_cst"], 16)
            sp.dma_start(ctx_sb[:, :, :], ctx_v).then_inc(s["d_ctx"], 16)
            sp.dma_start(rows_sb[:, :], rows.to_broadcast([P, R_END])).then_inc(s["d_rows"], 16)
            for b in range(B):
                sp.dma_start(x_sb[:, 2 * b:2 * b + 2, :], x_v[:, 2 * b:2 * b + 2, :]).then_inc(s[f"d_x{b}"], 16)
            sp.dma_start(cols_sb[:, :], cols).then_inc(s["d_cols"], 16)
            sp.dma_start(stg[:, :, :, :], wqkv[0]).then_inc(s["d_wqkv"], 16)
            sp.dma_start(stgo[:, :, :], wo[0]).then_inc(s["d_wo"], 16)
            sp.dma_start(w_out_sb[:, :, :], w_out_t).then_inc(s["d_wout"], 16)
            sp.dma_start(w_gate_sb[:, :, :], w_gate).then_inc(s["d_small"], 16)
            sp.dma_start(be2_sb[:, :], be2).then_inc(s["d_small"], 16)
            sp.dma_start(bv_sb[:, :], bv.to_broadcast([P, H * HD])).then_inc(s["d_bv"], 16)
            sp.dma_start(QT[:, 0:2, :].rearrange("p c n -> p (c n)"), we1).then_inc(s["d_we"], 16)
            sp.dma_start(QT[:, 2:4, :].rearrange("p c n -> p (c n)"), we2).then_inc(s["d_we"], 16)
            sp.wait_ge(s["wv_ready"], 1)
            sp.wait_ge(s["wqk_ready"], 4)
            sp.dma_start(stg[:, :, :, :], wqkv[1]).then_inc(s["d_wqkv"], 16)
            sp.wait_ge(s["wo_ready"], 1)
            sp.dma_start(stgo[:, :, :], wo[1]).then_inc(s["d_wo"], 16)

            def swap(n, q):
                sp.wait_ge(s["chunk_f"], n + 1)
                sp.dma_start(qk_sw[0:64, q, :], qk_f[64:128, q, :]).then_inc(s[f"d_sw{q}"], 16)
                sp.dma_start(qk_sw[64:128, q, :], qk_f[0:64, q, :]).then_inc(s[f"d_sw{q}"], 16)

            for n in range(LEAD):
                swap(n, n % 2)

            def step(i, j):
                if unit(i, j, -LEAD):
                    swap(U * i + j + LEAD, j % 2)
            steps(sp, step)
            for b in range(B):
                sp.wait_ge(s["c_fin"], b + 1)
                sp.dma_start(out_v[:, 2 * b:2 * b + 2, :], yacc[:, 2 * b:2 * b + 2, :]).then_inc(s["d_out"], 16)
            sp.wait_ge(s["d_out"], 16 * B)

        @block.gpsimd
        def _(pool):
            seq = [0]

            def link(ins):
                seq[0] += 1
                ins.then_inc(s["pool_seq"], 1)
                pool.wait_ge(s["pool_seq"], seq[0])

            pool.memset(vA[:, :, :, XD:VW], 1.0).then_inc(s["va_ready"], 1)
            pool.wait_ge(s["d_rows"], 16)
            pool.wait_ge(s["d_cst"], 16)
            for t in range(2):
                def table(col, heads):
                    return cst_sb[:, col + t * XD:col + (t + 1) * XD].unsqueeze(1).to_broadcast([P, heads, XD])
                w = rows_sb[:, R_KW:R_KW + 64].rearrange("p (h d) -> p h d", d=XD)
                c, sn = table(C_XCOS, 4), table(C_XSIN, 4)
                wks = WKS[:, t, :].rearrange("p (h d) -> p h d", d=XD)
                pool.tensor_tensor(WKC[:, t, :].rearrange("p (h d) -> p h d", d=XD), w, c, ALU.mult).then_inc(s["wtab_ready"], 1)
                pool.tensor_tensor(wks[:, :, 0:8], w[:, :, 8:16], sn[:, :, 0:8], ALU.mult).then_inc(s["wtab_ready"], 1)
                pool.tensor_tensor(wks[:, :, 8:16], w[:, :, 0:8], sn[:, :, 8:16], ALU.mult).then_inc(s["wtab_ready"], 1)
            for X in range(2):
                for t in range(2):
                    c = cst_sb[:, C_XCOS + t * XD:C_XCOS + (t + 1) * XD].unsqueeze(1).to_broadcast([P, 8, XD])
                    sn = cst_sb[:, C_XSIN + t * XD:C_XSIN + (t + 1) * XD].unsqueeze(1).to_broadcast([P, 8, XD])
                    w = rows_sb[:, R_QW + X * P:R_QW + (X + 1) * P].rearrange("p (h d) -> p h d", d=XD)
                    ws = WS[:, X, t, :].rearrange("p (h d) -> p h d", d=XD)
                    pool.tensor_tensor(WC[:, X, t, :].rearrange("p (h d) -> p h d", d=XD), w, c, ALU.mult)
                    pool.tensor_tensor(ws[:, :, 0:8], w[:, :, 8:16], sn[:, :, 0:8], ALU.mult)
                    last = pool.tensor_tensor(ws[:, :, 8:16], w[:, :, 0:8], sn[:, :, 8:16], ALU.mult)
            link(last)

            def prep(b, X):
                if X == 0:
                    pool.wait_ge(s["qn_ready"], b + 1)
                if b:
                    pool.wait_ge(s["m6_pe"], m6["Q", b - 1, X, 1] + 1)
                qv = qn[:, :, X * P:(X + 1) * P]
                q4 = qv.rearrange("p t (h d) -> p t h d", d=XD)
                g4 = qf2[:, :].rearrange("p (t h d) -> p t h d", t=2, d=XD)
                w4 = WS[:, X, :, :].rearrange("p t (h d) -> p t h d", d=XD)
                pool.tensor_tensor(qf[:, :].rearrange("p (t n) -> p t n", t=2), qv, WC[:, X, :, :], ALU.mult)
                for t in range(2):
                    pool.tensor_tensor(g4[:, t, :, 0:8], q4[:, t, :, 8:16], w4[:, t, :, 0:8], ALU.mult)
                    last = pool.tensor_tensor(g4[:, t, :, 8:16], q4[:, t, :, 0:8], w4[:, t, :, 8:16], ALU.mult)
                link(last)
                link(pool.tensor_tensor(qf[:, :], qf[:, :], qf2[:, :], ALU.add))
                part = qpack[:, X, :, :, :, :].rearrange("p t h s d -> p (t h) s d")
                f = qf[:, :].rearrange("p (n d) -> p n d", d=XD)
                r = qr[:, :].rearrange("p (n d) -> p n d", d=XD)
                link(pool.tensor_copy(part[:, :, 0, :], f))
                link(pool.tensor_tensor(r, f, part[:, :, 0, :], ALU.subtract))
                link(pool.tensor_copy(part[:, :, 3, :], r))
                link(pool.tensor_tensor(r, r, part[:, :, 3, :], ALU.subtract))
                pool.tensor_copy(part[:, :, 6, :], r).then_inc(s["q_parts"], 1)
                pool.wait_ge(s["q_parts"], 2 * b + X + 1)

            def low_qk(c, p):
                r, k = divmod(c, 2)
                col = B_BQ + 16 * k + 2 * p + r
                pool.tensor_copy(qk_bias[:, c:c + 1], cols_sb[:, bass.ds(col, 1)]).then_inc(s["wqk_bias"], 1)
                pool.wait_ge(s["wqk_half"], 4 * p + c + 1)
                pool.tensor_tensor(wqkL[:, c], stg[:, k, :, r * HD:(r + 1) * HD], wqkH[:, c].bitcast(F32),
                                   ALU.subtract).then_inc(s["wqk_ready"], 1)

            def low_v(p):
                pool.wait_ge(s["wv_half"], p + 1)
                pool.tensor_tensor(wvL[:, :, :], stg[:, W_V, :, :], wvH[:, :, :].bitcast(F32), ALU.subtract).then_inc(s["wv_ready"], 1)

            def low_o(p):
                pool.wait_ge(s["wo_half"], p + 1)
                pool.tensor_tensor(woL[:, :, :], stgo[:, :, :], woH[:, :, :].bitcast(F32), ALU.subtract).then_inc(s["wo_ready"], 1)

            prep(0, 0)
            prep(0, 1)
            pool.wait_ge(s["d_ctx"], 16)
            for b in range(B):
                pool.tensor_copy(vA[:, 2 * b:2 * b + 2, :, 0:XD].rearrange("p t g d -> p (t g) d"), ctx_sb[:, 2 * b:2 * b + 2, :].rearrange("p t (g d) -> p (t g) d", d=XD)).then_inc(s["va_ready"], 1)
            prep(1, 0)
            prep(1, 1)
            pool.wait_ge(s["d_wqkv"], 16)
            pool.wait_ge(s["d_cols"], 16)
            for c in range(4):
                r, k = divmod(c, 2)
                pool.tensor_copy(wqkH[:, c], stg[:, k, :, r * HD:(r + 1) * HD]).then_inc(s["wqk_half"], 1)
                low_qk(c, 0)
            pool.tensor_copy(wvH[:, :, :], stg[:, W_V, :, :]).then_inc(s["wv_half"], 1)
            low_v(0)
            pool.wait_ge(s["d_wo"], 16)
            pool.tensor_copy(woH[:, :, :], stgo[:, :, :]).then_inc(s["wo_half"], 1)
            low_o(0)
            prep(2, 0)
            prep(2, 1)
            pool.wait_ge(s["d_we"], 32)
            qt_flat = QT[:, :, :].rearrange("p c n -> p (c n)")
            for a in range(0, 4096, 1024):
                link(pool.tensor_copy(weH[:, a:a + 1024], qt_flat[:, a:a + 1024]))
                pool.tensor_tensor(weL[:, a:a + 1024], qt_flat[:, a:a + 1024],
                                   weH[:, a:a + 1024].bitcast(F32), ALU.subtract).then_inc(s["we_ready"], 1)
            prep(3, 0)
            prep(3, 1)
            for b in range(B):
                pool.wait_ge(s["nh_ready"], b + 1)
                y = yacc[:, 2 * b:2 * b + 2, :]
                pool.tensor_tensor(y, y, rows_sb[:, R_BO:R_BO + D].unsqueeze(1).to_broadcast([P, 2, D]), ALU.add).then_inc(s["yacc_init"], 1)
                pool.wait_ge(s["hH_ready"], b + 1)
                cut = slice(256 * b, 256 * (b + 1))
                pool.tensor_tensor(hL[:, :, cut], hT[:, :, :], hH[:, :, cut].bitcast(F32), ALU.subtract).then_inc(s["h_ready"], 1)

            def rope_sin(sw_count, q, k):
                pool.wait_ge(s[f"d_sw{q}"], sw_count)
                col = C_RSINK if k else C_RSINQ
                v = qk_sw[:, q, :].rearrange("p (b t) -> p b t", b=2)
                pool.tensor_tensor(v, v, cst_sb[:, col:col + 256].unsqueeze(1).to_broadcast([P, 2, 256]), ALU.mult).then_inc(s["chunk_sw"], 1)

            for n in range(LEAD):
                rope_sin(32 * (n // 2 + 1), n % 2, n % 2)

            def step(i, j):
                more = not (isinstance(i, int) and i >= NP - 1)
                if unit(i, j, -LEAD):
                    rope_sin(32 * (4 * i + (j + LEAD) // 2 + 1), j % 2, j % 2)
                if more and j < 4:
                    low_qk(j, i + 1)
                if j == 3 and not (isinstance(i, int) and (i == 0 or i >= NP)):
                    low_o(i)
                if more and j == 4:
                    low_v(i + 1)

            steps(pool, step)

            for b in range(B):
                pool.wait_ge(s["c_hH"], b + 1)
                cut = slice(256 * b, 256 * (b + 1))
                pool.tensor_tensor(hL[:, :, cut], h2T[:, :, cut], hH[:, :, cut].bitcast(F32), ALU.subtract).then_inc(s["c_h"], 1)
            for n in range(2 * NE):
                c, m = divmod(n, NE)
                e, ih = divmod(m, IT)
                pool.wait_ge(s["c_gelu"], n + 1)
                if n >= 4:
                    pool.wait_ge(s["c_exp_pe"], 2 * (n // 2 - 1))
                pool.tensor_copy(GH[:, (n // 2) % 2, n % 2, :], G[:, n % 2, :]).then_inc(s["c_gH"], 1)

        @block.scalar
        def _(act):
            act.wait_ge(s["d_ctx"], 16)
            for t in range(NT):
                ins = act.activation(kf2[:, t, :], ctx_sb[:, t, :], ACT.Square, accum_out=small[:, 8 + t:9 + t])
                ins.then_inc(s["ssk_done"], 1)
            act.wait_ge(s["d_rows"], 16)
            act.activation(small[:, 96:98], rows_sb[:, R_GX:R_GX + 2], ACT.Tanh).then_inc(s["tanh_done"], 1)

            def q_evac(b, X, t):
                n = m6["Q", b, X, t]
                act.wait_ge(s["m6_pe"], n + 1)
                act.activation(qT[:, X, t, :, :].rearrange("p h n -> p (h n)"), bank_bf[0][:, :], ACT.Copy).then_inc(s["m6_free"], 1)

            def o_evac(b):
                act.wait_ge(s["m6_pe"], m6["OT", b] + 1)
                act.activation(onT[:, :, :, :].rearrange("p k t n -> p (k t n)"), bank[6][:, :], ACT.Copy).then_inc(s["m6_free"], 1)

            def h_high(b):
                act.wait_ge(s["hT_ready"], b + 1)
                act.activation(hH[:, :, 256 * b:256 * (b + 1)], hT[:, :, :], ACT.Copy).then_inc(s["hH_ready"], 1)

            q_evac(0, 0, 0)
            q_evac(0, 0, 1)
            for p in range(NPX):
                b, k = divmod(p, XP)
                g, t, heads = piece(k)
                width = P * (t + 1)
                act.wait_ge(s["s_max"], p + 1)
                if p >= 2:
                    act.wait_ge(s["pt_pe"], p - 1)
                for n, h in enumerate(heads):
                    ins = act.activation(PR[:, p % 2, n * width:(n + 1) * width], S_B[p % 2][:, n * width:(n + 1) * width],
                                         ACT.Exp, bias=nxm[:, p % 2, n:n + 1])
                ins.then_inc(s["s_exp"], 1)
                if k in (1, 2):
                    q_evac(b, 1, k - 1)
                if k == 3 and b:
                    o_evac(b - 1)
                if k in (7, 9) and b + 1 < B:
                    q_evac(b + 1, 0, (k - 7) // 2)
                if k == 9 and b:
                    h_high(b - 1)
                if p >= 1 and (p - 1) % 3 == 2:
                    pt_copy(act, p - 1)
            pt_copy(act, NPX - 1)
            o_evac(B - 1)
            h_high(B - 1)

            def chunk_out(n, q, c, guard):
                act.wait_ge(s["chunk_pe"], n + 1)
                if guard:
                    act.wait_ge(s["rope_done"], n - 1)
                act.activation(qk_f[:, q, :], O_B[q][:, :], ACT.Identity, bias=qk_bias[:, c:c + 1]).then_inc(s["chunk_f"], 1)

            act.wait_ge(s["wqk_bias"], 4)
            for n in range(LEAD):
                chunk_out(n, n % 2, n % 4, n >= 2)

            def step(i, j):
                T = U * i + j
                q = j % 2
                more = not (isinstance(i, int) and i >= NP - 1)
                if unit(i, j, 0):
                    act.wait_ge(s["b_max"], T + 1)
                    if unit(i, j, 2):
                        act.wait_ge(s["b_pt"], T - 1)
                    for t in range(2):
                        a, e = ((0, P), (P, 3 * P))[t]
                        ins = act.activation(PR[:, q, a:e], sm[:, q, a:e], ACT.Exp, bias=nm[:, q, t:t + 1], scale=-1.0,
                                             accum_out=rs[:, q, t:t + 1])
                        ins.then_inc(s["b_exp"], 1)
                if unit(i, j, -LEAD):
                    if 2 <= j < 6:
                        act.wait_ge(s["wqk_bias"], 4 * (i + 1) + j - 2 + 1)
                    chunk_out(T + LEAD, q, chunk_at(j)[0], True)
                if unit(i, j, 1):
                    act.wait_ge(s["b_pt"], T)
                    if unit(i, j, 3):
                        act.wait_ge(s["b_pv"], T - 2)
                    act.activation(PTs[:, 1 - q, 0:384], bank[2][:, 0:384], ACT.Copy).then_inc(s["b_ptcopy"], 1)
                if unit(i, j, 2):
                    act.wait_ge(s["b_pv"], T - 1)
                    if unit(i, j, 6):
                        act.wait_ge(s["b_wo"], 4 * i + (j - 2) // 2 - 1)
                    act.activation(oH[:, ((j - 2) // 2) % 2, q, :], bank[3][:, 0:256], ACT.Copy).then_inc(s["b_oH"], 1)
                if more and j < 4:
                    if j == 0:
                        act.wait_ge(s["d_wqkv"], 16 * (i + 2))
                    r, k = divmod(j, 2)
                    act.activation(wqkH[:, j], stg[:, k, :, r * HD:(r + 1) * HD], ACT.Copy).then_inc(s["wqk_half"], 1)
                if j == 3 and not (isinstance(i, int) and (i == 0 or i >= NP)):
                    act.wait_ge(s["d_wo"], 16 * (i + 1))
                    act.wait_ge(s["b_wo"], 4 * i)
                    act.activation(woH[:, :, :], stgo[:, :, :], ACT.Copy).then_inc(s["wo_half"], 1)
                if more and j == 4:
                    act.wait_ge(s["v_pe"], 4 * i + 4)
                    act.activation(wvH[:, :, :], stg[:, W_V, :, :], ACT.Copy).then_inc(s["wv_half"], 1)
                if j == 5 and not (isinstance(i, int) and (i == 0 or i >= NP - 1)):
                    act.wait_ge(s["wo_ready"], i + 1)
                    act.dma_start(stgo[:, :, :], wo[bass.ds(i + 1, 1)].rearrange("a p w n -> (a p) w n")).then_inc(s["d_wo"], 16)
                if j == 6 and not (isinstance(i, int) and i >= NP - 2):
                    act.wait_ge(s["wqk_ready"], 4 * (i + 2))
                    act.wait_ge(s["wv_ready"], i + 2)
                    act.dma_start(stg[:, :, :, :], wqkv[bass.ds(i + 2, 1)].rearrange("a p w k n -> (a p) w k n")).then_inc(s["d_wqkv"], 16)

            steps(act, step, 2)

            for b in range(B):
                act.wait_ge(s["c_hT"], b + 1)
                act.activation(hH[:, :, 256 * b:256 * (b + 1)], h2T[:, :, 256 * b:256 * (b + 1)], ACT.Copy).then_inc(s["c_hH"], 1)
            act.wait_ge(s["c_gmax"], 1)
            act.activation(gate[:, 64:96], gate[:, 32:64], ACT.Exp).then_inc(s["c_gexp"], 1)
            act.wait_ge(s["c_gdiff"], 1)
            act.activation(gate[:, 400:408], gate[:, 392:400], ACT.Exp).then_inc(s["c_gexp"], 1)
            for n in range(2 * NE):
                c, m = divmod(n, NE)
                act.wait_ge(s["c_mid"], n + 1)
                if n >= 2:
                    act.wait_ge(s["c_gL"], n - 1)
                act.activation(G[:, n % 2, :], bank[n % 2][:, :], ACT.Gelu,
                               bias=cols_sb[:, B_BE1 + m:B_BE1 + m + 1]).then_inc(s["c_gelu"], 1)

        @block.vector
        def _(dve):
            seq = [0]

            def link(ins):
                seq[0] += 1
                ins.then_inc(s["dve_seq"], 1)
                dve.wait_ge(s["dve_seq"], seq[0])

            def rsqrt(v, y, t):
                link(dve.tensor_scalar(t.bitcast(I32), v.bitcast(I32), 1, None, ALU.logical_shift_right))
                link(dve.tensor_scalar(y.bitcast(I32), t.bitcast(I32), -1.0, RSQRT_SEED, ALU.mult, ALU.add))
                for _ in range(3):
                    link(dve.scalar_tensor_tensor(t, y, -0.5, y, ALU.mult, ALU.mult))
                    link(dve.tensor_tensor(t, t, v, ALU.mult))
                    link(dve.scalar_tensor_tensor(y, t, 1.5, y, ALU.add, ALU.mult))

            def two_norms(var, n, r1, r2, a, t):
                link(dve.tensor_scalar(a, var, EPS, None, ALU.add))
                rsqrt(a, r1, t)
                link(dve.tensor_tensor(a, var, r1, ALU.mult))
                link(dve.tensor_tensor(a, a, r1, ALU.mult))
                link(dve.tensor_scalar(a, a, EPS, None, ALU.add))
                rsqrt(a, r2, t)

            dve.wait_ge(s["d_cst"], 16)
            dve.tensor_copy(ident_bf, ident)
            dve.tensor_scalar(mask_bf, cst_sb[:, C_MASK + P:C_MASK + 2 * P], -1.0, None, ALU.mult).then_inc(s["bf_ready"], 1)

            for t in range(NT):
                if t % 2 == 0:
                    dve.wait_ge(s[f"d_x{t // 2}"], 16)
                ins = dve.bn_stats(bnst[:, t, :], x_sb[:, t, :])
            link(ins)
            for t in range(NT):
                ins = dve.bn_aggr(mv[:, t, :], bnst[:, t, :])
            link(ins)
            SM = lambda a, n: small[:, a:a + n]
            dve.wait_ge(s["ssk_done"], NT)
            link(dve.tensor_copy(SM(0, 8), mv[:, :, 1]))
            link(dve.tensor_scalar(SM(8, 8), SM(8, 8), 1.0 / 64, None, ALU.mult))
            link(dve.tensor_scalar(SM(16, 16), SM(0, 16), EPS, None, ALU.add))
            rsqrt(SM(16, 16), SM(32, 16), SM(48, 16))
            link(dve.tensor_tensor(SM(16, 8), SM(0, 8), SM(32, 8), ALU.mult))
            link(dve.tensor_tensor(SM(16, 8), SM(16, 8), SM(32, 8), ALU.mult))
            link(dve.tensor_scalar(SM(16, 8), SM(16, 8), EPS, None, ALU.add))
            rsqrt(SM(16, 8), SM(64, 8), SM(48, 8))
            link(dve.tensor_tensor(SM(72, 8), SM(32, 8), SM(64, 8), ALU.mult))

            def norm_q(b):
                if b:
                    dve.wait_ge(s["q_parts"], 2 * b)
                for t in range(2):
                    n = 2 * b + t
                    ins = dve.tensor_scalar(qn[:, t, :], x_sb[:, n, :], mv[:, n, 0:1], small[:, 72 + n:73 + n], ALU.subtract, ALU.mult)
                ins.then_inc(s["qn_ready"], 1)

            norm_q(0)
            for t in range(NT):
                ins = dve.tensor_scalar(kr[:, t, :], ctx_sb[:, t, :], small[:, 40 + t:41 + t], XD ** -0.5, ALU.mult, ALU.mult)
            link(ins)
            dve.wait_ge(s["wtab_ready"], 6)
            kb = kr[:, :, :].rearrange("p (b t) n -> p b (t n)", t=2)
            k4 = kr[:, :, :].rearrange("p (b t) (g d) -> p b (t g) d", t=2, d=XD)
            f4 = kf2[:, :, :].rearrange("p (b t) (g d) -> p b (t g) d", t=2, d=XD)
            w4 = WKS[:, :, :].rearrange("p t (g d) -> p (t g) d", d=XD)
            dve.tensor_tensor(kf[:, :, :].rearrange("p (b t) n -> p b (t n)", t=2), kb,
                              WKC[:, :, :].rearrange("p t n -> p (t n)").unsqueeze(1).to_broadcast([P, B, P]), ALU.mult)
            dve.tensor_tensor(f4[:, :, :, 0:8], k4[:, :, :, 8:16], w4[:, :, 0:8].unsqueeze(1).to_broadcast([P, B, 8, 8]), ALU.mult)
            link(dve.tensor_tensor(f4[:, :, :, 8:16], k4[:, :, :, 0:8], w4[:, :, 8:16].unsqueeze(1).to_broadcast([P, B, 8, 8]), ALU.mult))
            link(dve.tensor_tensor(kf[:, :, :], kf[:, :, :], kf2[:, :, :], ALU.add))
            kv = kf[:, :, :].rearrange("p t (g d) -> p (t g) d", d=XD)
            krv = kr[:, :, :].rearrange("p t (g d) -> p (t g) d", d=XD)
            link(dve.tensor_copy(kpack[:, :, 0, :], kv))
            link(dve.tensor_tensor(krv, kv, kpack[:, :, 0, :], ALU.subtract))
            link(dve.tensor_copy(kpack[:, :, 1, :], krv))
            link(dve.tensor_tensor(krv, krv, kpack[:, :, 1, :], ALU.subtract))
            link(dve.tensor_copy(kpack[:, :, 2, :], krv))
            dve.tensor_copy(kpack[:, :, 3:6, :], kpack[:, :, 0:3, :])
            dve.tensor_copy(kpack[:, :, 6:8, :], kpack[:, :, 0:2, :]).then_inc(s["kpack_ready"], 1)

            def pack(b, X):
                dve.wait_ge(s["q_parts"], 2 * b + X + 1)
                v = qpack[:, X, :, :, :, :].rearrange("p t h s d -> p (t h) s d")
                dve.tensor_copy(v[:, :, 1, :], v[:, :, 0, :])
                dve.tensor_copy(v[:, :, 2, :], v[:, :, 0, :])
                dve.tensor_copy(v[:, :, 4, :], v[:, :, 3, :])
                dve.tensor_copy(v[:, :, 5, :], v[:, :, 3, :])
                dve.tensor_copy(v[:, :, 7, :], v[:, :, 6, :]).then_inc(s["qpack_ready"], 1)

            pack(0, 0)
            pack(0, 1)
            for b in range(B):
                dve.wait_ge(s["m7_pe"], m7["K", b] + 1)
                dve.tensor_copy(kT[:, b, :, :].rearrange("p g n -> p (g n)"), bank_bf[1][:, :]).then_inc(s["m7_free"], 1)

            def norm_out(b):
                dve.wait_ge(s["pv_pe"], XP * (b + 1))
                for t in range(2):
                    o = O_B[t][:, 0:XH * VW].rearrange("p (h d) -> p h d", d=VW)
                    ins = dve.reciprocal(rden[:, t, :].unsqueeze(2), o[:, :, XD:VW])
                link(ins)
                for t in range(2):
                    o = O_B[t][:, 0:XH * VW].rearrange("p (h d) -> p h d", d=VW)
                    ins = dve.tensor_tensor(on[:, t, :].rearrange("p (h d) -> p h d", d=XD), o[:, :, 0:XD],
                                            rden[:, t, :].unsqueeze(2).to_broadcast([P, XH, XD]), ALU.mult)
                ins.then_inc(s["on_ready"], 1)

            def residual(b):
                dve.wait_ge(s["m7_pe"], m7["PJ", b] + 1)
                dve.wait_ge(s["tanh_done"], 1)
                xb = x_sb[:, 2 * b:2 * b + 2, :]
                ins = dve.scalar_tensor_tensor(xb.rearrange("p t n -> p (t n)"), bank[7][:, :], small[:, 96:97],
                                               xb.rearrange("p t n -> p (t n)"), ALU.mult, ALU.add)
                ins.then_inc(s["m7_free"], 1)
                dve.wait_ge(s["m7_free"], m7["PJ", b] + 1)
                for t in range(2):
                    ins = dve.bn_stats(bnst[:, t, :], x_sb[:, 2 * b + t, :])
                link(ins)
                for t in range(2):
                    ins = dve.bn_aggr(mv[:, 2 * b + t, :], bnst[:, t, :])
                link(ins)
                link(dve.tensor_copy(SM(100, 2), mv[:, 2 * b:2 * b + 2, 1]))
                two_norms(SM(100, 2), 2, SM(102, 2), SM(104, 2), SM(106, 2), SM(108, 2))
                for t in range(2):
                    n = 2 * b + t
                    ins = dve.tensor_scalar(yacc[:, n, :], x_sb[:, n, :], mv[:, n, 0:1], small[:, 102 + t:103 + t], ALU.subtract, ALU.mult)
                link(ins)
                if b:
                    dve.wait_ge(s["m7_pe"], m7["NT", b - 1] + 1)
                for t in range(2):
                    ins = dve.tensor_scalar(nh[:, t, :], yacc[:, 2 * b + t, :], small[:, 104 + t:105 + t], None, ALU.mult)
                ins.then_inc(s["nh_ready"], 1)

            def affine(b, dst, bank_n, w, bias):
                for k in range(KT):
                    ins = dve.tensor_scalar(dst[:, k, :], bank[bank_n][:, 256 * k:256 * (k + 1)], cols_sb[:, w + k:w + k + 1],
                                            cols_sb[:, bias + k:bias + k + 1], ALU.mult, ALU.add)
                return ins

            def hidden_t(b):
                dve.wait_ge(s["m7_pe"], m7["NT", b] + 1)
                if b == 0:
                    dve.wait_ge(s["d_cols"], 16)
                else:
                    dve.wait_ge(s["h_ready"], b)
                ins = affine(b, hT, 7, B_L1W, B_L1B)
                ins.then_inc(s["m7_free"], 1)
                dve.wait_ge(s["m7_free"], m7["NT", b] + 1)
                dve.tensor_copy(small[:, 110:111], small[:, 109:110]).then_inc(s["hT_ready"], 1)

            for p in range(NPX):
                b, k = divmod(p, XP)
                g, t, heads = piece(k)
                dve.wait_ge(s["s_pe"], p + 1)
                if p >= 2:
                    dve.wait_ge(s["s_exp"], p - 1)
                dve.tensor_reduce(nxm[:, p % 2, 0:len(heads)], S_B[p % 2][:, :].rearrange("p (h n) -> p h n", h=len(heads)),
                                  AX.X, ALU.max, negate=True).then_inc(s["s_max"], 1)
                if p >= 1 and (p - 1) % 3 != 2:
                    pt_copy(dve, p - 1)
                if k == 0 and b + 1 < B:
                    norm_q(b + 1)
                if k == 2 and b:
                    norm_out(b - 1)
                if k == 4 and b + 1 < B:
                    pack(b + 1, 0)
                if k == 6 and b:
                    residual(b - 1)
                if k == 8 and b + 1 < B:
                    pack(b + 1, 1)
                if k == 9 and b:
                    hidden_t(b - 1)
            norm_out(B - 1)
            residual(B - 1)
            hidden_t(B - 1)

            def rope_cos(n, q, c, cols_):
                dve.wait_ge(s["chunk_f"], n + 1)
                col = C_RCOSK if c % 2 else C_RCOSQ
                dve.tensor_tensor(QT[:, c, cols_].rearrange("p (b t) -> p b t", b=2), qk_f[:, q, :].rearrange("p (b t) -> p b t", b=2),
                                  cst_sb[:, col:col + 256].unsqueeze(1).to_broadcast([P, 2, 256]), ALU.mult).then_inc(s["chunk_cos"], 1)

            def rope_add(n, q, c, cols_):
                dve.wait_ge(s["chunk_sw"], n + 1)
                dve.wait_ge(s["chunk_cos"], n + 1)
                dve.tensor_tensor(QT[:, c, cols_], QT[:, c, cols_], qk_sw[:, q, :], ALU.add).then_inc(s["rope_done"], 1)

            def v_out(m, b, p):
                dve.wait_ge(s["v_pe"], m + 1)
                bias = bv_sb[:, bass.ds(256 * p, 256)].unsqueeze(1).to_broadcast([P, 2, 256])
                dve.tensor_tensor(V[:, 2 * b:2 * b + 2, :], bank[6][:, :].rearrange("p (t n) -> p t n", t=2), bias, ALU.add).then_inc(s["v_ready"], 1)

            groups = (slice(0, 512), slice(512, 1024))
            dve.wait_ge(s["we_ready"], 4)
            dve.wait_ge(s["d_bv"], 16)
            for n in range(LEAD):
                rope_cos(n, n % 2, n % 4, groups[n // 4])
                if n < 2:
                    v_out(n, n, 0)
                if 1 <= n <= 4:
                    rope_add(n - 1, (n - 1) % 2, n - 1, groups[0])
            dve.wait_ge(s["yacc_init"], B)

            def step(i, j):
                T = U * i + j
                q = j % 2
                if unit(i, j, 0):
                    dve.wait_ge(s["b_s"], T + 1)
                    if unit(i, j, 2):
                        dve.wait_ge(s["b_exp"], 2 * (T - 1))
                    dve.memset(small[:, 111:112], 0.0)
                    dve.tensor_tensor_reduce(sm[:, q, 0:P], S_B[q][:, 0:P], cst_sb[:, C_MASK + P:C_MASK + 256], 1.0, 3e38,
                                             ALU.add, ALU.min, nm[:, q, 0:1])
                    dve.tensor_tensor_reduce(sm[:, q, P:3 * P], S_B[q][:, P:3 * P], cst_sb[:, C_MASK:C_MASK + 256], 1.0, 3e38,
                                             ALU.add, ALU.min, nm[:, q, 1:2]).then_inc(s["b_max"], 1)
                if unit(i, j, -4):
                    rope_add(T + 4, q, j % 4, groups[(j + 4) // 4 % 2])
                m = (j + 2) // 2
                if j % 2 == 0 and (not isinstance(i, int) or (T > 0 and B * i + m < B * NP)):
                    v_out(B * i + m, m % B, i + m // B)
                if j % 2 == 1 and unit(i, j, 5):
                    m = (j - 5) // 2
                    dve.wait_ge(s["b_wo"], B * i + m + 1)
                    b = m % B
                    y = yacc[:, 2 * b:2 * b + 2, :].rearrange("p t n -> p (t n)")
                    dve.tensor_tensor(y, y, bank[7][:, :], ALU.add).then_inc(s["b_yadd"], 1)
                if unit(i, j, 0):
                    dve.wait_ge(s["b_exp"], 2 * (T + 1))
                    dve.reciprocal(rs[:, q, :], rs[:, q, :]).then_inc(s["b_recip"], 1)
                    dve.wait_ge(s["b_recip"], T + 1)
                    dve.tensor_scalar(PR[:, q, 0:P], PR[:, q, 0:P], rs[:, q, 0:1], None, ALU.mult)
                    dve.tensor_scalar(PR[:, q, P:3 * P], PR[:, q, P:3 * P], rs[:, q, 1:2], None, ALU.mult).then_inc(s["b_norm"], 1)
                if unit(i, j, -LEAD):
                    c, g = chunk_at(j)
                    rope_cos(T + LEAD, q, c, groups[g])
                if unit(i, j, 2):
                    dve.wait_ge(s["b_oH"], T - 1)
                    h = oH[:, ((j - 2) // 2) % 2, q, :]
                    dve.tensor_tensor(oL[:, ((j - 2) // 2) % 2, q, :], bank[3][:, 0:256], h.bitcast(F32), ALU.subtract).then_inc(s["b_oL"], 1)

            steps(dve, step)

            for b in range(B):
                dve.wait_ge(s["b_yadd"], NU // 2 - B + b + 1)
                for t in range(2):
                    ins = dve.bn_stats(bnst[:, t, :], yacc[:, 2 * b + t, :])
                link(ins)
                for t in range(2):
                    ins = dve.bn_aggr(mv[:, 2 * b + t, :], bnst[:, t, :])
                link(ins)
                link(dve.tensor_scalar(SM(100, 2), mv[:, 2 * b:2 * b + 2, 1], EPS, None, ALU.add))
                rsqrt(SM(100, 2), SM(102, 2), SM(104, 2))
                if b:
                    dve.wait_ge(s["c_tr"], b)
                for t in range(2):
                    n = 2 * b + t
                    ins = dve.tensor_scalar(nh[:, t, :], yacc[:, n, :], mv[:, n, 0:1], small[:, 102 + t:103 + t], ALU.subtract, ALU.mult)
                ins.then_inc(s["c_nh"], 1)
                dve.wait_ge(s["c_tr"], b + 1)
                affine(b, h2T[:, :, 256 * b:256 * (b + 1)], 4, B_L2W, B_L2B).then_inc(s["c_hT"], 1)
            Gt = lambda a, n: gate[:, a:a + n]
            V3 = lambda a: gate[:, a:a + 32].rearrange("p (t e) -> p t e", e=E)
            dve.wait_ge(s["c_logit"], 1)
            link(dve.tensor_copy(Gt(0, 32), bank[5][:, 0:32]))
            link(dve.tensor_reduce(Gt(96, 8), V3(0), AX.X, ALU.max))
            dve.tensor_tensor(V3(32), V3(0), Gt(96, 8).unsqueeze(2).to_broadcast([P, NT, E]), ALU.subtract).then_inc(s["c_gmax"], 1)
            dve.wait_ge(s["c_gexp"], 1)
            link(dve.tensor_reduce(Gt(104, 8), V3(64), AX.X, ALU.add))
            link(dve.reciprocal(Gt(112, 8), Gt(104, 8)))
            link(dve.tensor_tensor(V3(64), V3(64), Gt(112, 8).unsqueeze(2).to_broadcast([P, NT, E]), ALU.mult))
            Q4 = lambda a: gate[:, a:a + 128].rearrange("p (t e f) -> p t e f", e=E, f=E)
            for e in range(E):
                pe_ = V3(64)[:, :, e:e + 1].to_broadcast([P, NT, E])
                dve.tensor_tensor(Q4(120)[:, :, e, :], V3(64), pe_, ALU.is_gt)
                link(dve.tensor_tensor(Q4(248)[:, :, e, :], V3(64), pe_, ALU.is_equal))
            tie = cst_sb[:, C_TIE:C_TIE + 16].unsqueeze(1).to_broadcast([P, NT, 16])
            q16 = gate[:, 248:376].rearrange("p (t f) -> p t f", t=NT)
            link(dve.tensor_tensor(q16, q16, tie, ALU.mult))
            link(dve.tensor_tensor(Gt(120, 128), Gt(120, 128), Gt(248, 128), ALU.add))
            rank = gate[:, 408:440]
            link(dve.tensor_reduce(rank, gate[:, 120:248].rearrange("p (n f) -> p n f", f=E), AX.X, ALU.add))
            first, second = gate[:, 120:152], gate[:, 152:184]
            dve.tensor_scalar(first, rank, 0.0, None, ALU.is_equal)
            link(dve.tensor_scalar(second, rank, 1.0, None, ALU.is_equal))
            dve.tensor_tensor(Gt(184, 32), first, Gt(64, 32), ALU.mult)
            link(dve.tensor_tensor(Gt(216, 32), second, Gt(64, 32), ALU.mult))
            dve.tensor_reduce(Gt(376, 8), V3(184), AX.X, ALU.add)
            link(dve.tensor_reduce(Gt(384, 8), V3(216), AX.X, ALU.add))
            dve.tensor_tensor(Gt(392, 8), Gt(384, 8), Gt(376, 8), ALU.subtract).then_inc(s["c_gdiff"], 1)
            dve.wait_ge(s["c_gexp"], 2)
            link(dve.tensor_scalar(Gt(248, 8), Gt(400, 8), 1.0, None, ALU.add))
            link(dve.reciprocal(Gt(256, 8), Gt(248, 8)))
            link(dve.tensor_tensor(Gt(264, 8), Gt(256, 8), Gt(400, 8), ALU.mult))
            dve.tensor_tensor(V3(120), V3(120), Gt(256, 8).unsqueeze(2).to_broadcast([P, NT, E]), ALU.mult)
            link(dve.tensor_tensor(V3(152), V3(152), Gt(264, 8).unsqueeze(2).to_broadcast([P, NT, E]), ALU.mult))
            dve.tensor_tensor(Gt(0, 32), Gt(120, 32), Gt(152, 32), ALU.add).then_inc(s["c_comb"], 1)
            dve.wait_ge(s["c_combT_pe"], 1)
            dve.tensor_copy(combT[:, 0:4, :].rearrange("p t n -> p (t n)"), bank[2][0:E, :])
            dve.tensor_copy(combT[:, 4:8, :].rearrange("p t n -> p (t n)"), bank[3][0:E, :]).then_inc(s["c_combT"], 1)
            for b in range(B):
                dve.wait_ge(s["c_be"], b + 1)
                y = yacc[:, 2 * b:2 * b + 2, :].rearrange("p t n -> p (t n)")
                dve.tensor_tensor(y, y, bank[6 + b % 2][:, :], ALU.add).then_inc(s["c_init"], 1)
            dve.wait_ge(s["c_init"], B)

            def low(n):
                dve.wait_ge(s["c_gH"], n + 1)
                dve.tensor_tensor(GL[:, (n // 2) % 2, n % 2, :], G[:, n % 2, :], GH[:, (n // 2) % 2, n % 2, :].bitcast(F32),
                                  ALU.subtract).then_inc(s["c_gL"], 1)

            def accumulate(m):
                c, e = divmod(m, E)
                for hf in range(2):
                    dve.wait_ge(s["c_exp_pe"], 2 * m + hf + 1)
                    if m:
                        dve.wait_ge(s["c_acc"], 2 * m)
                    for t in range(2):
                        n = 4 * c + 2 * hf + t
                        ins = dve.scalar_tensor_tensor(yacc[:, n, :], bank[6 + hf][:, 256 * t:256 * (t + 1)],
                                                       gate[:, 4 * n + e:4 * n + e + 1], yacc[:, n, :], ALU.mult, ALU.add)
                    ins.then_inc(s["c_acc"], 1)
                if e == E - 1:
                    dve.wait_ge(s["c_acc"], 2 * m + 2)
                    for b in range(2 * c, 2 * c + 2):
                        y = yacc[:, 2 * b:2 * b + 2, :].rearrange("p t n -> p (t n)")
                        xb = x_sb[:, 2 * b:2 * b + 2, :].rearrange("p t n -> p (t n)")
                        dve.scalar_tensor_tensor(y, y, small[:, 97:98], xb, ALU.mult, ALU.add).then_inc(s["c_fin"], 1)

            for n in range(2 * NE):
                low(n)
                if n >= 3 and n % 2:
                    accumulate((n - 3) // 2)
            accumulate(2 * E - 1)

        @block.tensor
        def _(pe):
            pe.wait_ge(s["bf_ready"], 1)
            pe.wait_ge(s["d_cst"], 16)
            pe.wait_ge(s["kpack_ready"], 1)
            for b in range(B):
                if b:
                    pe.wait_ge(s["m7_free"], b)
                for g in range(XG):
                    for t in range(2):
                        ins = pe.transpose(bank_bf[1][:, (2 * g + t) * P:(2 * g + t + 1) * P],
                                           kpack[:, (2 * b + t) * XG + g, :, :].rearrange("p s d -> p (s d)"), ident_bf)
                ins.then_inc(s["m7_pe"], 1)

            def q_turn(b, X, t):
                n = m6["Q", b, X, t]
                pe.wait_ge(s["qpack_ready"], 2 * b + X + 1)
                if n:
                    pe.wait_ge(s["m6_free"], n)
                for h in range(8):
                    ins = pe.transpose(bank_bf[0][:, h * P:(h + 1) * P], qpack[:, X, t, h, :, :].rearrange("p s d -> p (s d)"), ident_bf)
                ins.then_inc(s["m6_pe"], 1)

            def out_turn(b):
                n = m6["OT", b]
                pe.wait_ge(s["on_ready"], b + 1)
                pe.wait_ge(s["m6_free"], n)
                for k in range(KT):
                    for t in range(2):
                        ins = pe.transpose(bank[6][:, (2 * k + t) * P:(2 * k + t + 1) * P], on[:, t, k * P:(k + 1) * P], ident)
                ins.then_inc(s["m6_pe"], 1)

            def out_project(b):
                n = m7["PJ", b]
                pe.wait_ge(s["m6_free"], m6["OT", b] + 1)
                pe.wait_ge(s["m7_free"], n)
                if b == 0:
                    pe.wait_ge(s["d_wout"], 16)
                for t in range(2):
                    for k in range(KT):
                        ins = pe.matmul(bank[7][:, 256 * t:256 * (t + 1)], onT[:, k, t, :], w_out_sb[:, k, :], start=(k == 0), stop=(k == 1))
                ins.then_inc(s["m7_pe"], 1)

            def norm_turn(b):
                n = m7["NT", b]
                pe.wait_ge(s["nh_ready"], b + 1)
                pe.wait_ge(s["m7_free"], n)
                for k in range(KT):
                    for t in range(2):
                        ins = pe.transpose(bank[7][:, (2 * k + t) * P:(2 * k + t + 1) * P], nh[:, t, k * P:(k + 1) * P], ident)
                ins.then_inc(s["m7_pe"], 1)

            def x_scores(p):
                b, k = divmod(p, XP)
                g, t, heads = piece(k)
                width = P * (t + 1)
                pe.wait_ge(s["m6_free"], m6["Q", b, k // 6, 1] + 1)
                if p == 0:
                    pe.wait_ge(s["m7_free"], B)
                if p >= 2:
                    pe.wait_ge(s["s_exp"], p - 1)
                for n, h in enumerate(heads):
                    pe.matmul(S_B[p % 2][:, n * width:(n + 1) * width], qT[:, h // 8, t, h % 8, :], kT[:, b, g, 0:width], start=True, stop=False)
                    ins = pe.matmul(S_B[p % 2][:, (n + 1) * width - P:(n + 1) * width], ident_bf, mask_bf, start=False, stop=True)
                ins.then_inc(s["s_pe"], 1)

            def x_turn(p):
                pe.wait_ge(s["s_exp"], p + 1)
                if p >= 2:
                    pe.wait_ge(s[copier(p - 2)[0]], copier(p - 2)[1])
                for n in range(4):
                    ins = pe.transpose(PT_B[p % 2][:, n * P:(n + 1) * P], PR[:, p % 2, n * P:(n + 1) * P], ident)
                ins.then_inc(s["pt_pe"], 1)

            def x_values(p):
                b, k = divmod(p, XP)
                g, t, heads = piece(k)
                pe.wait_ge(s[copier(p)[0]], copier(p)[1])
                if p == 0:
                    pe.wait_ge(s["va_ready"], 1 + B)
                if k == 0 and b:
                    pe.wait_ge(s["on_ready"], b)
                for n, h in enumerate(heads):
                    for kt in range(t + 1):
                        ins = pe.matmul(O_B[t][:, h * VW:(h + 1) * VW], PTs[:, p % 2, (n * (t + 1) + kt) * P:(n * (t + 1) + kt + 1) * P],
                                        vA[:, 2 * b + kt, g, :], start=(kt == 0), stop=(kt == t))
                ins.then_inc(s["pv_pe"], 1)

            q_turn(0, 0, 0)
            q_turn(0, 0, 1)
            for p in range(NPX + 2):
                b, k = divmod(p, XP)
                if p < NPX:
                    x_scores(p)
                    if k in (1, 2):
                        q_turn(b, 1, k - 1)
                    if k == 3 and b:
                        out_turn(b - 1)
                    if k == 5 and b:
                        out_project(b - 1)
                    if k == 9 and b:
                        norm_turn(b - 1)
                    if k in (7, 9) and b + 1 < B:
                        q_turn(b + 1, 0, (k - 7) // 2)
                if 1 <= p <= NPX:
                    x_turn(p - 1)
                if p >= 2:
                    x_values(p - 2)
            out_turn(B - 1)
            out_project(B - 1)
            norm_turn(B - 1)

            def three(outp, pairs):
                n = 3 * len(pairs)
                m = 0
                for (aH, aL), (bH, bL) in pairs:
                    for l, r in ((aH, bL), (aL, bH), (aH, bH)):
                        ins = pe.matmul(outp, l, r, start=(m == 0), stop=(m == n - 1))
                        m += 1
                return ins

            def project_qk(n, q, c, g, guard):
                if guard:
                    pe.wait_ge(s["chunk_f"], n - 1)
                cut = slice(512 * g, 512 * (g + 1))
                three(O_B[q][:, :], [((wqkH[:, c, k, :], wqkL[:, c, k, :]), (hH[:, k, cut], hL[:, k, cut])) for k in range(KT)]).then_inc(s["chunk_pe"], 1)

            def project_v(m, b, guard):
                if guard:
                    pe.wait_ge(s["v_ready"], m)
                for t in range(2):
                    cut = slice((2 * b + t) * P, (2 * b + t + 1) * P)
                    ins = three(bank[6][:, 256 * t:256 * (t + 1)], [((hH[:, k, cut], hL[:, k, cut]), (wvH[:, k, :], wvL[:, k, :])) for k in range(KT)])
                ins.then_inc(s["v_pe"], 1)

            pe.wait_ge(s["h_ready"], B)
            pe.wait_ge(s["m7_free"], len(M7))
            pe.wait_ge(s["m6_free"], len(M6))
            pe.wait_ge(s["on_ready"], B)
            pe.wait_ge(s["wv_ready"], 1)
            pe.wait_ge(s["wqk_ready"], 4)
            for n in range(LEAD):
                project_qk(n, n % 2, n % 4, n // 4, n >= 2)
                if n < 2:
                    project_v(n, n, n >= 1)

            def step(i, j):
                T = U * i + j
                q = j % 2
                if unit(i, j, 0):
                    b, r = j // 2, j % 2
                    pe.wait_ge(s["rope_done"], U * i + 4 * (j // 4) + 2 * r + 2)
                    if unit(i, j, 2):
                        pe.wait_ge(s["b_max"], T - 1)
                    kt_ = QT[:, 2 * r + 1, 256 * b:256 * (b + 1)]
                    pe.matmul(S_B[q][:, 0:P], QT[:, 2 * r, 256 * b:256 * b + P], kt_[:, 0:P], start=True, stop=True)
                    pe.matmul(S_B[q][:, P:3 * P], QT[:, 2 * r, 256 * b + P:256 * (b + 1)], kt_, start=True, stop=True).then_inc(s["b_s"], 1)
                if unit(i, j, -LEAD):
                    if 2 <= j < 6:
                        pe.wait_ge(s["wqk_ready"], 4 * (i + 1) + j - 2 + 1)
                    c, g = chunk_at(j)
                    project_qk(T + LEAD, q, c, g, True)
                if unit(i, j, 1):
                    pe.wait_ge(s["b_norm"], T)
                    if unit(i, j, 2):
                        pe.wait_ge(s["b_ptcopy"], T - 1)
                    for n in range(3):
                        ins = pe.transpose(bank[2][:, n * P:(n + 1) * P], PR[:, 1 - q, n * P:(n + 1) * P], ident)
                    ins.then_inc(s["b_pt"], 1)
                if unit(i, j, 2):
                    u = (j - 2) % U
                    b, r = u // 2, u % 2
                    pe.wait_ge(s["b_ptcopy"], T - 1)
                    pe.wait_ge(s["v_ready"], 4 * i + (j - 2) // 2 + 1)
                    if unit(i, j, 3):
                        pe.wait_ge(s["b_oL"], T - 2)
                    pe.matmul(bank[3][:, 0:256], V[:, 2 * b, r * HD:(r + 1) * HD], PTs[:, q, 0:256], start=True, stop=False)
                    pe.matmul(bank[3][:, P:256], V[:, 2 * b + 1, r * HD:(r + 1) * HD], PTs[:, q, 256:384], start=False, stop=True).then_inc(s["b_pv"], 1)
                if v_event(i, j):
                    m = (j + 3) // 2
                    pe.wait_ge(s["wv_ready"], i + m // B + 1)
                    project_v(B * i + m, m % B, True)
                if j % 2 == 0 and unit(i, j, 4):
                    mo = (j - 4) // 2
                    pe.wait_ge(s["b_oL"], 8 * i + 2 * mo + 2)
                    pe.wait_ge(s["wo_ready"], i + mo // 4 + 1)
                    if not (isinstance(i, int) and i == 0 and mo == 0):
                        pe.wait_ge(s["b_yadd"], 4 * i + mo)
                    for t in range(2):
                        ins = three(bank[7][:, 256 * t:256 * (t + 1)],
                                    [((oH[:, mo % 2, r, t * P:(t + 1) * P], oL[:, mo % 2, r, t * P:(t + 1) * P]), (woH[:, r, :], woL[:, r, :])) for r in range(2)])
                    ins.then_inc(s["b_wo"], 1)

            steps(pe, step)

            for b in range(B):
                pe.wait_ge(s["c_nh"], b + 1)
                if b:
                    pe.wait_ge(s["c_hT"], b)
                for k in range(KT):
                    for t in range(2):
                        ins = pe.transpose(bank[4][:, (2 * k + t) * P:(2 * k + t + 1) * P], nh[:, t, k * P:(k + 1) * P], ident)
                ins.then_inc(s["c_tr"], 1)
            pe.wait_ge(s["c_hT"], B)
            pe.wait_ge(s["d_small"], 32)
            for n in range(NT):
                for k in range(KT):
                    ins = pe.matmul(bank[5][:, E * n:E * (n + 1)], h2T[:, k, n * P:(n + 1) * P], w_gate_sb[:, k, :], start=(k == 0), stop=(k == 1))
            ins.then_inc(s["c_logit"], 1)

            def middle(n):
                c, m = divmod(n, NE)
                if n >= 2:
                    pe.wait_ge(s["c_gelu"], n - 1)
                if m == 0:
                    pe.wait_ge(s["c_h"], 2 * c + 2)
                cut = slice(512 * c, 512 * (c + 1))
                three(bank[n % 2][:, :], [((we1H[:, k, m * P:(m + 1) * P], we1L[:, k, m * P:(m + 1) * P]), (hH[:, k, cut], hL[:, k, cut])) for k in range(KT)]).then_inc(s["c_mid"], 1)

            def expert_out(m):
                c, e = divmod(m, E)
                pe.wait_ge(s["c_gL"], 2 * m + 2)
                for hf in range(2):
                    if m:
                        pe.wait_ge(s["c_acc"], 2 * (m - 1) + hf + 1)
                    for t in range(2):
                        cut = slice((2 * hf + t) * P, (2 * hf + t + 1) * P)
                        ins = three(bank[6 + hf][:, 256 * t:256 * (t + 1)],
                                    [((GH[:, m % 2, k, cut], GL[:, m % 2, k, cut]), (we2H[:, 2 * e + k, :], we2L[:, 2 * e + k, :])) for k in range(IT)])
                    ins.then_inc(s["c_exp_pe"], 1)

            middle(0)
            middle(1)
            pe.wait_ge(s["c_comb"], 1)
            for n in range(NT):
                ins = pe.transpose(bank[2 + n // 4][0:E, (n % 4) * P:(n % 4 + 1) * P], gate[:, E * n:E * (n + 1)], ident)
            ins.then_inc(s["c_combT_pe"], 1)
            pe.wait_ge(s["c_combT"], 1)
            for b in range(B):
                if b >= 2:
                    pe.wait_ge(s["c_init"], b - 1)
                for t in range(2):
                    ins = pe.matmul(bank[6 + b % 2][:, 256 * t:256 * (t + 1)], combT[:, 2 * b + t, :], be2_sb[:, :], start=True, stop=True)
                ins.then_inc(s["c_be"], 1)
            pe.wait_ge(s["c_init"], B)
            for n in range(2, 2 * NE):
                middle(n)
                if n % 2:
                    expert_out((n - 3) // 2)
            expert_out(2 * E - 1)


def constants():
    f = np.float32
    c = np.zeros((P, C_END), f)
    c[:, C_ID:C_ID + P] = np.eye(P, dtype=f)
    above = np.triu(np.ones((P, P), f), 1)
    c[:, C_MASK + P:C_MASK + 256] = above * f(BIG)

    def angles(width):
        inv = f(1.0) / f(10000.0) ** (np.arange(0, width, 2, dtype=f) / f(width))
        a = np.arange(S, dtype=f)[:, None] * inv[None, :].astype(f)
        return np.cos(a).astype(f), np.sin(a).astype(f)

    co, si = angles(XD)
    for t in range(2):
        c[:, C_XCOS + t * XD:C_XCOS + (t + 1) * XD] = np.concatenate([co, co], 1)[t * P:(t + 1) * P]
        c[:, C_XSIN + t * XD:C_XSIN + (t + 1) * XD] = np.concatenate([-si, si], 1)[t * P:(t + 1) * P]
    co, si = angles(HD)
    scale = f(-1.0 / np.sqrt(HD))
    cos_t, sin_t = np.concatenate([co, co], 1).T, np.concatenate([-si, si], 1).T
    c[:, C_RCOSQ:C_RCOSQ + 256] = cos_t * scale
    c[:, C_RSINQ:C_RSINQ + 256] = sin_t * scale
    c[:, C_RCOSK:C_RCOSK + 256] = cos_t
    c[:, C_RSINK:C_RSINK + 256] = sin_t
    c[:, C_TIE:C_TIE + 16] = np.tril(np.ones((E, E), f), -1).reshape(1, 16)
    return c


def kernel(**inputs):
    import concourse.bacc as bacc
    from concourse.bass_utils import run_bass_kernel_spmd

    a = {k: np.ascontiguousarray(v) for k, v in inputs.items()}
    w = {k[7:]: v for k, v in a.items() if k.startswith("L0_ffn_")}

    def kxn(m, n):
        return m.reshape(n, P, *m.shape[1:]).swapaxes(0, 1)

    def col(v):
        return v.reshape(-1, P).T

    def pairs(m):
        return m.reshape(KT, P, NP, 256).transpose(2, 1, 0, 3)

    c = constants()
    arrays = {
        "x": a["x"],
        "ctx": a["ctx_512"],
        "cst": c,
        "cols": np.concatenate([col(w["bq"]), col(w["bk"]), col(w["ln1_w"]), col(w["ln1_b"]), col(w["ln2_w"]),
                                col(w["ln2_b"]), col(w["be1"])], 1),
        "rows": np.concatenate([a["L0_xattn_q_norm_w"], a["L0_xattn_k_norm_w"], w["bo"], a["g_xattn"], a["g_ffn"]])[None],
        "bv": w["bv"][None],
        "wqkv": np.stack([pairs(w["wq"]), pairs(w["wk"]), pairs(w["wv"])], 2),
        "wo": w["wo"].reshape(NP, 2, P, D).swapaxes(1, 2),
        "w_out_t": kxn(a["L0_xattn_w_out"].T, KT),
        "w_gate": kxn(w["w_gate"], KT),
        "be2": w["be2"],
        "we1": kxn(w["we1"].transpose(1, 0, 2).reshape(D, E * I), KT).reshape(P, -1),
        "we2": kxn(w["we2"].reshape(E * I, D), NE).reshape(P, -1),
    }
    nc = bacc.Bacc("TRN2", target_bir_lowering=False, num_devices=1)
    args, arrays = [], {f"in_{k}": np.ascontiguousarray(v) for k, v in arrays.items()}
    for name, v in arrays.items():
        args.append(nc.dram_tensor(name, v.shape, mybir.dt.from_np(v.dtype), kind="ExternalInput").ap())
    args.append(nc.dram_tensor("out_y", (B, S, D), F32, kind="ExternalOutput").ap())
    build_kernel(nc, *args)
    r = run_bass_kernel_spmd(nc, [arrays], core_ids=[0])
    return r.results[0]["out_y"]
```

```python
from contextlib import ExitStack

import numpy as np

import concourse.bass as bass
from concourse import mybir

F32 = mybir.dt.float32
F32R = mybir.dt.float32r
BF16 = mybir.dt.bfloat16
I32 = mybir.dt.int32
ALU = mybir.AluOpType
ACT = mybir.ActivationFunctionType
AX = mybir.AxisListType

P = 128
B, S, D = 4, 256, 256
NT = B * S // P
KT = D // P
XH, XG, XD = 16, 4, 16
XS = 8
XP = 12
VP, VZ = 128, 96
H, HD = 16, 128
NP = H // 2
U = 2 * B
NU = NP * U
LEAD = 6
E, I, IT = 4, 256, 2
NE = E * IT
WE_CUT = (KT * E * I + NE * D) // NP
BIG = 1e30
EPS = 1e-5
RSQRT_SEED = 1597463007.0

C_ID, C_MASK, C_XCOS, C_XSIN, C_RCOSQ, C_RSINQ, C_RCOSK, C_RSINK, C_TIE = 0, 128, 384, 416, 448, 704, 960, 1216, 1472
C_END = 1488
B_BQ, B_BK, B_L1W, B_L1B, B_L2W, B_L2B, B_BE1, B_END = 0, 16, 32, 34, 36, 38, 40, 48
R_QW, R_KW, R_BO, R_GX, R_GF, R_END = 0, 256, 320, 576, 577, 578
W_Q, W_K, W_V = 0, 1, 2


def build_kernel(nc, x, ctx_in, cst, cols, rows, bv, wqkv, wo, w_out_t, w_gate, be2, we, out):
    with ExitStack() as stack:
        def sb(name, shape, dt=F32):
            return stack.enter_context(nc.sbuf_tensor(name, shape, dt))

        def ps(name, shape=(P, 512), dt=F32):
            return stack.enter_context(nc.psum_tensor(name, list(shape), dt))

        def sem(name):
            return stack.enter_context(nc.semaphore(name))

        x_sb = sb("x_sb", [P, NT, D])
        ctx_sb = sb("ctx_sb", [P, NT, 64])
        cst_sb = sb("cst_sb", [P, C_END])
        bf_sb = sb("bf_sb", [P, 256], BF16)
        cols_sb = sb("cols_sb", [P, B_END])
        rows_sb = sb("rows_sb", [P, R_END])
        bv_sb = sb("bv_sb", [P, H * HD])
        w_out_sb = sb("w_out_sb", [P, KT, D])
        w_gate_sb = sb("w_gate_sb", [P, KT, E])
        be2_sb = sb("be2_sb", [E, D])
        yacc = sb("yacc", [P, NT, D])
        hH = sb("hH", [P, KT, NT * P], F32R)
        hL = sb("hL", [P, KT, NT * P], F32R)
        mv = sb("mv", [P, NT, 2])
        bnst = sb("bnst", [P, NT, 6])
        small = sb("small", [P, 160])
        stg = sb("stg", [P, 3, KT, 256])
        stgo = sb("stgo", [P, 2, D])
        qk_parts = sb("qk_parts", [P, 2, 4 * KT * HD], F32R)
        wqkH = qk_parts[:, 0, :].rearrange("p (c k n) -> p c k n", c=4, k=KT)
        wqkL = qk_parts[:, 1, :].rearrange("p (c k n) -> p c k n", c=4, k=KT)
        wvH = sb("wvH", [P, KT, 256], F32R)
        wvL = sb("wvL", [P, KT, 256], F32R)
        woH = sb("woH", [P, 2, D], F32R)
        woL = sb("woL", [P, 2, D], F32R)
        qk_bias = sb("qk_bias", [P, 4])
        qk_room = sb("qk_room", [P, 4, 512])
        qk_f = qk_room[:, 0:2, :]
        qk_sw = qk_room[:, 2:4, :]
        room = sb("room", [P, VZ + 4 * NT * P])
        QT = room[:, 0:4 * NT * P].rearrange("p (c n) -> p c n", c=4)
        V = sb("V", [P, NT, 256])
        sm = sb("sm", [P, 2, 384])
        nm = sb("nm", [P, 2, 2])
        rs = sb("rs", [P, 2, 2])
        PR = sb("PR", [P, 2, 512])
        PTs = sb("PTs", [P, 2, 512])
        o_parts = sb("o_parts", [P, 2, 1024], F32R)
        oH = o_parts[:, 0, :].rearrange("p (m r n) -> p m r n", m=2, r=2)
        oL = o_parts[:, 1, :].rearrange("p (m r n) -> p m r n", m=2, r=2)
        weH = sb("weH", [P, 4096], F32R)
        weL = sb("weL", [P, 4096], F32R)
        stge = sb("stge", [P, WE_CUT])
        we1H = weH[:, 0:2048].rearrange("p (k n) -> p k n", k=KT)
        we1L = weL[:, 0:2048].rearrange("p (k n) -> p k n", k=KT)
        we2H = weH[:, 2048:4096].rearrange("p (e n) -> p e n", e=NE)
        we2L = weL[:, 2048:4096].rearrange("p (e n) -> p e n", e=NE)
        G = sb("G", [P, 2, 512])
        GH = o_parts[:, :, :].rearrange("p m (k n) -> p m k n", k=IT)
        GL = qk_parts[:, :, :].rearrange("p m (k n) -> p m k n", k=IT)
        gate = sb("gate", [P, 512])
        combT = sb("combT", [E, NT, P])
        qn = sb("qn", [P, 2, D])
        kpack = V[:, :, :].rearrange("p t n -> p (t n)").bitcast(BF16).rearrange("p (n s d) -> p n s d", s=XS, d=XD)
        qpack = sb("qpack", [P, 2, 2, 8, XS, XD], BF16)
        kT = sb("kT", [P, B, XG, 256], BF16)
        qT = qk_room[:, :, :].rearrange("p a n -> p (a n)").bitcast(BF16).rearrange("p (x t h n) -> p x t h n", x=2, t=2, h=8)
        v_slots = room[:, VZ:VZ + NT * XG * VP].rearrange("p (n d) -> p n d", d=VP)
        oT = V[:, 0:2, :]
        WC = sb("WC", [P, 2, 2, P])
        WS = sb("WS", [P, 2, 2, P])
        qf, qf2, qr = G[:, 0, 0:256], G[:, 0, 256:512], G[:, 1, 0:256]
        on = sb("on", [P, 2, D])
        onT = sb("onT", [P, KT, 2, P])
        nxm = sb("nxm", [P, 2, 4])
        rden = sb("rden", [P, 2, 2, 4])
        WKC = sb("WKC", [P, 2, 64])
        WKS = sb("WKS", [P, 2, 64])
        kf = yacc[:, 0:2, :].rearrange("p t n -> p (t n)").rearrange("p (t n) -> p t n", t=NT)
        kf2 = yacc[:, 2:4, :].rearrange("p t n -> p (t n)").rearrange("p (t n) -> p t n", t=NT)
        kr = yacc[:, 4:6, :].rearrange("p t n -> p (t n)").rearrange("p (t n) -> p t n", t=NT)

        nh = sb("nh", [P, 2, D])
        hT = sm[:, :, :].rearrange("p a n -> p (a n)")[:, 0:512].rearrange("p (k n) -> p k n", k=KT)

        bank = [ps(f"bank{n}") for n in range(8)]
        S_B = bank[0:2]
        PT_B = bank[2:4]
        O_B = bank[4:6]
        M_B = bank[6:8]

        ident = cst_sb[:, C_ID:C_ID + P]
        ident_bf = bf_sb[:, 0:P]
        mask_bf = bf_sb[:, P:2 * P]

        names = """d_x0 d_x1 d_x2 d_x3 d_ctx d_cst d_cols d_rows d_bv d_wout d_small d_wqkv d_wo d_we d_sw0 d_sw1 d_out
        bf_ready dve_seq pool_seq ssk_done wtab_ready va_ready qn_ready q_parts qpack_ready kpack_ready
        m6_pe m7_pe m6_free m7_free s_pe s_max s_exp pt_pe pt_copy_act pt_copy_dve pv_pe oT_ready o_pe o_done tanh_done
        nh_ready yacc_init hT_ready hH_ready h_ready we_half we_ready
        wqk_ready wqk_half wqk_bias wv_ready wv_half wo_ready wo_half b_recip c_gmax c_gexp c_gdiff chunk_pe chunk_f chunk_cos chunk_sw rope_done
        b_s b_max b_exp b_norm b_pt b_ptcopy b_pv b_oH b_oL b_wo b_yadd v_pe v_ready
        c_nh c_tr c_hT c_hH c_h c_logit c_comb c_combT_pe c_combT c_be c_init c_mid c_gelu c_gH c_gL c_exp_pe c_acc c_fin"""
        s = {n: sem(n) for n in names.split()}

        def wait(eng, name, value):
            eng.wait_ge(s[name], value)

        x_v = x.rearrange("b (t p) d -> p (b t) d", p=P)
        ctx_v = ctx_in.rearrange("b (t p) d -> p (b t) d", p=P)
        out_v = out.rearrange("b (t p) d -> p (b t) d", p=P)

        def piece(k):
            g, j = divmod(k, 3)
            return (g, 0, [4 * g + n for n in range(4)]) if j == 0 else (g, 1, [4 * g + 2 * (j - 1) + n for n in range(2)])

        M6, M7 = [("Q", 0, 0, 0), ("Q", 0, 0, 1)], [("K", b) for b in range(B)]
        for b in range(B):
            M6 += [("Q", b, 1, 0), ("Q", b, 1, 1)] + ([("OT", b - 1)] if b else [])
            M6 += [("Q", b + 1, 0, 0), ("Q", b + 1, 0, 1)] if b + 1 < B else []
            M7 += [("PJ", b), ("NT", b)]
        M6 += [("OT", B - 1)]
        m6 = {e: n for n, e in enumerate(M6)}
        m7 = {e: n for n, e in enumerate(M7)}
        NPX = XP * B

        def copied_by_act(p):
            return p % 3 != 0

        def copier(p):
            by_act = [copied_by_act(n) for n in range(p + 1)]
            return ("pt_copy_act", sum(by_act)) if by_act[p] else ("pt_copy_dve", p + 1 - sum(by_act))

        def steps(eng, step, peeled=1):
            for j in range(U):
                step(0, j)
            with eng.Fori(1, NP - peeled) as i:
                for j in range(U):
                    step(i, j)
            for i in range(NP - peeled, NP):
                for j in range(U):
                    step(i, j)
            for j in range(4):
                step(NP, j)

        def unit(i, j, lag):
            if not isinstance(i, int):
                return True
            return 0 <= U * i + j - lag < NU

        def chunk_at(j):
            return (j + LEAD) % 4, (j + LEAD) // 4 % 2

        def v_event(i, j):
            return j % 2 == 1 and (not isinstance(i, int) or (i < NP and B * i + (j + 3) // 2 < B * NP))

        def pt_copy(eng, p):
            eng.wait_ge(s["pt_pe"], p + 1)
            if p >= 2:
                eng.wait_ge(s["pv_pe"], p - 1)
            copy = eng.tensor_copy if eng is nc.vector else eng.copy
            copy(PTs[:, p % 2, :], PT_B[p % 2][:, :]).then_inc(s[copier(p)[0]], 1)

        h2T = qk_room[:, :, :].rearrange("p a n -> p (a n)").rearrange("p (k n) -> p k n", k=KT)

        def out_bank(m, hf):
            return bank[(6, 2)[m % 2] + hf]

        bank_bf = [bank[n][:, :].bitcast(BF16) for n in (6, 7)]
        block = stack.enter_context(nc.Block())

        @block.sync
        def _(sp):
            sp.dma_start(cst_sb[:, :], cst).then_inc(s["d_cst"], 16)
            sp.dma_start(ctx_sb[:, :, :], ctx_v).then_inc(s["d_ctx"], 16)
            sp.dma_start(rows_sb[:, :], rows.to_broadcast([P, R_END])).then_inc(s["d_rows"], 16)
            for b in range(B):
                sp.dma_start(x_sb[:, 2 * b:2 * b + 2, :], x_v[:, 2 * b:2 * b + 2, :]).then_inc(s[f"d_x{b}"], 16)
            sp.dma_start(cols_sb[:, :], cols).then_inc(s["d_cols"], 16)
            sp.dma_start(stg[:, :, :, :], wqkv[0]).then_inc(s["d_wqkv"], 16)
            sp.dma_start(stgo[:, :, :], wo[0]).then_inc(s["d_wo"], 16)
            sp.dma_start(w_out_sb[:, :, :], w_out_t).then_inc(s["d_wout"], 16)
            sp.dma_start(stge[:, :], we[0]).then_inc(s["d_we"], 16)
            sp.dma_start(w_gate_sb[:, :, :], w_gate).then_inc(s["d_small"], 16)
            sp.dma_start(be2_sb[:, :], be2).then_inc(s["d_small"], 16)
            sp.dma_start(bv_sb[:, :], bv.to_broadcast([P, H * HD])).then_inc(s["d_bv"], 16)
            sp.wait_ge(s["wv_ready"], 1)
            sp.wait_ge(s["wqk_ready"], 4)
            sp.dma_start(stg[:, :, :, :], wqkv[1]).then_inc(s["d_wqkv"], 16)
            sp.wait_ge(s["wo_ready"], 1)
            sp.dma_start(stgo[:, :, :], wo[1]).then_inc(s["d_wo"], 16)

            def swap(n, q):
                sp.wait_ge(s["chunk_f"], n + 1)
                sp.dma_start(qk_sw[0:64, q, :], qk_f[64:128, q, :]).then_inc(s[f"d_sw{q}"], 16)
                sp.dma_start(qk_sw[64:128, q, :], qk_f[0:64, q, :]).then_inc(s[f"d_sw{q}"], 16)

            for n in range(LEAD):
                swap(n, n % 2)

            def step(i, j):
                if unit(i, j, -LEAD):
                    swap(U * i + j + LEAD, j % 2)
            steps(sp, step)
            for b in range(B):
                sp.wait_ge(s["c_fin"], b + 1)
                sp.dma_start(out_v[:, 2 * b:2 * b + 2, :], yacc[:, 2 * b:2 * b + 2, :]).then_inc(s["d_out"], 16)
            sp.wait_ge(s["d_out"], 16 * B)

        @block.gpsimd
        def _(pool):
            seq = [0]

            def link(ins):
                seq[0] += 1
                ins.then_inc(s["pool_seq"], 1)
                pool.wait_ge(s["pool_seq"], seq[0])

            pool.wait_ge(s["d_rows"], 16)
            pool.wait_ge(s["d_cst"], 16)
            for t in range(2):
                def table(col, heads):
                    return cst_sb[:, col + t * XD:col + (t + 1) * XD].unsqueeze(1).to_broadcast([P, heads, XD])
                w = rows_sb[:, R_KW:R_KW + 64].rearrange("p (h d) -> p h d", d=XD)
                c, sn = table(C_XCOS, 4), table(C_XSIN, 4)
                wks = WKS[:, t, :].rearrange("p (h d) -> p h d", d=XD)
                pool.tensor_tensor(WKC[:, t, :].rearrange("p (h d) -> p h d", d=XD), w, c, ALU.mult).then_inc(s["wtab_ready"], 1)
                pool.tensor_tensor(wks[:, :, 0:8], w[:, :, 8:16], sn[:, :, 0:8], ALU.mult).then_inc(s["wtab_ready"], 1)
                pool.tensor_tensor(wks[:, :, 8:16], w[:, :, 0:8], sn[:, :, 8:16], ALU.mult).then_inc(s["wtab_ready"], 1)
            for X in range(2):
                for t in range(2):
                    c = cst_sb[:, C_XCOS + t * XD:C_XCOS + (t + 1) * XD].unsqueeze(1).to_broadcast([P, 8, XD])
                    sn = cst_sb[:, C_XSIN + t * XD:C_XSIN + (t + 1) * XD].unsqueeze(1).to_broadcast([P, 8, XD])
                    w = rows_sb[:, R_QW + X * P:R_QW + (X + 1) * P].rearrange("p (h d) -> p h d", d=XD)
                    ws = WS[:, X, t, :].rearrange("p (h d) -> p h d", d=XD)
                    pool.tensor_tensor(WC[:, X, t, :].rearrange("p (h d) -> p h d", d=XD), w, c, ALU.mult)
                    pool.tensor_tensor(ws[:, :, 0:8], w[:, :, 8:16], sn[:, :, 0:8], ALU.mult)
                    last = pool.tensor_tensor(ws[:, :, 8:16], w[:, :, 0:8], sn[:, :, 8:16], ALU.mult)
            link(last)

            def prep(b, X):
                if X == 0:
                    pool.wait_ge(s["qn_ready"], b + 1)
                if b:
                    pool.wait_ge(s["m6_pe"], m6["Q", b - 1, X, 1] + 1)
                qv = qn[:, :, X * P:(X + 1) * P]
                q4 = qv.rearrange("p t (h d) -> p t h d", d=XD)
                g4 = qf2[:, :].rearrange("p (t h d) -> p t h d", t=2, d=XD)
                w4 = WS[:, X, :, :].rearrange("p t (h d) -> p t h d", d=XD)
                pool.tensor_tensor(qf[:, :].rearrange("p (t n) -> p t n", t=2), qv, WC[:, X, :, :], ALU.mult)
                for t in range(2):
                    pool.tensor_tensor(g4[:, t, :, 0:8], q4[:, t, :, 8:16], w4[:, t, :, 0:8], ALU.mult)
                    last = pool.tensor_tensor(g4[:, t, :, 8:16], q4[:, t, :, 0:8], w4[:, t, :, 8:16], ALU.mult)
                link(last)
                link(pool.tensor_tensor(qf[:, :], qf[:, :], qf2[:, :], ALU.add))
                part = qpack[:, X, :, :, :, :].rearrange("p t h s d -> p (t h) s d")
                f = qf[:, :].rearrange("p (n d) -> p n d", d=XD)
                r = qr[:, :].rearrange("p (n d) -> p n d", d=XD)
                link(pool.tensor_copy(part[:, :, 0, :], f))
                link(pool.tensor_tensor(r, f, part[:, :, 0, :], ALU.subtract))
                link(pool.tensor_copy(part[:, :, 3, :], r))
                link(pool.tensor_tensor(r, r, part[:, :, 3, :], ALU.subtract))
                pool.tensor_copy(part[:, :, 6, :], r).then_inc(s["q_parts"], 1)
                pool.wait_ge(s["q_parts"], 2 * b + X + 1)

            def low_qk(c, p):
                r, k = divmod(c, 2)
                col = B_BQ + 16 * k + 2 * p + r
                pool.tensor_copy(qk_bias[:, c:c + 1], cols_sb[:, bass.ds(col, 1)]).then_inc(s["wqk_bias"], 1)
                pool.wait_ge(s["wqk_half"], 4 * p + c + 1)
                pool.tensor_tensor(wqkL[:, c], stg[:, k, :, r * HD:(r + 1) * HD], wqkH[:, c].bitcast(F32),
                                   ALU.subtract).then_inc(s["wqk_ready"], 1)

            def low_v(p):
                pool.wait_ge(s["wv_half"], p + 1)
                pool.tensor_tensor(wvL[:, :, :], stg[:, W_V, :, :], wvH[:, :, :].bitcast(F32), ALU.subtract).then_inc(s["wv_ready"], 1)

            def low_o(p):
                pool.wait_ge(s["wo_half"], p + 1)
                pool.tensor_tensor(woL[:, :, :], stgo[:, :, :], woH[:, :, :].bitcast(F32), ALU.subtract).then_inc(s["wo_ready"], 1)

            prep(0, 0)
            prep(0, 1)
            pool.wait_ge(s["d_ctx"], 16)
            for b in range(B):
                if b == 0:
                    pool.wait_ge(s["va_ready"], 1)
                pool.tensor_copy(v_slots[:, 2 * XG * b:2 * XG * (b + 1), 0:XD], ctx_sb[:, 2 * b:2 * b + 2, :].rearrange("p t (g d) -> p (t g) d", d=XD)).then_inc(s["va_ready"], 1)
            prep(1, 0)
            prep(1, 1)
            prep(2, 0)
            prep(2, 1)
            prep(3, 0)
            prep(3, 1)
            pool.wait_ge(s["d_wqkv"], 16)
            pool.wait_ge(s["d_cols"], 16)
            for c in range(4):
                r, k = divmod(c, 2)
                pool.tensor_copy(wqkH[:, c], stg[:, k, :, r * HD:(r + 1) * HD]).then_inc(s["wqk_half"], 1)
                low_qk(c, 0)
            pool.tensor_copy(wvH[:, :, :], stg[:, W_V, :, :]).then_inc(s["wv_half"], 1)
            low_v(0)
            pool.wait_ge(s["d_wo"], 16)
            pool.tensor_copy(woH[:, :, :], stgo[:, :, :]).then_inc(s["wo_half"], 1)
            low_o(0)
            def hidden_low(b):
                pool.wait_ge(s["nh_ready"], b + 1)
                y = yacc[:, 2 * b:2 * b + 2, :]
                pool.tensor_tensor(y, y, rows_sb[:, R_BO:R_BO + D].unsqueeze(1).to_broadcast([P, 2, D]), ALU.add).then_inc(s["yacc_init"], 1)
                pool.wait_ge(s["hH_ready"], b + 1)
                cut = slice(256 * b, 256 * (b + 1))
                pool.tensor_tensor(hL[:, :, cut], hT[:, :, :], hH[:, :, cut].bitcast(F32), ALU.subtract).then_inc(s["h_ready"], 1)

            def rope_sin(sw_count, q, k):
                pool.wait_ge(s[f"d_sw{q}"], sw_count)
                col = C_RSINK if k else C_RSINQ
                v = qk_sw[:, q, :].rearrange("p (b t) -> p b t", b=2)
                pool.tensor_tensor(v, v, cst_sb[:, col:col + 256].unsqueeze(1).to_broadcast([P, 2, 256]), ALU.mult).then_inc(s["chunk_sw"], 1)

            for b in range(B - 1):
                hidden_low(b)
            for n in range(LEAD):
                rope_sin(32 * (n // 2 + 1), n % 2, n % 2)
                if n == 3:
                    hidden_low(B - 1)

            def step(i, j):
                more = not (isinstance(i, int) and i >= NP - 1)
                if more and j < 4:
                    low_qk(j, i + 1)
                if j == 3 and not (isinstance(i, int) and (i == 0 or i >= NP)):
                    low_o(i)
                if more and j == 4:
                    low_v(i + 1)
                if j == 7 and not (isinstance(i, int) and i >= NP):
                    pool.wait_ge(s["we_half"], i + 1)
                    cut = bass.ds(WE_CUT * i, WE_CUT)
                    pool.tensor_tensor(weL[:, cut], stge[:, :], weH[:, cut].bitcast(F32), ALU.subtract).then_inc(s["we_ready"], 1)
                if unit(i, j, -LEAD):
                    rope_sin(32 * (4 * i + (j + LEAD) // 2 + 1), j % 2, j % 2)

            steps(pool, step)

            def hidden_low2(b):
                pool.wait_ge(s["c_hH"], b + 1)
                cut = slice(256 * b, 256 * (b + 1))
                pool.tensor_tensor(hL[:, :, cut], h2T[:, :, cut], hH[:, :, cut].bitcast(F32), ALU.subtract).then_inc(s["c_h"], 1)

            def middle_low(n):
                pool.wait_ge(s["c_gH"], n + 1)
                pool.tensor_tensor(GL[:, (n // 2) % 2, n % 2, :], G[:, n % 2, :], GH[:, (n // 2) % 2, n % 2, :].bitcast(F32),
                                   ALU.subtract).then_inc(s["c_gL"], 1)

            hidden_low2(0)
            hidden_low2(1)
            for n in range(2 * NE):
                if n in (2, 4):
                    hidden_low2(1 + n // 2)
                middle_low(n)

        @block.scalar
        def _(act):
            act.wait_ge(s["d_ctx"], 16)
            for t in range(NT):
                ins = act.activation(kf2[:, t, :], ctx_sb[:, t, :], ACT.Square, accum_out=small[:, 8 + t:9 + t])
                ins.then_inc(s["ssk_done"], 1)
            act.wait_ge(s["d_rows"], 16)
            act.activation(small[:, 96:98], rows_sb[:, R_GX:R_GX + 2], ACT.Tanh).then_inc(s["tanh_done"], 1)

            def q_evac(b, X, t):
                n = m6["Q", b, X, t]
                act.wait_ge(s["m6_pe"], n + 1)
                act.activation(qT[:, X, t, :, :].rearrange("p h n -> p (h n)"), bank_bf[0][:, :], ACT.Copy).then_inc(s["m6_free"], 1)

            def o_evac(b):
                act.wait_ge(s["m6_pe"], m6["OT", b] + 1)
                act.activation(onT[:, :, :, :].rearrange("p k t n -> p (k t n)"), bank[6][:, :], ACT.Copy).then_inc(s["m6_free"], 1)

            def h_high(b):
                act.wait_ge(s["hT_ready"], b + 1)
                act.activation(hH[:, :, 256 * b:256 * (b + 1)], hT[:, :, :], ACT.Copy).then_inc(s["hH_ready"], 1)

            def oT_evac(m):
                act.wait_ge(s["pv_pe"], 3 * m + 3)
                if m >= 2:
                    act.wait_ge(s["o_pe"], m - 1)
                act.activation(oT[:, m % 2, :], bank[4][:, 0:256], ACT.Copy).then_inc(s["oT_ready"], 1)

            q_evac(0, 0, 0)
            q_evac(0, 0, 1)
            for p in range(NPX):
                b, k = divmod(p, XP)
                g, t, heads = piece(k)
                width = P * (t + 1)
                act.wait_ge(s["s_max"], p + 1)
                if p >= 2:
                    act.wait_ge(s["pt_pe"], p - 1)
                for n, h in enumerate(heads):
                    ins = act.activation(PR[:, p % 2, n * width:(n + 1) * width], S_B[p % 2][:, n * width:(n + 1) * width],
                                         ACT.Exp, bias=nxm[:, p % 2, n:n + 1])
                ins.then_inc(s["s_exp"], 1)
                if k in (1, 2):
                    q_evac(b, 1, k - 1)
                if k == 5 and b:
                    o_evac(b - 1)
                if k in (7, 9) and b + 1 < B:
                    q_evac(b + 1, 0, (k - 7) // 2)
                if k == 2 and b >= 2:
                    h_high(b - 2)
                if p >= 2 and copied_by_act(p - 2):
                    pt_copy(act, p - 2)
                if p >= 5 and p % 3 == 2:
                    oT_evac((p - 5) // 3)
            for p in range(NPX - 2, NPX):
                if copied_by_act(p):
                    pt_copy(act, p)
            oT_evac(NPX // 3 - 1)
            h_high(B - 2)
            o_evac(B - 1)

            def chunk_out(n, q, c, guard):
                act.wait_ge(s["chunk_pe"], n + 1)
                if guard:
                    act.wait_ge(s["rope_done"], n - 1)
                act.activation(qk_f[:, q, :], O_B[q][:, :], ACT.Identity, bias=qk_bias[:, c:c + 1]).then_inc(s["chunk_f"], 1)

            act.wait_ge(s["wqk_bias"], 4)
            for n in range(LEAD):
                if n == 4:
                    h_high(B - 1)
                chunk_out(n, n % 2, n % 4, n >= 2)

            def step(i, j):
                T = U * i + j
                q = j % 2
                more = not (isinstance(i, int) and i >= NP - 1)
                if unit(i, j, 0):
                    act.wait_ge(s["b_max"], T + 1)
                    if unit(i, j, 2):
                        act.wait_ge(s["b_pt"], T - 1)
                    for t in range(2):
                        a, e = ((0, P), (P, 3 * P))[t]
                        ins = act.activation(PR[:, q, a:e], sm[:, q, a:e], ACT.Exp, bias=nm[:, q, t:t + 1], scale=-1.0,
                                             accum_out=rs[:, q, t:t + 1])
                        ins.then_inc(s["b_exp"], 1)
                if unit(i, j, -LEAD):
                    if 2 <= j < 6:
                        act.wait_ge(s["wqk_bias"], 4 * (i + 1) + j - 2 + 1)
                    chunk_out(T + LEAD, q, chunk_at(j)[0], True)
                if unit(i, j, 1):
                    act.wait_ge(s["b_pt"], T)
                    if unit(i, j, 3):
                        act.wait_ge(s["b_pv"], T - 2)
                    act.activation(PTs[:, 1 - q, 0:384], bank[2][:, 0:384], ACT.Copy).then_inc(s["b_ptcopy"], 1)
                if unit(i, j, 2):
                    act.wait_ge(s["b_pv"], T - 1)
                    if unit(i, j, 6):
                        act.wait_ge(s["b_wo"], 4 * i + (j - 2) // 2 - 1)
                    act.activation(oH[:, ((j - 2) // 2) % 2, q, :], bank[3][:, 0:256], ACT.Copy).then_inc(s["b_oH"], 1)
                if more and j < 4:
                    if j == 0:
                        act.wait_ge(s["d_wqkv"], 16 * (i + 2))
                    r, k = divmod(j, 2)
                    act.activation(wqkH[:, j], stg[:, k, :, r * HD:(r + 1) * HD], ACT.Copy).then_inc(s["wqk_half"], 1)
                if j == 3 and not (isinstance(i, int) and (i == 0 or i >= NP)):
                    act.wait_ge(s["d_wo"], 16 * (i + 1))
                    act.wait_ge(s["b_wo"], 4 * i)
                    act.activation(woH[:, :, :], stgo[:, :, :], ACT.Copy).then_inc(s["wo_half"], 1)
                if more and j == 4:
                    act.wait_ge(s["v_pe"], 4 * i + 4)
                    act.activation(wvH[:, :, :], stg[:, W_V, :, :], ACT.Copy).then_inc(s["wv_half"], 1)
                if j == 0 and not (isinstance(i, int) and (i == 0 or i >= NP)):
                    act.wait_ge(s["we_ready"], i)
                    act.dma_start(stge[:, :], we[bass.ds(i, 1)].rearrange("a p n -> (a p) n")).then_inc(s["d_we"], 16)
                if j == 5 and not (isinstance(i, int) and (i == 0 or i >= NP - 1)):
                    act.wait_ge(s["wo_ready"], i + 1)
                    act.dma_start(stgo[:, :, :], wo[bass.ds(i + 1, 1)].rearrange("a p w n -> (a p) w n")).then_inc(s["d_wo"], 16)
                if j == 6 and not (isinstance(i, int) and i >= NP):
                    act.wait_ge(s["d_we"], 16 * (i + 1))
                    act.activation(weH[:, bass.ds(WE_CUT * i, WE_CUT)], stge[:, :], ACT.Copy).then_inc(s["we_half"], 1)
                if j == 6 and not (isinstance(i, int) and i >= NP - 2):
                    act.wait_ge(s["wqk_ready"], 4 * (i + 2))
                    act.wait_ge(s["wv_ready"], i + 2)
                    act.dma_start(stg[:, :, :, :], wqkv[bass.ds(i + 2, 1)].rearrange("a p w k n -> (a p) w k n")).then_inc(s["d_wqkv"], 16)

            steps(act, step, 2)

            def hidden_high2(b):
                act.wait_ge(s["c_hT"], b + 1)
                act.activation(hH[:, :, 256 * b:256 * (b + 1)], h2T[:, :, 256 * b:256 * (b + 1)], ACT.Copy).then_inc(s["c_hH"], 1)

            hidden_high2(0)
            hidden_high2(1)
            act.wait_ge(s["b_wo"], NU // 2)
            for n in range(2 * NE):
                if n in (2, 4):
                    hidden_high2(1 + n // 2)
                if n == 4:
                    act.wait_ge(s["c_gmax"], 1)
                    act.activation(gate[:, 64:96], gate[:, 32:64], ACT.Exp).then_inc(s["c_gexp"], 1)
                    act.wait_ge(s["c_gdiff"], 1)
                    act.activation(gate[:, 400:408], gate[:, 392:400], ACT.Exp).then_inc(s["c_gexp"], 1)
                c, m = divmod(n, NE)
                act.wait_ge(s["c_mid"], n + 1)
                if n >= 2:
                    act.wait_ge(s["c_gL"], n - 1)
                act.activation(G[:, n % 2, :], bank[n % 2][:, :], ACT.Gelu,
                               bias=cols_sb[:, B_BE1 + m:B_BE1 + m + 1]).then_inc(s["c_gelu"], 1)
                act.wait_ge(s["c_gelu"], n + 1)
                if n >= 4:
                    act.wait_ge(s["c_exp_pe"], 2 * (n // 2 - 1))
                act.activation(GH[:, (n // 2) % 2, n % 2, :], G[:, n % 2, :], ACT.Copy).then_inc(s["c_gH"], 1)

        @block.vector
        def _(dve):
            seq = [0]

            def link(ins):
                seq[0] += 1
                ins.then_inc(s["dve_seq"], 1)
                dve.wait_ge(s["dve_seq"], seq[0])

            def rsqrt_seed(v, y, t):
                link(dve.tensor_scalar(t.bitcast(I32), v.bitcast(I32), 1, None, ALU.logical_shift_right))
                link(dve.tensor_scalar(y.bitcast(I32), t.bitcast(I32), -1.0, RSQRT_SEED, ALU.mult, ALU.add))

            def rsqrt_step(v, y, t):
                link(dve.scalar_tensor_tensor(t, y, -0.5, y, ALU.mult, ALU.mult))
                link(dve.tensor_tensor(t, t, v, ALU.mult))
                link(dve.scalar_tensor_tensor(y, t, 1.5, y, ALU.add, ALU.mult))

            def rsqrt(v, y, t):
                rsqrt_seed(v, y, t)
                for _ in range(3):
                    rsqrt_step(v, y, t)


            link(dve.memset(room[:, :], 0.0))
            dve.memset(v_slots[:, :, XD:XD + 1], 1.0).then_inc(s["va_ready"], 1)
            dve.wait_ge(s["d_cst"], 16)
            dve.tensor_copy(ident_bf, ident)
            dve.tensor_scalar(mask_bf, cst_sb[:, C_MASK + P:C_MASK + 2 * P], -1.0, None, ALU.mult).then_inc(s["bf_ready"], 1)


            for t in range(NT):
                if t % 2 == 0:
                    dve.wait_ge(s[f"d_x{t // 2}"], 16)
                ins = dve.bn_stats(bnst[:, t, :], x_sb[:, t, :])
            link(ins)
            for t in range(NT):
                ins = dve.bn_aggr(mv[:, t, :], bnst[:, t, :])
            link(ins)
            SM = lambda a, n: small[:, a:a + n]
            dve.wait_ge(s["ssk_done"], NT)
            link(dve.tensor_copy(SM(0, 8), mv[:, :, 1]))
            dve.tensor_scalar(SM(16, 8), SM(0, 8), 1.0 + EPS, EPS * EPS, ALU.mult, ALU.add)
            link(dve.tensor_scalar(SM(24, 8), SM(8, 8), 1.0 / 64, EPS, ALU.mult, ALU.add))
            rsqrt(SM(16, 16), SM(32, 16), SM(48, 16))

            def norm_q(b):
                if b:
                    dve.wait_ge(s["q_parts"], 2 * b)
                for t in range(2):
                    n = 2 * b + t
                    ins = dve.tensor_scalar(qn[:, t, :], x_sb[:, n, :], mv[:, n, 0:1], small[:, 32 + n:33 + n], ALU.subtract, ALU.mult)
                ins.then_inc(s["qn_ready"], 1)

            norm_q(0)
            for t in range(NT):
                ins = dve.tensor_scalar(kr[:, t, :], ctx_sb[:, t, :], small[:, 40 + t:41 + t], XD ** -0.5, ALU.mult, ALU.mult)
            link(ins)
            dve.wait_ge(s["wtab_ready"], 6)
            kb = kr[:, :, :].rearrange("p (b t) n -> p b (t n)", t=2)
            k4 = kr[:, :, :].rearrange("p (b t) (g d) -> p b (t g) d", t=2, d=XD)
            f4 = kf2[:, :, :].rearrange("p (b t) (g d) -> p b (t g) d", t=2, d=XD)
            w4 = WKS[:, :, :].rearrange("p t (g d) -> p (t g) d", d=XD)
            dve.tensor_tensor(kf[:, :, :].rearrange("p (b t) n -> p b (t n)", t=2), kb,
                              WKC[:, :, :].rearrange("p t n -> p (t n)").unsqueeze(1).to_broadcast([P, B, P]), ALU.mult)
            dve.tensor_tensor(f4[:, :, :, 0:8], k4[:, :, :, 8:16], w4[:, :, 0:8].unsqueeze(1).to_broadcast([P, B, 8, 8]), ALU.mult)
            link(dve.tensor_tensor(f4[:, :, :, 8:16], k4[:, :, :, 0:8], w4[:, :, 8:16].unsqueeze(1).to_broadcast([P, B, 8, 8]), ALU.mult))
            link(dve.tensor_tensor(kf[:, :, :], kf[:, :, :], kf2[:, :, :], ALU.add))
            kv = kf[:, :, :].rearrange("p t (g d) -> p (t g) d", d=XD)
            krv = kr[:, :, :].rearrange("p t (g d) -> p (t g) d", d=XD)
            link(dve.tensor_copy(kpack[:, :, 0, :], kv))
            link(dve.tensor_tensor(krv, kv, kpack[:, :, 0, :], ALU.subtract))
            link(dve.tensor_copy(kpack[:, :, 1, :], krv))
            link(dve.tensor_tensor(krv, krv, kpack[:, :, 1, :], ALU.subtract))
            link(dve.tensor_copy(kpack[:, :, 2, :], krv))
            dve.tensor_copy(kpack[:, :, 3:6, :], kpack[:, :, 0:3, :])
            dve.tensor_copy(kpack[:, :, 6:8, :], kpack[:, :, 0:2, :]).then_inc(s["kpack_ready"], 1)

            def pack(b, X):
                dve.wait_ge(s["q_parts"], 2 * b + X + 1)
                v = qpack[:, X, :, :, :, :].rearrange("p t h s d -> p (t h) s d")
                dve.tensor_copy(v[:, :, 1, :], v[:, :, 0, :])
                dve.tensor_copy(v[:, :, 2, :], v[:, :, 0, :])
                dve.tensor_copy(v[:, :, 4, :], v[:, :, 3, :])
                dve.tensor_copy(v[:, :, 5, :], v[:, :, 3, :])
                dve.tensor_copy(v[:, :, 7, :], v[:, :, 6, :]).then_inc(s["qpack_ready"], 1)

            for b in range(B):
                if b in (1, 2):
                    pack(0, b - 1)
                dve.wait_ge(s["m7_pe"], m7["K", b] + 1)
                dve.tensor_copy(kT[:, b, :, :].rearrange("p g n -> p (g n)"), bank_bf[1][:, :]).then_inc(s["m7_free"], 1)

            def norm_out(m):
                b, g = divmod(m, XG)
                dve.wait_ge(s["o_pe"], m + 1)
                if g == 0 and b:
                    dve.wait_ge(s["m6_pe"], m6["OT", b - 1] + 1)
                o = bank[5][:, 0:256].rearrange("p (t h d) -> p t h d", t=2, h=4)
                r = rden[:, m % 2, :, :]
                dve.reciprocal(r.unsqueeze(3), o[:, :, :, XD:XD + 1]).then_inc(s["o_done"], 1)
                dve.wait_ge(s["o_done"], 2 * m + 1)
                ins = dve.tensor_tensor(on[:, :, 64 * g:64 * (g + 1)].rearrange("p t (h d) -> p t h d", d=XD), o[:, :, :, 0:XD],
                                        r.unsqueeze(3).to_broadcast([P, 2, 4, XD]), ALU.mult)
                ins.then_inc(s["o_done"], 1)

            def residual(b, phase):
                v, y, w = SM(112, 4), SM(116, 4), SM(120, 4)
                xb = x_sb[:, 2 * b:2 * b + 2, :]
                if phase == 0:
                    dve.wait_ge(s["m7_pe"], m7["PJ", b] + 1)
                    dve.wait_ge(s["tanh_done"], 1)
                    ins = dve.scalar_tensor_tensor(xb.rearrange("p t n -> p (t n)"), bank[7][:, :], small[:, 96:97],
                                                   xb.rearrange("p t n -> p (t n)"), ALU.mult, ALU.add)
                    ins.then_inc(s["m7_free"], 1)
                if phase == 1:
                    dve.wait_ge(s["m7_free"], m7["PJ", b] + 1)
                    for t in range(2):
                        ins = dve.bn_stats(bnst[:, t, :], x_sb[:, 2 * b + t, :])
                    link(ins)
                    for t in range(2):
                        ins = dve.bn_aggr(mv[:, 2 * b + t, :], bnst[:, t, :])
                    link(ins)
                if phase == 2:
                    dve.tensor_scalar(v[:, 0:2], mv[:, 2 * b:2 * b + 2, 1], EPS, None, ALU.add)
                    link(dve.tensor_scalar(v[:, 2:4], mv[:, 2 * b:2 * b + 2, 1], 1.0 + EPS, EPS * EPS, ALU.mult, ALU.add))
                    rsqrt_seed(v, y, w)
                if 3 <= phase <= 5:
                    rsqrt_step(v, y, w)
                if phase == 5:
                    for t in range(2):
                        n = 2 * b + t
                        ins = dve.tensor_scalar(yacc[:, n, :], x_sb[:, n, :], mv[:, n, 0:1], y[:, t:t + 1], ALU.subtract, ALU.mult)
                    if b:
                        dve.wait_ge(s["m7_pe"], m7["NT", b - 1] + 1)
                    for t in range(2):
                        n = 2 * b + t
                        ins = dve.tensor_scalar(nh[:, t, :], x_sb[:, n, :], mv[:, n, 0:1], y[:, 2 + t:3 + t], ALU.subtract, ALU.mult)
                    ins.then_inc(s["nh_ready"], 1)

            def affine(b, dst, bank_n, w, bias):
                for k in range(KT):
                    ins = dve.tensor_scalar(dst[:, k, :], bank[bank_n][:, 256 * k:256 * (k + 1)], cols_sb[:, w + k:w + k + 1],
                                            cols_sb[:, bias + k:bias + k + 1], ALU.mult, ALU.add)
                return ins

            def hidden_t(b):
                dve.wait_ge(s["m7_pe"], m7["NT", b] + 1)
                if b == 0:
                    dve.wait_ge(s["d_cols"], 16)
                else:
                    dve.wait_ge(s["h_ready"], b)
                ins = affine(b, hT, 7, B_L1W, B_L1B)
                ins.then_inc(s["m7_free"], 1)
                dve.wait_ge(s["m7_free"], m7["NT", b] + 1)
                dve.memset(small[:, 110:111], 0.0).then_inc(s["hT_ready"], 1)

            for p in range(NPX):
                b, k = divmod(p, XP)
                g, t, heads = piece(k)
                dve.wait_ge(s["s_pe"], p + 1)
                if p >= 2:
                    dve.wait_ge(s["s_exp"], p - 1)
                dve.tensor_reduce(nxm[:, p % 2, 0:len(heads)], S_B[p % 2][:, :].rearrange("p (h n) -> p h n", h=len(heads)),
                                  AX.X, ALU.max, negate=True).then_inc(s["s_max"], 1)
                if p >= 2 and not copied_by_act(p - 2):
                    pt_copy(dve, p - 2)
                if k == 0 and b + 1 < B:
                    norm_q(b + 1)
                if k == 1 and b >= 2:
                    hidden_t(b - 2)
                if p >= 6 and p % 3 == 0:
                    norm_out((p - 6) // 3)
                if k == 5 and b + 1 < B:
                    pack(b + 1, 0)
                if k >= 6 and b:
                    residual(b - 1, k - 6)
                if k == 10 and b + 1 < B:
                    pack(b + 1, 1)
            for p in range(NPX - 2, NPX):
                if not copied_by_act(p):
                    pt_copy(dve, p)
            norm_out(NPX // 3 - 2)
            hidden_t(B - 2)
            norm_out(NPX // 3 - 1)

            def rope_cos(n, q, c, cols_):
                dve.wait_ge(s["chunk_f"], n + 1)
                col = C_RCOSK if c % 2 else C_RCOSQ
                dve.tensor_tensor(QT[:, c, cols_].rearrange("p (b t) -> p b t", b=2), qk_f[:, q, :].rearrange("p (b t) -> p b t", b=2),
                                  cst_sb[:, col:col + 256].unsqueeze(1).to_broadcast([P, 2, 256]), ALU.mult).then_inc(s["chunk_cos"], 1)

            def rope_add(n, q, c, cols_):
                dve.wait_ge(s["chunk_sw"], n + 1)
                dve.wait_ge(s["chunk_cos"], n + 1)
                dve.tensor_tensor(QT[:, c, cols_], QT[:, c, cols_], qk_sw[:, q, :], ALU.add).then_inc(s["rope_done"], 1)

            def v_out(m, b, p):
                dve.wait_ge(s["v_pe"], m + 1)
                bias = bv_sb[:, bass.ds(256 * p, 256)].unsqueeze(1).to_broadcast([P, 2, 256])
                dve.tensor_tensor(V[:, 2 * b:2 * b + 2, :], bank[6][:, :].rearrange("p (t n) -> p t n", t=2), bias, ALU.add).then_inc(s["v_ready"], 1)

            groups = (slice(0, 512), slice(512, 1024))
            dve.wait_ge(s["d_bv"], 16)
            residual(B - 1, 0)
            residual(B - 1, 1)
            rope_cos(0, 0, 0, groups[0])
            residual(B - 1, 2)
            rope_cos(1, 1, 1, groups[0])
            rope_add(0, 0, 0, groups[0])
            for phase in (3, 4, 5):
                residual(B - 1, phase)
            rope_add(1, 1, 1, groups[0])
            v_out(0, 0, 0)
            rope_cos(2, 0, 2, groups[0])
            rope_add(2, 0, 2, groups[0])
            v_out(1, 1, 0)
            rope_cos(3, 1, 3, groups[0])
            hidden_t(B - 1)
            rope_add(3, 1, 3, groups[0])
            for n in range(4, LEAD):
                rope_cos(n, n % 2, n % 4, groups[1])
            dve.wait_ge(s["h_ready"], B)
            dve.wait_ge(s["yacc_init"], B)

            def second_norm(b, phase):
                v, y, w = SM(100, 2), SM(102, 2), SM(104, 2)
                if phase == 0:
                    dve.wait_ge(s["b_yadd"], NU // 2 - B + b + 1)
                    for t in range(2):
                        ins = dve.bn_stats(bnst[:, t, :], yacc[:, 2 * b + t, :])
                    link(ins)
                    for t in range(2):
                        ins = dve.bn_aggr(mv[:, 2 * b + t, :], bnst[:, t, :])
                    link(ins)
                if phase == 1:
                    link(dve.tensor_scalar(v, mv[:, 2 * b:2 * b + 2, 1], EPS, None, ALU.add))
                    rsqrt_seed(v, y, w)
                if 2 <= phase <= 4:
                    rsqrt_step(v, y, w)
                if phase == 5:
                    if b:
                        dve.wait_ge(s["c_tr"], b)
                    for t in range(2):
                        n = 2 * b + t
                        ins = dve.tensor_scalar(nh[:, t, :], yacc[:, n, :], mv[:, n, 0:1], y[:, t:t + 1], ALU.subtract, ALU.mult)
                    ins.then_inc(s["c_nh"], 1)

            def second_t(b):
                dve.wait_ge(s["c_tr"], b + 1)
                affine(b, h2T[:, :, 256 * b:256 * (b + 1)], 4, B_L2W, B_L2B).then_inc(s["c_hT"], 1)

            extra = {61: [(0, 0), (0, 1)], 62: [(0, 2), (0, 3)], 63: [(0, 4), (0, 5), (1, 0), (1, 1)],
                     64: [(0, -1), (1, 2), (1, 3), (1, 4), (1, 5)], 65: [(1, -1)] + [(2, n) for n in range(6)], 66: [(2, -1)]}

            def step(i, j):
                T = U * i + j
                q = j % 2
                if unit(i, j, 0):
                    dve.wait_ge(s["b_s"], T + 1)
                    if unit(i, j, 2):
                        dve.wait_ge(s["b_exp"], 2 * (T - 1))
                    dve.memset(small[:, 111:112], 0.0)
                    dve.tensor_tensor_reduce(sm[:, q, 0:P], S_B[q][:, 0:P], cst_sb[:, C_MASK + P:C_MASK + 256], 1.0, 3e38,
                                             ALU.add, ALU.min, nm[:, q, 0:1])
                    dve.tensor_tensor_reduce(sm[:, q, P:3 * P], S_B[q][:, P:3 * P], cst_sb[:, C_MASK:C_MASK + 256], 1.0, 3e38,
                                             ALU.add, ALU.min, nm[:, q, 1:2]).then_inc(s["b_max"], 1)
                if unit(i, j, -4):
                    rope_add(T + 4, q, j % 4, groups[(j + 4) // 4 % 2])
                m = (j + 2) // 2
                if j % 2 == 0 and (not isinstance(i, int) or (T > 0 and B * i + m < B * NP)):
                    v_out(B * i + m, m % B, i + m // B)
                if j % 2 == 1 and unit(i, j, 5):
                    m = (j - 5) // 2
                    dve.wait_ge(s["b_wo"], B * i + m + 1)
                    b = m % B
                    y = yacc[:, 2 * b:2 * b + 2, :].rearrange("p t n -> p (t n)")
                    dve.tensor_tensor(y, y, bank[7][:, :], ALU.add).then_inc(s["b_yadd"], 1)
                if unit(i, j, 0):
                    dve.wait_ge(s["b_exp"], 2 * (T + 1))
                    dve.reciprocal(rs[:, q, :], rs[:, q, :]).then_inc(s["b_recip"], 1)
                    dve.wait_ge(s["b_recip"], T + 1)
                    dve.tensor_scalar(PR[:, q, 0:P], PR[:, q, 0:P], rs[:, q, 0:1], None, ALU.mult)
                    dve.tensor_scalar(PR[:, q, P:3 * P], PR[:, q, P:3 * P], rs[:, q, 1:2], None, ALU.mult).then_inc(s["b_norm"], 1)
                if unit(i, j, -LEAD):
                    c, g = chunk_at(j)
                    rope_cos(T + LEAD, q, c, groups[g])
                if unit(i, j, 2):
                    dve.wait_ge(s["b_oH"], T - 1)
                    h = oH[:, ((j - 2) // 2) % 2, q, :]
                    dve.tensor_tensor(oL[:, ((j - 2) // 2) % 2, q, :], bank[3][:, 0:256], h.bitcast(F32), ALU.subtract).then_inc(s["b_oL"], 1)
                for b, phase in extra.get(T, []) if isinstance(i, int) else []:
                    second_t(b) if phase < 0 else second_norm(b, phase)

            steps(dve, step)

            for phase in range(6):
                second_norm(B - 1, phase)
            second_t(B - 1)

            Gt = lambda a, n: gate[:, a:a + n]
            V3 = lambda a: gate[:, a:a + 32].rearrange("p (t e) -> p t e", e=E)
            dve.wait_ge(s["c_logit"], 1)
            link(dve.tensor_copy(Gt(0, 32), bank[5][:, 0:32]))
            link(dve.tensor_reduce(Gt(96, 8), V3(0), AX.X, ALU.max))
            dve.tensor_tensor(V3(32), V3(0), Gt(96, 8).unsqueeze(2).to_broadcast([P, NT, E]), ALU.subtract).then_inc(s["c_gmax"], 1)
            dve.wait_ge(s["c_gexp"], 1)
            link(dve.tensor_reduce(Gt(104, 8), V3(64), AX.X, ALU.add))
            link(dve.reciprocal(Gt(112, 8), Gt(104, 8)))
            link(dve.tensor_tensor(V3(64), V3(64), Gt(112, 8).unsqueeze(2).to_broadcast([P, NT, E]), ALU.mult))
            Q4 = lambda a: gate[:, a:a + 128].rearrange("p (t e f) -> p t e f", e=E, f=E)
            for e in range(E):
                pe_ = V3(64)[:, :, e:e + 1].to_broadcast([P, NT, E])
                dve.tensor_tensor(Q4(120)[:, :, e, :], V3(64), pe_, ALU.is_gt)
                link(dve.tensor_tensor(Q4(248)[:, :, e, :], V3(64), pe_, ALU.is_equal))
            tie = cst_sb[:, C_TIE:C_TIE + 16].unsqueeze(1).to_broadcast([P, NT, 16])
            q16 = gate[:, 248:376].rearrange("p (t f) -> p t f", t=NT)
            link(dve.tensor_tensor(q16, q16, tie, ALU.mult))
            link(dve.tensor_tensor(Gt(120, 128), Gt(120, 128), Gt(248, 128), ALU.add))
            rank = gate[:, 408:440]
            link(dve.tensor_reduce(rank, gate[:, 120:248].rearrange("p (n f) -> p n f", f=E), AX.X, ALU.add))
            first, second = gate[:, 120:152], gate[:, 152:184]
            dve.tensor_scalar(first, rank, 0.0, None, ALU.is_equal)
            link(dve.tensor_scalar(second, rank, 1.0, None, ALU.is_equal))
            dve.tensor_tensor(Gt(184, 32), first, Gt(64, 32), ALU.mult)
            link(dve.tensor_tensor(Gt(216, 32), second, Gt(64, 32), ALU.mult))
            dve.tensor_reduce(Gt(376, 8), V3(184), AX.X, ALU.add)
            link(dve.tensor_reduce(Gt(384, 8), V3(216), AX.X, ALU.add))
            dve.tensor_tensor(Gt(392, 8), Gt(384, 8), Gt(376, 8), ALU.subtract).then_inc(s["c_gdiff"], 1)
            dve.wait_ge(s["c_gexp"], 2)
            link(dve.tensor_scalar(Gt(248, 8), Gt(400, 8), 1.0, None, ALU.add))
            link(dve.reciprocal(Gt(256, 8), Gt(248, 8)))
            link(dve.tensor_tensor(Gt(264, 8), Gt(256, 8), Gt(400, 8), ALU.mult))
            dve.tensor_tensor(V3(120), V3(120), Gt(256, 8).unsqueeze(2).to_broadcast([P, NT, E]), ALU.mult)
            link(dve.tensor_tensor(V3(152), V3(152), Gt(264, 8).unsqueeze(2).to_broadcast([P, NT, E]), ALU.mult))
            dve.tensor_tensor(Gt(0, 32), Gt(120, 32), Gt(152, 32), ALU.add).then_inc(s["c_comb"], 1)
            dve.wait_ge(s["c_combT_pe"], 1)
            dve.tensor_copy(combT[:, 0:4, :].rearrange("p t n -> p (t n)"), bank[4][0:E, :])
            dve.tensor_copy(combT[:, 4:8, :].rearrange("p t n -> p (t n)"), bank[5][0:E, :]).then_inc(s["c_combT"], 1)
            for b in range(B):
                dve.wait_ge(s["c_be"], b + 1)
                y = yacc[:, 2 * b:2 * b + 2, :].rearrange("p t n -> p (t n)")
                dve.tensor_tensor(y, y, bank[4 + b % 2][:, :], ALU.add).then_inc(s["c_init"], 1)
            dve.wait_ge(s["c_init"], B)

            for m in range(2 * E):
                c, e = divmod(m, E)
                for hf in range(2):
                    b = 2 * c + hf
                    dve.wait_ge(s["c_exp_pe"], 2 * m + hf + 1)
                    if m:
                        dve.wait_ge(s["c_acc"], 2 * (m - 1) + hf + 1)
                    for t in range(2):
                        n = 2 * b + t
                        ins = dve.scalar_tensor_tensor(yacc[:, n, :], out_bank(m, hf)[:, 256 * t:256 * (t + 1)],
                                                       gate[:, 4 * n + e:4 * n + e + 1], yacc[:, n, :], ALU.mult, ALU.add)
                    ins.then_inc(s["c_acc"], 1)
                    if e == E - 1:
                        dve.wait_ge(s["c_acc"], 2 * m + hf + 1)
                        y = yacc[:, 2 * b:2 * b + 2, :].rearrange("p t n -> p (t n)")
                        xb = x_sb[:, 2 * b:2 * b + 2, :].rearrange("p t n -> p (t n)")
                        dve.scalar_tensor_tensor(y, y, small[:, 97:98], xb, ALU.mult, ALU.add).then_inc(s["c_fin"], 1)

        @block.tensor
        def _(pe):
            pe.wait_ge(s["bf_ready"], 1)
            pe.wait_ge(s["d_cst"], 16)
            pe.wait_ge(s["kpack_ready"], 1)

            def k_turn(b):
                if b:
                    pe.wait_ge(s["m7_free"], b)
                for g in range(XG):
                    for t in range(2):
                        ins = pe.transpose(bank_bf[1][:, (2 * g + t) * P:(2 * g + t + 1) * P],
                                           kpack[:, (2 * b + t) * XG + g, :, :].rearrange("p s d -> p (s d)"), ident_bf)
                ins.then_inc(s["m7_pe"], 1)

            def q_turn(b, X, t):
                n = m6["Q", b, X, t]
                pe.wait_ge(s["qpack_ready"], 2 * b + X + 1)
                if n:
                    pe.wait_ge(s["m6_free"], n)
                for h in range(8):
                    ins = pe.transpose(bank_bf[0][:, h * P:(h + 1) * P], qpack[:, X, t, h, :, :].rearrange("p s d -> p (s d)"), ident_bf)
                ins.then_inc(s["m6_pe"], 1)

            def out_turn(b):
                n = m6["OT", b]
                pe.wait_ge(s["o_done"], 2 * XG * (b + 1))
                pe.wait_ge(s["m6_free"], n)
                for k in range(KT):
                    for t in range(2):
                        ins = pe.transpose(bank[6][:, (2 * k + t) * P:(2 * k + t + 1) * P], on[:, t, k * P:(k + 1) * P], ident)
                ins.then_inc(s["m6_pe"], 1)

            def out_project(b):
                n = m7["PJ", b]
                pe.wait_ge(s["m6_free"], m6["OT", b] + 1)
                pe.wait_ge(s["m7_free"], n)
                if b == 0:
                    pe.wait_ge(s["d_wout"], 16)
                for t in range(2):
                    for k in range(KT):
                        ins = pe.matmul(bank[7][:, 256 * t:256 * (t + 1)], onT[:, k, t, :], w_out_sb[:, k, :], start=(k == 0), stop=(k == 1))
                ins.then_inc(s["m7_pe"], 1)

            def norm_turn(b):
                n = m7["NT", b]
                pe.wait_ge(s["nh_ready"], b + 1)
                pe.wait_ge(s["m7_free"], n)
                for k in range(KT):
                    for t in range(2):
                        ins = pe.transpose(bank[7][:, (2 * k + t) * P:(2 * k + t + 1) * P], nh[:, t, k * P:(k + 1) * P], ident)
                ins.then_inc(s["m7_pe"], 1)

            def x_scores(p):
                b, k = divmod(p, XP)
                g, t, heads = piece(k)
                width = P * (t + 1)
                pe.wait_ge(s["m6_free"], m6["Q", b, k // 6, 1] + 1)
                if k == 0:
                    pe.wait_ge(s["m7_free"], b + 1)
                if p >= 2:
                    pe.wait_ge(s["s_exp"], p - 1)
                for n, h in enumerate(heads):
                    pe.matmul(S_B[p % 2][:, n * width:(n + 1) * width], qT[:, h // 8, t, h % 8, :], kT[:, b, g, 0:width], start=True, stop=False)
                    ins = pe.matmul(S_B[p % 2][:, (n + 1) * width - P:(n + 1) * width], ident_bf, mask_bf, start=False, stop=True)
                ins.then_inc(s["s_pe"], 1)

            def x_turn(p):
                pe.wait_ge(s["s_exp"], p + 1)
                if p >= 2:
                    pe.wait_ge(s[copier(p - 2)[0]], copier(p - 2)[1])
                for n in range(4):
                    ins = pe.transpose(PT_B[p % 2][:, n * P:(n + 1) * P], PR[:, p % 2, n * P:(n + 1) * P], ident)
                ins.then_inc(s["pt_pe"], 1)

            def x_values(p):
                b, k = divmod(p, XP)
                g, t, heads = piece(k)
                m = p // 3
                pe.wait_ge(s[copier(p)[0]], copier(p)[1])
                if p == 0:
                    pe.wait_ge(s["va_ready"], 1 + B)
                if t == 0 and m:
                    pe.wait_ge(s["oT_ready"], m)
                c = P * t
                for n, h in enumerate(heads):
                    for kt in range(t + 1):
                        a = VZ + VP * (XG * (2 * b + kt) + g) - 32 * (h % 4)
                        ins = pe.matmul(bank[4][:, c:c + P], room[:, a:a + P], PTs[:, p % 2, (n * (t + 1) + kt) * P:(n * (t + 1) + kt + 1) * P],
                                        start=(h % 4 == 0 and kt == 0), stop=(h % 4 == 3 and kt == t))
                ins.then_inc(s["pv_pe"], 1)

            def o_turn(m):
                pe.wait_ge(s["oT_ready"], m + 1)
                if m:
                    pe.wait_ge(s["o_done"], 2 * m)
                for t in range(2):
                    ins = pe.transpose(bank[5][:, t * P:(t + 1) * P], oT[:, m % 2, t * P:(t + 1) * P], ident)
                ins.then_inc(s["o_pe"], 1)

            k_turn(0)
            q_turn(0, 0, 0)
            k_turn(1)
            q_turn(0, 0, 1)
            k_turn(2)
            k_turn(3)
            for p in range(NPX + 3):
                b, k = divmod(p, XP)
                if k == 0 and b >= 2:
                    norm_turn(b - 2)
                if p < NPX:
                    x_scores(p)
                    if k in (1, 2):
                        q_turn(b, 1, k - 1)
                    if k == 5 and b:
                        out_turn(b - 1)
                    if k == 6 and b:
                        out_project(b - 1)
                    if k in (7, 9) and b + 1 < B:
                        q_turn(b + 1, 0, (k - 7) // 2)
                if p >= 6 and p % 3 == 0:
                    o_turn((p - 6) // 3)
                if 2 <= p < NPX + 2:
                    x_turn(p - 2)
                if p >= 3:
                    x_values(p - 3)

            def three(outp, pairs):
                n = 3 * len(pairs)
                m = 0
                for (aH, aL), (bH, bL) in pairs:
                    for l, r in ((aH, bL), (aL, bH), (aH, bH)):
                        ins = pe.matmul(outp, l, r, start=(m == 0), stop=(m == n - 1))
                        m += 1
                return ins

            def project_qk(n, q, c, g, guard):
                if guard:
                    pe.wait_ge(s["chunk_f"], n - 1)
                cut = slice(512 * g, 512 * (g + 1))
                three(O_B[q][:, :], [((wqkH[:, c, k, :], wqkL[:, c, k, :]), (hH[:, k, cut], hL[:, k, cut])) for k in range(KT)]).then_inc(s["chunk_pe"], 1)

            def project_v(m, b, guard):
                if guard:
                    pe.wait_ge(s["v_ready"], m)
                for t in range(2):
                    cut = slice((2 * b + t) * P, (2 * b + t + 1) * P)
                    ins = three(bank[6][:, 256 * t:256 * (t + 1)], [((hH[:, k, cut], hL[:, k, cut]), (wvH[:, k, :], wvL[:, k, :])) for k in range(KT)])
                ins.then_inc(s["v_pe"], 1)

            pe.wait_ge(s["h_ready"], 2)
            pe.wait_ge(s["wqk_ready"], 4)
            pe.wait_ge(s["oT_ready"], NPX // 3)
            project_qk(0, 0, 0, 0, False)
            o_turn(NPX // 3 - 1)
            out_turn(B - 1)
            project_qk(1, 1, 1, 0, False)
            out_project(B - 1)
            pe.wait_ge(s["wv_ready"], 1)
            pe.wait_ge(s["m6_free"], len(M6))
            project_v(0, 0, False)
            project_qk(2, 0, 2, 0, True)
            project_v(1, 1, True)
            project_qk(3, 1, 3, 0, True)
            norm_turn(B - 1)
            pe.wait_ge(s["m7_free"], len(M7))
            pe.wait_ge(s["h_ready"], B)
            for n in range(4, LEAD):
                project_qk(n, n % 2, n % 4, 1, True)

            def step(i, j):
                T = U * i + j
                q = j % 2
                if unit(i, j, 0):
                    b, r = j // 2, j % 2
                    pe.wait_ge(s["rope_done"], U * i + 4 * (j // 4) + 2 * r + 2)
                    if unit(i, j, 2):
                        pe.wait_ge(s["b_max"], T - 1)
                    kt_ = QT[:, 2 * r + 1, 256 * b:256 * (b + 1)]
                    pe.matmul(S_B[q][:, 0:P], QT[:, 2 * r, 256 * b:256 * b + P], kt_[:, 0:P], start=True, stop=True)
                    pe.matmul(S_B[q][:, P:3 * P], QT[:, 2 * r, 256 * b + P:256 * (b + 1)], kt_, start=True, stop=True).then_inc(s["b_s"], 1)
                if unit(i, j, -LEAD):
                    if 2 <= j < 6:
                        pe.wait_ge(s["wqk_ready"], 4 * (i + 1) + j - 2 + 1)
                    c, g = chunk_at(j)
                    project_qk(T + LEAD, q, c, g, True)
                if unit(i, j, 1):
                    pe.wait_ge(s["b_norm"], T)
                    if unit(i, j, 2):
                        pe.wait_ge(s["b_ptcopy"], T - 1)
                    for n in range(3):
                        ins = pe.transpose(bank[2][:, n * P:(n + 1) * P], PR[:, 1 - q, n * P:(n + 1) * P], ident)
                    ins.then_inc(s["b_pt"], 1)
                if unit(i, j, 2):
                    u = (j - 2) % U
                    b, r = u // 2, u % 2
                    pe.wait_ge(s["b_ptcopy"], T - 1)
                    pe.wait_ge(s["v_ready"], 4 * i + (j - 2) // 2 + 1)
                    if unit(i, j, 3):
                        pe.wait_ge(s["b_oL"], T - 2)
                    pe.matmul(bank[3][:, 0:256], V[:, 2 * b, r * HD:(r + 1) * HD], PTs[:, q, 0:256], start=True, stop=False)
                    pe.matmul(bank[3][:, P:256], V[:, 2 * b + 1, r * HD:(r + 1) * HD], PTs[:, q, 256:384], start=False, stop=True).then_inc(s["b_pv"], 1)
                if v_event(i, j):
                    m = (j + 3) // 2
                    pe.wait_ge(s["wv_ready"], i + m // B + 1)
                    project_v(B * i + m, m % B, True)
                if j % 2 == 0 and unit(i, j, 4):
                    mo = (j - 4) // 2
                    pe.wait_ge(s["b_oL"], 8 * i + 2 * mo + 2)
                    pe.wait_ge(s["wo_ready"], i + mo // 4 + 1)
                    if not (isinstance(i, int) and i == 0 and mo == 0):
                        pe.wait_ge(s["b_yadd"], 4 * i + mo)
                    for t in range(2):
                        ins = three(bank[7][:, 256 * t:256 * (t + 1)],
                                    [((oH[:, mo % 2, r, t * P:(t + 1) * P], oL[:, mo % 2, r, t * P:(t + 1) * P]), (woH[:, r, :], woL[:, r, :])) for r in range(2)])
                    ins.then_inc(s["b_wo"], 1)

            def second_turn(b):
                pe.wait_ge(s["c_nh"], b + 1)
                if b:
                    pe.wait_ge(s["c_hT"], b)
                for k in range(KT):
                    for t in range(2):
                        ins = pe.transpose(bank[4][:, (2 * k + t) * P:(2 * k + t + 1) * P], nh[:, t, k * P:(k + 1) * P], ident)
                ins.then_inc(s["c_tr"], 1)

            def step_and_turns(i, j):
                step(i, j)
                if isinstance(i, int) and i == NP and j in (0, 2):
                    second_turn(j // 2)

            steps(pe, step_and_turns)

            def middle(n):
                c, m = divmod(n, NE)
                if n >= 2:
                    pe.wait_ge(s["c_gelu"], n - 1)
                if m == 0:
                    pe.wait_ge(s["c_h"], 2 * c + 2)
                cut = slice(512 * c, 512 * (c + 1))
                three(bank[n % 2][:, :], [((we1H[:, k, m * P:(m + 1) * P], we1L[:, k, m * P:(m + 1) * P]), (hH[:, k, cut], hL[:, k, cut])) for k in range(KT)]).then_inc(s["c_mid"], 1)

            def expert_out(m):
                c, e = divmod(m, E)
                pe.wait_ge(s["c_gL"], 2 * m + 2)
                if m < 2:
                    pe.wait_ge(s["b_yadd"], NU // 2)
                for hf in range(2):
                    if m >= 2:
                        pe.wait_ge(s["c_acc"], 2 * (m - 2) + hf + 1)
                    for t in range(2):
                        cut = slice((2 * hf + t) * P, (2 * hf + t + 1) * P)
                        ins = three(out_bank(m, hf)[:, 256 * t:256 * (t + 1)],
                                    [((GH[:, m % 2, k, cut], GL[:, m % 2, k, cut]), (we2H[:, 2 * e + k, :], we2L[:, 2 * e + k, :])) for k in range(IT)])
                    ins.then_inc(s["c_exp_pe"], 1)

            pe.wait_ge(s["we_ready"], NP)
            middle(0)
            middle(1)
            second_turn(2)
            middle(2)
            second_turn(3)
            middle(3)
            expert_out(0)
            pe.wait_ge(s["c_hT"], B)
            pe.wait_ge(s["d_small"], 32)
            for n in range(NT):
                for k in range(KT):
                    ins = pe.matmul(bank[5][:, E * n:E * (n + 1)], h2T[:, k, n * P:(n + 1) * P], w_gate_sb[:, k, :], start=(k == 0), stop=(k == 1))
            ins.then_inc(s["c_logit"], 1)
            expert_out(1)
            middle(4)
            middle(5)
            pe.wait_ge(s["c_comb"], 1)
            for n in range(NT):
                ins = pe.transpose(bank[4 + n // 4][0:E, (n % 4) * P:(n % 4 + 1) * P], gate[:, E * n:E * (n + 1)], ident)
            ins.then_inc(s["c_combT_pe"], 1)
            pe.wait_ge(s["c_combT"], 1)
            for b in range(B):
                if b >= 2:
                    pe.wait_ge(s["c_init"], b - 1)
                for t in range(2):
                    ins = pe.matmul(bank[4 + b % 2][:, 256 * t:256 * (t + 1)], combT[:, 2 * b + t, :], be2_sb[:, :], start=True, stop=True)
                ins.then_inc(s["c_be"], 1)
            for n in range(6, 2 * NE):
                middle(n)
                if n % 2:
                    expert_out((n - 3) // 2)
            expert_out(2 * E - 1)


def constants():
    f = np.float32
    c = np.zeros((P, C_END), f)
    c[:, C_ID:C_ID + P] = np.eye(P, dtype=f)
    above = np.triu(np.ones((P, P), f), 1)
    c[:, C_MASK + P:C_MASK + 256] = above * f(BIG)

    def angles(width):
        inv = f(1.0) / f(10000.0) ** (np.arange(0, width, 2, dtype=f) / f(width))
        a = np.arange(S, dtype=f)[:, None] * inv[None, :].astype(f)
        return np.cos(a).astype(f), np.sin(a).astype(f)

    co, si = angles(XD)
    for t in range(2):
        c[:, C_XCOS + t * XD:C_XCOS + (t + 1) * XD] = np.concatenate([co, co], 1)[t * P:(t + 1) * P]
        c[:, C_XSIN + t * XD:C_XSIN + (t + 1) * XD] = np.concatenate([-si, si], 1)[t * P:(t + 1) * P]
    co, si = angles(HD)
    scale = f(-1.0 / np.sqrt(HD))
    cos_t, sin_t = np.concatenate([co, co], 1).T, np.concatenate([-si, si], 1).T
    c[:, C_RCOSQ:C_RCOSQ + 256] = cos_t * scale
    c[:, C_RSINQ:C_RSINQ + 256] = sin_t * scale
    c[:, C_RCOSK:C_RCOSK + 256] = cos_t
    c[:, C_RSINK:C_RSINK + 256] = sin_t
    c[:, C_TIE:C_TIE + 16] = np.tril(np.ones((E, E), f), -1).reshape(1, 16)
    return c


def kernel(**inputs):
    import concourse.bacc as bacc
    from concourse.bass_utils import run_bass_kernel_spmd

    a = {k: np.ascontiguousarray(v) for k, v in inputs.items()}
    w = {k[7:]: v for k, v in a.items() if k.startswith("L0_ffn_")}

    def kxn(m, n):
        return m.reshape(n, P, *m.shape[1:]).swapaxes(0, 1)

    def col(v):
        return v.reshape(-1, P).T

    def pairs(m):
        return m.reshape(KT, P, NP, 256).transpose(2, 1, 0, 3)

    c = constants()
    arrays = {
        "x": a["x"],
        "ctx": a["ctx_512"],
        "cst": c,
        "cols": np.concatenate([col(w["bq"]), col(w["bk"]), col(w["ln1_w"]), col(w["ln1_b"]), col(w["ln2_w"]),
                                col(w["ln2_b"]), col(w["be1"])], 1),
        "rows": np.concatenate([a["L0_xattn_q_norm_w"], a["L0_xattn_k_norm_w"], w["bo"], a["g_xattn"], a["g_ffn"]])[None],
        "bv": w["bv"][None],
        "wqkv": np.stack([pairs(w["wq"]), pairs(w["wk"]), pairs(w["wv"])], 2),
        "wo": w["wo"].reshape(NP, 2, P, D).swapaxes(1, 2),
        "w_out_t": kxn(a["L0_xattn_w_out"].T, KT),
        "w_gate": kxn(w["w_gate"], KT),
        "be2": w["be2"],
        "we": np.concatenate([kxn(w["we1"].transpose(1, 0, 2).reshape(D, E * I), KT).reshape(P, -1),
                              kxn(w["we2"].reshape(E * I, D), NE).reshape(P, -1)], 1).reshape(P, NP, WE_CUT).swapaxes(0, 1),
    }
    nc = bacc.Bacc("TRN2", target_bir_lowering=False, num_devices=1)
    args, arrays = [], {f"in_{k}": np.ascontiguousarray(v) for k, v in arrays.items()}
    for name, v in arrays.items():
        args.append(nc.dram_tensor(name, v.shape, mybir.dt.from_np(v.dtype), kind="ExternalInput").ap())
    args.append(nc.dram_tensor("out_y", (B, S, D), F32, kind="ExternalOutput").ap())
    build_kernel(nc, *args)
    r = run_bass_kernel_spmd(nc, [arrays], core_ids=[0])
    return r.results[0]["out_y"]
```

```python
from contextlib import ExitStack

import numpy as np

import concourse.bass as bass
from concourse import mybir

F32 = mybir.dt.float32
F32R = mybir.dt.float32r
BF16 = mybir.dt.bfloat16
I32 = mybir.dt.int32
ALU = mybir.AluOpType
ACT = mybir.ActivationFunctionType
AX = mybir.AxisListType

P = 128
B, S, D = 4, 256, 256
NT = B * S // P
KT = D // P
XH, XG, XD = 16, 4, 16
XS = 8
XP = 12
VP, VZ = 128, 96
H, HD = 16, 128
NP = H // 2
U = 2 * B
NU = NP * U
LEAD = 6
E, I, IT = 4, 256, 2
NE = E * IT
WE_CUT = (KT * E * I + NE * D) // NP
BIG = 1e30
EPS = 1e-5
RSQRT_SEED = 1597463007.0

C_ID, C_MASK, C_XCOS, C_XSIN, C_RCOSQ, C_RSINQ, C_RCOSK, C_RSINK, C_TIE = 0, 128, 384, 416, 448, 704, 960, 1216, 1472
C_END = 1488
B_BQ, B_BK, B_L1W, B_L1B, B_L2W, B_L2B, B_BE1, B_END = 0, 16, 32, 34, 36, 38, 40, 48
R_QW, R_KW, R_BO, R_GX, R_GF, R_END = 0, 256, 320, 576, 577, 578
W_Q, W_K, W_V = 0, 1, 2


def build_kernel(nc, x, ctx_in, cst, cols, rows, bv, wqkv, wo, w_out_t, w_gate, be2, we, out):
    with ExitStack() as stack:
        def sb(name, shape, dt=F32):
            return stack.enter_context(nc.sbuf_tensor(name, shape, dt))

        def ps(name, shape=(P, 512), dt=F32):
            return stack.enter_context(nc.psum_tensor(name, list(shape), dt))

        def sem(name):
            return stack.enter_context(nc.semaphore(name))

        x_sb = sb("x_sb", [P, NT, D])
        ctx_sb = sb("ctx_sb", [P, NT, 64])
        cst_sb = sb("cst_sb", [P, C_END])
        bf_sb = sb("bf_sb", [P, 256], BF16)
        cols_sb = sb("cols_sb", [P, B_END])
        rows_sb = sb("rows_sb", [P, R_END])
        bv_sb = sb("bv_sb", [P, H * HD])
        w_out_sb = sb("w_out_sb", [P, KT, D])
        w_gate_sb = sb("w_gate_sb", [P, KT, E])
        be2_sb = sb("be2_sb", [E, D])
        yacc = sb("yacc", [P, NT, D])
        hH = sb("hH", [P, KT, NT * P], F32R)
        hL = sb("hL", [P, KT, NT * P], F32R)
        mv = sb("mv", [P, NT, 2])
        bnst = sb("bnst", [P, NT, 6])
        small = sb("small", [P, 160])
        stg = sb("stg", [P, 3, KT, 256])
        stgo = sb("stgo", [P, 2, D])
        qk_parts = sb("qk_parts", [P, 2, 4 * KT * HD], F32R)
        wqkH = qk_parts[:, 0, :].rearrange("p (c k n) -> p c k n", c=4, k=KT)
        wqkL = qk_parts[:, 1, :].rearrange("p (c k n) -> p c k n", c=4, k=KT)
        wvH = sb("wvH", [P, KT, 256], F32R)
        wvL = sb("wvL", [P, KT, 256], F32R)
        woH = sb("woH", [P, 2, D], F32R)
        woL = sb("woL", [P, 2, D], F32R)
        qk_bias = sb("qk_bias", [P, 4])
        qk_room = sb("qk_room", [P, 4, 512])
        qk_f = qk_room[:, 0:2, :]
        qk_sw = qk_room[:, 2:4, :]
        room = sb("room", [P, VZ + 4 * NT * P])
        QT = room[:, 0:4 * NT * P].rearrange("p (c n) -> p c n", c=4)
        split_room = sb("split_room", [P, 2, 3 * NT * P], F32R)
        k_split = split_room[:, :, 0:2 * NT * P].rearrange("p m (r n) -> p m r n", r=2)
        q_split = split_room[:, :, 2 * NT * P:3 * NT * P].rearrange("p m (r b n) -> p m r b n", r=2, b=B)
        V = sb("V", [P, NT, 256])
        sm = sb("sm", [P, 2, 384])
        nm = sb("nm", [P, 2, 2])
        rs = sb("rs", [P, 2, 2])
        PR = sb("PR", [P, 2, 512])
        PTs = sb("PTs", [P, 2, 512])
        o_parts = sb("o_parts", [P, 2, 1024], F32R)
        oH = o_parts[:, 0, :].rearrange("p (m r n) -> p m r n", m=2, r=2)
        oL = o_parts[:, 1, :].rearrange("p (m r n) -> p m r n", m=2, r=2)
        weH = sb("weH", [P, 4096], F32R)
        weL = sb("weL", [P, 4096], F32R)
        stge = sb("stge", [P, WE_CUT])
        we1H = weH[:, 0:2048].rearrange("p (k n) -> p k n", k=KT)
        we1L = weL[:, 0:2048].rearrange("p (k n) -> p k n", k=KT)
        we2H = weH[:, 2048:4096].rearrange("p (e n) -> p e n", e=NE)
        we2L = weL[:, 2048:4096].rearrange("p (e n) -> p e n", e=NE)
        G = sb("G", [P, 2, 512])
        GH = o_parts[:, :, :].rearrange("p m (k n) -> p m k n", k=IT)
        GL = qk_parts[:, :, :].rearrange("p m (k n) -> p m k n", k=IT)
        gate = sb("gate", [P, 512])
        combT = V[0:E, 0:4, :].rearrange("p t n -> p (t n)").rearrange("p (t n) -> p t n", t=NT)
        qn = sb("qn", [P, 2, D])
        kpack = V[:, :, :].rearrange("p t n -> p (t n)").bitcast(BF16).rearrange("p (n s d) -> p n s d", s=XS, d=XD)
        qpack = bv_sb[:, :].bitcast(BF16).rearrange("p (x t h s d) -> p x t h s d", x=2, t=2, h=8, s=XS)
        kT = yacc[:, :, :].rearrange("p t n -> p (t n)").bitcast(BF16).rearrange("p (b g n) -> p b g n", b=B, g=XG)
        qT = qk_room[:, :, :].rearrange("p a n -> p (a n)").bitcast(BF16).rearrange("p (x t h n) -> p x t h n", x=2, t=2, h=8)
        v_slots = room[:, VZ:VZ + NT * XG * VP].rearrange("p (n d) -> p n d", d=VP)
        oT = V[:, 0:2, :]
        WC = sb("WC", [P, 2, 2, P])
        WS = sb("WS", [P, 2, 2, P])
        qf, qf2, qr = G[:, 0, 0:256], G[:, 0, 256:512], G[:, 1, 0:256]
        on = sb("on", [P, 2, D])
        onT = sb("onT", [P, KT, 2, P])
        nxm = sb("nxm", [P, 2, 4])
        rden = sb("rden", [P, 2, 2, 4])
        WKC = sb("WKC", [P, 2, 64])
        WKS = sb("WKS", [P, 2, 64])
        kf = yacc[:, 0:2, :].rearrange("p t n -> p (t n)").rearrange("p (t n) -> p t n", t=NT)
        kf2 = yacc[:, 2:4, :].rearrange("p t n -> p (t n)").rearrange("p (t n) -> p t n", t=NT)
        kr = yacc[:, 4:6, :].rearrange("p t n -> p (t n)").rearrange("p (t n) -> p t n", t=NT)

        nh = sb("nh", [P, 2, D])
        hT = sm[:, :, :].rearrange("p a n -> p (a n)")[:, 0:512].rearrange("p (k n) -> p k n", k=KT)

        bank = [ps(f"bank{n}") for n in range(8)]
        S_B = bank[0:2]
        PT_B = bank[2:4]
        O_B = bank[4:6]

        ident = cst_sb[:, C_ID:C_ID + P]
        ident_bf = bf_sb[:, 0:P]
        mask_bf = bf_sb[:, P:2 * P]

        names = """d_x0 d_x1 d_x2 d_x3 d_ctx d_cst d_rope d_cols d_rows d_bv d_wout d_small d_wqkv d_wo d_we d_sw0 d_sw1 d_out
        bf_ready dve_seq pool_seq ssk_done wtab_ready va_ready qn_ready q_parts qpack_ready kpack_ready
        m6_pe m7_pe m6_free m7_free s_pe s_max s_exp pt_pe pt_copy_act pt_copy_dve pv_pe oT_ready o_pe o_done tanh_done
        nh_ready yacc_init hT_ready hH_ready h_ready we_half we_ready
        wqk_ready wqk_half wqk_bias wv_ready wv_half wo_ready wo_half b_recip c_gmax c_gexp c_gdiff chunk_pe chunk_f chunk_cos chunk_sw rope_done split_high split_low
        b_s b_max b_exp b_norm b_pt b_ptcopy b_pv b_oH b_oL b_wo b_yadd v_pe v_ready
        c_nh c_tr c_hT c_hH c_h c_logit c_comb c_combT_pe c_combT c_be c_init c_mid c_gelu c_gH c_gL c_exp_pe c_acc c_fin"""
        s = {n: sem(n) for n in names.split()}

        def wait(eng, name, value):
            eng.wait_ge(s[name], value)

        x_v = x.rearrange("b (t p) d -> p (b t) d", p=P)
        ctx_v = ctx_in.rearrange("b (t p) d -> p (b t) d", p=P)
        out_v = out.rearrange("b (t p) d -> p (b t) d", p=P)

        def piece(k):
            g, j = divmod(k, 3)
            return (g, 0, [4 * g + n for n in range(4)]) if j == 0 else (g, 1, [4 * g + 2 * (j - 1) + n for n in range(2)])

        M6, M7 = [("Q", 0, 0, 0), ("Q", 0, 0, 1)], [("K", b) for b in range(B)]
        for b in range(B):
            M6 += [("Q", b, 1, 0), ("Q", b, 1, 1)] + ([("OT", b - 1)] if b else [])
            M6 += [("Q", b + 1, 0, 0), ("Q", b + 1, 0, 1)] if b + 1 < B else []
            M7 += [("PJ", b), ("NT", b)]
        M6 += [("OT", B - 1)]
        m6 = {e: n for n, e in enumerate(M6)}
        m7 = {e: n for n, e in enumerate(M7)}
        NPX = XP * B

        def copied_by_act(p):
            return p % 3 != 0

        def copier(p):
            by_act = [copied_by_act(n) for n in range(p + 1)]
            return ("pt_copy_act", sum(by_act)) if by_act[p] else ("pt_copy_dve", p + 1 - sum(by_act))

        def steps(eng, step, peeled=1):
            for j in range(U):
                step(0, j)
            with eng.Fori(1, NP - peeled) as i:
                for j in range(U):
                    step(i, j)
            for i in range(NP - peeled, NP):
                for j in range(U):
                    step(i, j)
            for j in range(4):
                step(NP, j)

        def unit(i, j, lag):
            if not isinstance(i, int):
                return True
            return 0 <= U * i + j - lag < NU

        def chunk_at(j):
            return (j + LEAD) % 4, (j + LEAD) // 4 % 2

        def v_event(i, j):
            return j % 2 == 1 and (not isinstance(i, int) or (i < NP and 2 < B * i + (j + 3) // 2 < B * NP))

        def pt_copy(eng, p):
            eng.wait_ge(s["pt_pe"], p + 1)
            if p >= 2:
                eng.wait_ge(s["pv_pe"], p - 1)
            copy = eng.tensor_copy if eng is nc.vector else eng.copy
            copy(PTs[:, p % 2, :], PT_B[p % 2][:, :]).then_inc(s[copier(p)[0]], 1)

        def to_split(c, g):
            v = QT[:, c, 512 * g:512 * (g + 1)]
            if c % 2:
                return (v, *(k_split[:, m, c // 2, 512 * g:512 * (g + 1)] for m in range(2)))
            return (v.rearrange("p (b t n) -> p b t n", b=2, t=2)[:, :, 1, :], *(q_split[:, m, c // 2, 2 * g:2 * g + 2, :] for m in range(2)))

        def roped_low(eng, n, c, g):
            eng.wait_ge(s["split_high"], n + 1)
            v, high, low = to_split(c, g)
            eng.tensor_tensor(low, v, high.bitcast(F32), ALU.subtract).then_inc(s["split_low"], 1)

        h2T = qk_room[:, :, :].rearrange("p a n -> p (a n)").rearrange("p (k n) -> p k n", k=KT)

        second_nh = (nh, on)

        def output_bank(m):
            return bank[5 if isinstance(m, int) and m == NU // 2 - 1 else 7]

        def out_bank(m, hf):
            return bank[(6, 2)[m % 2] + hf]

        bank_bf = [bank[n][:, :].bitcast(BF16) for n in (6, 7)]
        block = stack.enter_context(nc.Block())

        @block.sync
        def _(sp):
            for b in range(B):
                sp.dma_start(x_sb[:, 2 * b:2 * b + 2, :], x_v[:, 2 * b:2 * b + 2, :]).then_inc(s[f"d_x{b}"], 16)
                if b == 0:
                    sp.dma_start(cst_sb[:, 0:C_RCOSQ], cst[:, 0:C_RCOSQ]).then_inc(s["d_cst"], 16)
            sp.dma_start(cols_sb[:, :], cols).then_inc(s["d_cols"], 16)
            sp.dma_start(cst_sb[:, C_RCOSQ:C_END], cst[:, C_RCOSQ:C_END]).then_inc(s["d_rope"], 16)
            sp.dma_start(stg[:, :, :, :], wqkv[0]).then_inc(s["d_wqkv"], 16)
            sp.dma_start(stgo[:, :, :], wo[0]).then_inc(s["d_wo"], 16)
            sp.dma_start(w_out_sb[:, :, :], w_out_t).then_inc(s["d_wout"], 16)
            sp.dma_start(stge[:, :], we[0]).then_inc(s["d_we"], 16)
            sp.dma_start(w_gate_sb[:, :, :], w_gate).then_inc(s["d_small"], 16)
            sp.dma_start(be2_sb[:, :], be2).then_inc(s["d_small"], 16)
            sp.wait_ge(s["wv_ready"], 1)
            sp.wait_ge(s["wqk_ready"], 4)
            sp.dma_start(stg[:, :, :, :], wqkv[1]).then_inc(s["d_wqkv"], 16)
            sp.wait_ge(s["wo_ready"], 1)
            sp.dma_start(stgo[:, :, :], wo[1]).then_inc(s["d_wo"], 16)
            sp.wait_ge(s["m6_pe"], m6["Q", B - 1, 1, 1] + 1)
            sp.dma_start(bv_sb[:, :], bv.to_broadcast([P, H * HD])).then_inc(s["d_bv"], 16)

            def swap(n, q):
                sp.wait_ge(s["chunk_f"], n + 1)
                sp.dma_start(qk_sw[0:64, q, :], qk_f[64:128, q, :]).then_inc(s[f"d_sw{q}"], 16)
                sp.dma_start(qk_sw[64:128, q, :], qk_f[0:64, q, :]).then_inc(s[f"d_sw{q}"], 16)

            for n in range(LEAD):
                swap(n, n % 2)

            def step(i, j):
                if unit(i, j, -LEAD):
                    swap(U * i + j + LEAD, j % 2)
            steps(sp, step)
            for b in range(B):
                sp.wait_ge(s["c_fin"], b + 1)
                sp.dma_start(out_v[:, 2 * b:2 * b + 2, :], yacc[:, 2 * b:2 * b + 2, :]).then_inc(s["d_out"], 16)
            sp.wait_ge(s["d_out"], 16 * B)

        @block.gpsimd
        def _(pool):
            seq = [0]

            def link(ins):
                seq[0] += 1
                ins.then_inc(s["pool_seq"], 1)
                pool.wait_ge(s["pool_seq"], seq[0])

            link(pool.memset(room[:, :], 0.0))
            pool.memset(v_slots[:, :, XD:XD + 1], 1.0).then_inc(s["va_ready"], 1)
            pool.wait_ge(s["d_rows"], 16)
            pool.wait_ge(s["d_cst"], 16)
            for t in range(2):
                def table(col, heads):
                    return cst_sb[:, col + t * XD:col + (t + 1) * XD].unsqueeze(1).to_broadcast([P, heads, XD])
                w = rows_sb[:, R_KW:R_KW + 64].rearrange("p (h d) -> p h d", d=XD)
                c, sn = table(C_XCOS, 4), table(C_XSIN, 4)
                wks = WKS[:, t, :].rearrange("p (h d) -> p h d", d=XD)
                pool.tensor_tensor(WKC[:, t, :].rearrange("p (h d) -> p h d", d=XD), w, c, ALU.mult).then_inc(s["wtab_ready"], 1)
                pool.tensor_tensor(wks[:, :, 0:8], w[:, :, 8:16], sn[:, :, 0:8], ALU.mult).then_inc(s["wtab_ready"], 1)
                pool.tensor_tensor(wks[:, :, 8:16], w[:, :, 0:8], sn[:, :, 8:16], ALU.mult).then_inc(s["wtab_ready"], 1)
            for X in range(2):
                for t in range(2):
                    c = cst_sb[:, C_XCOS + t * XD:C_XCOS + (t + 1) * XD].unsqueeze(1).to_broadcast([P, 8, XD])
                    sn = cst_sb[:, C_XSIN + t * XD:C_XSIN + (t + 1) * XD].unsqueeze(1).to_broadcast([P, 8, XD])
                    w = rows_sb[:, R_QW + X * P:R_QW + (X + 1) * P].rearrange("p (h d) -> p h d", d=XD)
                    ws = WS[:, X, t, :].rearrange("p (h d) -> p h d", d=XD)
                    pool.tensor_tensor(WC[:, X, t, :].rearrange("p (h d) -> p h d", d=XD), w, c, ALU.mult)
                    pool.tensor_tensor(ws[:, :, 0:8], w[:, :, 8:16], sn[:, :, 0:8], ALU.mult)
                    last = pool.tensor_tensor(ws[:, :, 8:16], w[:, :, 0:8], sn[:, :, 8:16], ALU.mult)
            link(last)

            def prep(b, X):
                if X == 0:
                    pool.wait_ge(s["qn_ready"], b + 1)
                if b:
                    pool.wait_ge(s["m6_pe"], m6["Q", b - 1, X, 1] + 1)
                qv = qn[:, :, X * P:(X + 1) * P]
                q4 = qv.rearrange("p t (h d) -> p t h d", d=XD)
                g4 = qf2[:, :].rearrange("p (t h d) -> p t h d", t=2, d=XD)
                w4 = WS[:, X, :, :].rearrange("p t (h d) -> p t h d", d=XD)
                pool.tensor_tensor(qf[:, :].rearrange("p (t n) -> p t n", t=2), qv, WC[:, X, :, :], ALU.mult)
                for t in range(2):
                    pool.tensor_tensor(g4[:, t, :, 0:8], q4[:, t, :, 8:16], w4[:, t, :, 0:8], ALU.mult)
                    last = pool.tensor_tensor(g4[:, t, :, 8:16], q4[:, t, :, 0:8], w4[:, t, :, 8:16], ALU.mult)
                link(last)
                link(pool.tensor_tensor(qf[:, :], qf[:, :], qf2[:, :], ALU.add))
                part = qpack[:, X, :, :, :, :].rearrange("p t h s d -> p (t h) s d")
                f = qf[:, :].rearrange("p (n d) -> p n d", d=XD)
                r = qr[:, :].rearrange("p (n d) -> p n d", d=XD)
                link(pool.tensor_copy(part[:, :, 0, :], f))
                link(pool.tensor_tensor(r, f, part[:, :, 0, :], ALU.subtract))
                link(pool.tensor_copy(part[:, :, 3, :], r))
                link(pool.tensor_tensor(r, r, part[:, :, 3, :], ALU.subtract))
                pool.tensor_copy(part[:, :, 6, :], r).then_inc(s["q_parts"], 1)
                pool.wait_ge(s["q_parts"], 2 * b + X + 1)

            def low_qk(c, p):
                r, k = divmod(c, 2)
                col = B_BQ + 16 * k + 2 * p + r
                pool.tensor_copy(qk_bias[:, c:c + 1], cols_sb[:, bass.ds(col, 1)]).then_inc(s["wqk_bias"], 1)
                pool.wait_ge(s["wqk_half"], 4 * p + c + 1)
                pool.tensor_tensor(wqkL[:, c], stg[:, k, :, r * HD:(r + 1) * HD], wqkH[:, c].bitcast(F32),
                                   ALU.subtract).then_inc(s["wqk_ready"], 1)

            def low_v(p):
                pool.wait_ge(s["wv_half"], p + 1)
                pool.tensor_tensor(wvL[:, :, :], stg[:, W_V, :, :], wvH[:, :, :].bitcast(F32), ALU.subtract).then_inc(s["wv_ready"], 1)

            def low_o(p):
                pool.wait_ge(s["wo_half"], p + 1)
                pool.tensor_tensor(woL[:, :, :], stgo[:, :, :], woH[:, :, :].bitcast(F32), ALU.subtract).then_inc(s["wo_ready"], 1)

            prep(0, 0)
            prep(0, 1)
            pool.wait_ge(s["d_ctx"], 16)
            for b in range(B):
                if b == 0:
                    pool.wait_ge(s["va_ready"], 1)
                pool.tensor_copy(v_slots[:, 2 * XG * b:2 * XG * (b + 1), 0:XD], ctx_sb[:, 2 * b:2 * b + 2, :].rearrange("p t (g d) -> p (t g) d", d=XD)).then_inc(s["va_ready"], 1)
            prep(1, 0)
            prep(1, 1)
            prep(2, 0)
            prep(2, 1)
            prep(3, 0)
            prep(3, 1)
            pool.wait_ge(s["d_wqkv"], 16)
            pool.wait_ge(s["d_cols"], 16)
            for c in range(4):
                r, k = divmod(c, 2)
                pool.tensor_copy(wqkH[:, c], stg[:, k, :, r * HD:(r + 1) * HD]).then_inc(s["wqk_half"], 1)
                low_qk(c, 0)
            pool.tensor_copy(wvH[:, :, :], stg[:, W_V, :, :]).then_inc(s["wv_half"], 1)
            low_v(0)
            pool.wait_ge(s["d_wo"], 16)
            pool.tensor_copy(woH[:, :, :], stgo[:, :, :]).then_inc(s["wo_half"], 1)
            low_o(0)

            def hidden_low(b):
                pool.wait_ge(s["hH_ready"], b + 1)
                cut = slice(256 * b, 256 * (b + 1))
                pool.tensor_tensor(hL[:, :, cut], hT[:, :, :], hH[:, :, cut].bitcast(F32), ALU.subtract).then_inc(s["h_ready"], 1)
                pool.wait_ge(s["nh_ready"], b + 1)
                y = yacc[:, 2 * b:2 * b + 2, :]
                pool.tensor_tensor(y, y, rows_sb[:, R_BO:R_BO + D].unsqueeze(1).to_broadcast([P, 2, D]), ALU.add).then_inc(s["yacc_init"], 1)

            def rope_sin(sw_count, q, k):
                pool.wait_ge(s[f"d_sw{q}"], sw_count)
                col = C_RSINK if k else C_RSINQ
                v = qk_sw[:, q, :].rearrange("p (b t) -> p b t", b=2)
                pool.tensor_tensor(v, v, cst_sb[:, col:col + 256].unsqueeze(1).to_broadcast([P, 2, 256]), ALU.mult).then_inc(s["chunk_sw"], 1)

            for b in range(B - 1):
                hidden_low(b)
            pool.wait_ge(s["d_rope"], 16)
            for n in range(LEAD):
                rope_sin(32 * (n // 2 + 1), n % 2, n % 2)
                if n == 1:
                    hidden_low(B - 1)
            pool.wait_ge(s["split_low"], 4)

            def step(i, j):
                more = not (isinstance(i, int) and i >= NP - 1)
                if more and j < 4:
                    low_qk(j, i + 1)
                if j == 3 and not (isinstance(i, int) and (i == 0 or i >= NP - 1)):
                    low_o(i)
                if more and j == 4:
                    low_v(i + 1)
                if j == 7 and not (isinstance(i, int) and i >= NP):
                    pool.wait_ge(s["we_half"], i + 1)
                    cut = bass.ds(WE_CUT * i, WE_CUT)
                    pool.tensor_tensor(weL[:, cut], stge[:, :], weH[:, cut].bitcast(F32), ALU.subtract).then_inc(s["we_ready"], 1)
                if unit(i, j, -4):
                    roped_low(pool, U * i + j + 4, j % 4, (j + 4) // 4 % 2)
                if j == 3 and isinstance(i, int) and i == NP - 1:
                    low_o(i)
                if unit(i, j, -LEAD):
                    rope_sin(32 * (4 * i + (j + LEAD) // 2 + 1), j % 2, j % 2)

            steps(pool, step)

            def hidden_low2(b):
                pool.wait_ge(s["c_hH"], b + 1)
                cut = slice(256 * b, 256 * (b + 1))
                pool.tensor_tensor(hL[:, :, cut], h2T[:, :, cut], hH[:, :, cut].bitcast(F32), ALU.subtract).then_inc(s["c_h"], 1)

            def middle_low(n):
                pool.wait_ge(s["c_gH"], n + 1)
                pool.tensor_tensor(GL[:, (n // 2) % 2, n % 2, :], G[:, n % 2, :], GH[:, (n // 2) % 2, n % 2, :].bitcast(F32),
                                   ALU.subtract).then_inc(s["c_gL"], 1)

            hidden_low2(0)
            hidden_low2(1)
            for n in range(2 * NE):
                if n in (2, 4):
                    hidden_low2(1 + n // 2)
                middle_low(n)

        @block.scalar
        def _(act):
            act.dma_start(ctx_sb[:, :, :], ctx_v).then_inc(s["d_ctx"], 16)
            act.dma_start(rows_sb[:, :], rows.to_broadcast([P, R_END])).then_inc(s["d_rows"], 16)
            act.wait_ge(s["d_ctx"], 16)
            for t in range(NT):
                ins = act.activation(kf2[:, t, :], ctx_sb[:, t, :], ACT.Square, accum_out=small[:, 8 + t:9 + t])
                ins.then_inc(s["ssk_done"], 1)
            act.wait_ge(s["d_rows"], 16)
            act.activation(small[:, 96:98], rows_sb[:, R_GX:R_GX + 2], ACT.Tanh).then_inc(s["tanh_done"], 1)

            def q_evac(b, X, t):
                n = m6["Q", b, X, t]
                act.wait_ge(s["m6_pe"], n + 1)
                act.activation(qT[:, X, t, :, :].rearrange("p h n -> p (h n)"), bank_bf[0][:, :], ACT.Copy).then_inc(s["m6_free"], 1)

            def o_evac(b):
                act.wait_ge(s["m6_pe"], m6["OT", b] + 1)
                act.activation(onT[:, :, :, :].rearrange("p k t n -> p (k t n)"), bank[6][:, :], ACT.Copy).then_inc(s["m6_free"], 1)

            def h_high(b):
                act.wait_ge(s["hT_ready"], b + 1)
                act.activation(hH[:, :, 256 * b:256 * (b + 1)], hT[:, :, :], ACT.Copy).then_inc(s["hH_ready"], 1)

            def oT_evac(m):
                act.wait_ge(s["pv_pe"], 3 * m + 3)
                if m >= 2:
                    act.wait_ge(s["o_pe"], m - 1)
                act.activation(oT[:, m % 2, :], bank[4][:, 0:256], ACT.Copy).then_inc(s["oT_ready"], 1)

            q_evac(0, 0, 0)
            q_evac(0, 0, 1)
            for p in range(NPX):
                b, k = divmod(p, XP)
                g, t, heads = piece(k)
                width = P * (t + 1)
                if p >= 2 and copied_by_act(p - 2):
                    pt_copy(act, p - 2)
                act.wait_ge(s["s_max"], p + 1)
                if p >= 2:
                    act.wait_ge(s["pt_pe"], p - 1)
                for n, h in enumerate(heads):
                    ins = act.activation(PR[:, p % 2, n * width:(n + 1) * width], S_B[p % 2][:, n * width:(n + 1) * width],
                                         ACT.Exp, bias=nxm[:, p % 2, n:n + 1])
                ins.then_inc(s["s_exp"], 1)
                if k in (2, 3):
                    q_evac(b, 1, k - 2)
                if k == 5 and b:
                    o_evac(b - 1)
                if k in (7, 9) and b + 1 < B:
                    q_evac(b + 1, 0, (k - 7) // 2)
                if k == 4 and b >= 2:
                    h_high(b - 2)
                if p >= 5 and p % 3 == 2:
                    oT_evac((p - 5) // 3)
            for p in range(NPX - 2, NPX):
                if copied_by_act(p):
                    pt_copy(act, p)
            oT_evac(NPX // 3 - 1)
            h_high(B - 2)
            o_evac(B - 1)

            def chunk_out(n, q, c, guard):
                act.wait_ge(s["chunk_pe"], n + 1)
                if guard:
                    act.wait_ge(s["rope_done"], n - 1)
                act.activation(qk_f[:, q, :], O_B[q][:, :], ACT.Identity, bias=qk_bias[:, c:c + 1]).then_inc(s["chunk_f"], 1)

            def roped_high(n, c, g):
                act.wait_ge(s["rope_done"], n + 1)
                v, high, _ = to_split(c, g)
                act.activation(high, v, ACT.Copy).then_inc(s["split_high"], 1)

            act.wait_ge(s["wqk_bias"], 4)
            for n in range(LEAD):
                if n == 3:
                    h_high(B - 1)
                if n >= 2:
                    roped_high(n - 2, n - 2, 0)
                chunk_out(n, n % 2, n % 4, n >= 2)

            def step(i, j):
                T = U * i + j
                q = j % 2
                more = not (isinstance(i, int) and i >= NP - 1)
                if unit(i, j, 0):
                    act.wait_ge(s["b_max"], T + 1)
                    if unit(i, j, 2):
                        act.wait_ge(s["b_pt"], T - 1)
                    for t in range(2):
                        a, e = ((0, P), (P, 3 * P))[t]
                        ins = act.activation(PR[:, q, a:e], sm[:, q, a:e], ACT.Exp, bias=nm[:, q, t:t + 1], scale=-1.0,
                                             accum_out=rs[:, q, t:t + 1])
                        ins.then_inc(s["b_exp"], 1)
                if unit(i, j, -LEAD):
                    if 2 <= j < 6:
                        act.wait_ge(s["wqk_bias"], 4 * (i + 1) + j - 2 + 1)
                    chunk_out(T + LEAD, q, chunk_at(j)[0], True)
                elif unit(i, j, -4):
                    roped_high(T + 4, j % 4, (j + 4) // 4 % 2)
                if unit(i, j, 1):
                    act.wait_ge(s["b_pt"], T)
                    if unit(i, j, 3):
                        act.wait_ge(s["b_pv"], T - 2)
                    act.activation(PTs[:, 1 - q, 0:384], bank[2][:, 0:384], ACT.Copy).then_inc(s["b_ptcopy"], 1)
                if unit(i, j, 2):
                    act.wait_ge(s["b_pv"], T - 1)
                    if unit(i, j, 6):
                        act.wait_ge(s["b_wo"], 4 * i + (j - 2) // 2 - 1)
                    act.activation(oH[:, ((j - 2) // 2) % 2, q, :], bank[3][:, 0:256], ACT.Copy).then_inc(s["b_oH"], 1)
                if unit(i, j, -LEAD):
                    roped_high(U * i + j + 4, j % 4, (j + 4) // 4 % 2)
                if more and j < 4:
                    if j == 0:
                        act.wait_ge(s["d_wqkv"], 16 * (i + 2))
                    r, k = divmod(j, 2)
                    act.activation(wqkH[:, j], stg[:, k, :, r * HD:(r + 1) * HD], ACT.Copy).then_inc(s["wqk_half"], 1)
                if j == 3 and not (isinstance(i, int) and (i == 0 or i >= NP)):
                    act.wait_ge(s["d_wo"], 16 * (i + 1))
                    act.wait_ge(s["b_wo"], 4 * i)
                    act.activation(woH[:, :, :], stgo[:, :, :], ACT.Copy).then_inc(s["wo_half"], 1)
                if more and j == 4:
                    act.wait_ge(s["v_pe"], 4 * i + 4)
                    act.activation(wvH[:, :, :], stg[:, W_V, :, :], ACT.Copy).then_inc(s["wv_half"], 1)
                if j == 0 and not (isinstance(i, int) and (i == 0 or i >= NP)):
                    act.wait_ge(s["we_ready"], i)
                    act.dma_start(stge[:, :], we[bass.ds(i, 1)].rearrange("a p n -> (a p) n")).then_inc(s["d_we"], 16)
                if j == 5 and not (isinstance(i, int) and (i == 0 or i >= NP - 1)):
                    act.wait_ge(s["wo_ready"], i + 1)
                    act.dma_start(stgo[:, :, :], wo[bass.ds(i + 1, 1)].rearrange("a p w n -> (a p) w n")).then_inc(s["d_wo"], 16)
                if j == 6 and not (isinstance(i, int) and i >= NP):
                    act.wait_ge(s["d_we"], 16 * (i + 1))
                    act.activation(weH[:, bass.ds(WE_CUT * i, WE_CUT)], stge[:, :], ACT.Copy).then_inc(s["we_half"], 1)
                if j == 6 and not (isinstance(i, int) and i >= NP - 2):
                    act.wait_ge(s["wqk_ready"], 4 * (i + 2))
                    act.wait_ge(s["wv_ready"], i + 2)
                    act.dma_start(stg[:, :, :, :], wqkv[bass.ds(i + 2, 1)].rearrange("a p w k n -> (a p) w k n")).then_inc(s["d_wqkv"], 16)

            steps(act, step, 2)

            def hidden_high2(b):
                act.wait_ge(s["c_hT"], b + 1)
                act.activation(hH[:, :, 256 * b:256 * (b + 1)], h2T[:, :, 256 * b:256 * (b + 1)], ACT.Copy).then_inc(s["c_hH"], 1)

            hidden_high2(0)
            hidden_high2(1)
            act.wait_ge(s["b_wo"], NU // 2)
            for n in range(2 * NE):
                if n in (2, 4):
                    hidden_high2(1 + n // 2)
                if n == 4:
                    act.wait_ge(s["c_gmax"], 1)
                    act.activation(gate[:, 64:96], gate[:, 32:64], ACT.Exp).then_inc(s["c_gexp"], 1)
                    act.wait_ge(s["c_gdiff"], 1)
                    act.activation(gate[:, 400:408], gate[:, 392:400], ACT.Exp).then_inc(s["c_gexp"], 1)
                c, m = divmod(n, NE)
                act.wait_ge(s["c_mid"], n + 1)
                if n >= 2:
                    act.wait_ge(s["c_gL"], n - 1)
                act.activation(G[:, n % 2, :], bank[n % 2][:, :], ACT.Gelu,
                               bias=cols_sb[:, B_BE1 + m:B_BE1 + m + 1]).then_inc(s["c_gelu"], 1)
                act.wait_ge(s["c_gelu"], n + 1)
                if n >= 4:
                    act.wait_ge(s["c_exp_pe"], 2 * (n // 2 - 1))
                act.activation(GH[:, (n // 2) % 2, n % 2, :], G[:, n % 2, :], ACT.Copy).then_inc(s["c_gH"], 1)

        @block.vector
        def _(dve):
            seq = [0]

            def link(ins):
                seq[0] += 1
                ins.then_inc(s["dve_seq"], 1)
                dve.wait_ge(s["dve_seq"], seq[0])

            def rsqrt_seed(v, y, h):
                dve.tensor_scalar(y.bitcast(I32), v.bitcast(I32), -0.5, RSQRT_SEED, ALU.mult, ALU.add)
                link(dve.tensor_scalar(h, v, -0.5, None, ALU.mult))

            def rsqrt_step(h, y, t, n):
                if n <= 2:
                    for c in range(n):
                        ins = dve.tensor_scalar(t[:, c:c + 1], y[:, c:c + 1], y[:, c:c + 1], h[:, c:c + 1], ALU.mult, ALU.mult)
                    link(ins)
                else:
                    link(dve.tensor_tensor(t, y, y, ALU.mult))
                    link(dve.tensor_tensor(t, t, h, ALU.mult))
                link(dve.scalar_tensor_tensor(y, t, 1.5, y, ALU.add, ALU.mult))


            dve.wait_ge(s["d_cst"], 16)
            dve.tensor_copy(ident_bf, ident)
            dve.tensor_scalar(mask_bf, cst_sb[:, C_MASK + P:C_MASK + 2 * P], -1.0, None, ALU.mult).then_inc(s["bf_ready"], 1)

            SM = lambda a, n: small[:, a:a + n]
            q_scale = lambda n: 32 + n if n < 2 else 54 + n

            def stats(first, last):
                for t in range(first, last):
                    if t % 2 == 0:
                        dve.wait_ge(s[f"d_x{t // 2}"], 16)
                    ins = dve.bn_stats(bnst[:, t, :], x_sb[:, t, :])
                link(ins)
                for t in range(first, last):
                    ins = dve.bn_aggr(mv[:, t, :], bnst[:, t, :])
                link(ins)

            stats(0, 2)
            dve.tensor_scalar(SM(16, 2), mv[:, 0:2, 1], 1.0 + EPS, EPS * EPS, ALU.mult, ALU.add)
            dve.wait_ge(s["ssk_done"], NT)
            link(dve.tensor_scalar(SM(18, 8), SM(8, 8), XD / 64, XD * EPS, ALU.mult, ALU.add))
            rsqrt_seed(SM(16, 10), SM(32, 10), SM(70, 10))
            for _ in range(3):
                rsqrt_step(SM(70, 10), SM(32, 10), SM(80, 10), 10)

            def norm_q(b):
                if b:
                    dve.wait_ge(s["q_parts"], 2 * b)
                for t in range(2):
                    n = 2 * b + t
                    ins = dve.tensor_scalar(qn[:, t, :], x_sb[:, n, :], mv[:, n, 0:1], small[:, q_scale(n):q_scale(n) + 1], ALU.subtract, ALU.mult)
                ins.then_inc(s["qn_ready"], 1)

            norm_q(0)
            link(dve.tensor_tensor(kr, ctx_sb[:, :, :], SM(34, 8).unsqueeze(2).to_broadcast([P, NT, 64]), ALU.mult))
            dve.wait_ge(s["wtab_ready"], 6)
            kb = kr[:, :, :].rearrange("p (b t) n -> p b (t n)", t=2)
            k4 = kr[:, :, :].rearrange("p (b t) (g d) -> p b (t g) d", t=2, d=XD)
            f4 = kf2[:, :, :].rearrange("p (b t) (g d) -> p b (t g) d", t=2, d=XD)
            w4 = WKS[:, :, :].rearrange("p t (g d) -> p (t g) d", d=XD)
            dve.tensor_tensor(kf[:, :, :].rearrange("p (b t) n -> p b (t n)", t=2), kb,
                              WKC[:, :, :].rearrange("p t n -> p (t n)").unsqueeze(1).to_broadcast([P, B, P]), ALU.mult)
            dve.tensor_tensor(f4[:, :, :, 0:8], k4[:, :, :, 8:16], w4[:, :, 0:8].unsqueeze(1).to_broadcast([P, B, 8, 8]), ALU.mult)
            link(dve.tensor_tensor(f4[:, :, :, 8:16], k4[:, :, :, 0:8], w4[:, :, 8:16].unsqueeze(1).to_broadcast([P, B, 8, 8]), ALU.mult))
            link(dve.tensor_tensor(kf[:, :, :], kf[:, :, :], kf2[:, :, :], ALU.add))
            kv = kf[:, :, :].rearrange("p t (g d) -> p (t g) d", d=XD)
            krv = kr[:, :, :].rearrange("p t (g d) -> p (t g) d", d=XD)
            link(dve.tensor_copy(kpack[:, :, 0, :], kv))
            link(dve.tensor_tensor(krv, kv, kpack[:, :, 0, :], ALU.subtract))
            link(dve.tensor_copy(kpack[:, :, 1, :], krv))
            link(dve.tensor_tensor(krv, krv, kpack[:, :, 1, :], ALU.subtract))
            link(dve.tensor_copy(kpack[:, :, 2, :], krv))
            dve.tensor_copy(kpack[:, :, 3:6, :], kpack[:, :, 0:3, :])
            dve.tensor_copy(kpack[:, :, 6:8, :], kpack[:, :, 0:2, :]).then_inc(s["kpack_ready"], 1)

            def pack(b, X):
                dve.wait_ge(s["q_parts"], 2 * b + X + 1)
                v = qpack[:, X, :, :, :, :].rearrange("p t h s d -> p (t h) s d")
                dve.tensor_copy(v[:, :, 1, :], v[:, :, 0, :])
                dve.tensor_copy(v[:, :, 2, :], v[:, :, 0, :])
                dve.tensor_copy(v[:, :, 4, :], v[:, :, 3, :])
                dve.tensor_copy(v[:, :, 5, :], v[:, :, 3, :])
                dve.tensor_copy(v[:, :, 7, :], v[:, :, 6, :]).then_inc(s["qpack_ready"], 1)

            def k_out(b):
                dve.wait_ge(s["m7_pe"], m7["K", b] + 1)
                dve.tensor_copy(kT[:, b, :, :].rearrange("p g n -> p (g n)"), bank_bf[1][:, :]).then_inc(s["m7_free"], 1)

            k_out(0)
            pack(0, 0)
            stats(2, NT)
            k_out(1)
            link(dve.tensor_scalar(SM(48, 6), mv[:, 2:NT, 1], 1.0 + EPS, EPS * EPS, ALU.mult, ALU.add))
            rsqrt_seed(SM(48, 6), SM(56, 6), SM(124, 6))
            rsqrt_step(SM(124, 6), SM(56, 6), SM(130, 6), 6)
            k_out(2)
            rsqrt_step(SM(124, 6), SM(56, 6), SM(130, 6), 6)
            k_out(3)

            def norm_out(m):
                b, g = divmod(m, XG)
                dve.wait_ge(s["o_pe"], m + 1)
                if g == 0 and b:
                    dve.wait_ge(s["m6_pe"], m6["OT", b - 1] + 1)
                o = bank[5][:, 0:256].rearrange("p (t h d) -> p t h d", t=2, h=4)
                r = rden[:, m % 2, :, :]
                dve.reciprocal(r.unsqueeze(3), o[:, :, :, XD:XD + 1]).then_inc(s["o_done"], 1)
                dve.wait_ge(s["o_done"], 2 * m + 1)
                ins = dve.tensor_tensor(on[:, :, 64 * g:64 * (g + 1)].rearrange("p t (h d) -> p t h d", d=XD), o[:, :, :, 0:XD],
                                        r.unsqueeze(3).to_broadcast([P, 2, 4, XD]), ALU.mult)
                ins.then_inc(s["o_done"], 1)

            def residual(b, phase):
                v, y, h, w = SM(112, 4), SM(116, 4), SM(120, 4), SM(136, 4)
                xb = x_sb[:, 2 * b:2 * b + 2, :]
                if phase == 0:
                    dve.wait_ge(s["m7_pe"], m7["PJ", b] + 1)
                    dve.wait_ge(s["tanh_done"], 1)
                    ins = dve.scalar_tensor_tensor(xb.rearrange("p t n -> p (t n)"), bank[7][:, :], small[:, 96:97],
                                                   xb.rearrange("p t n -> p (t n)"), ALU.mult, ALU.add)
                    ins.then_inc(s["m7_free"], 1)
                if phase == 1:
                    dve.wait_ge(s["m7_free"], m7["PJ", b] + 1)
                    for t in range(2):
                        ins = dve.bn_stats(bnst[:, t, :], x_sb[:, 2 * b + t, :])
                    link(ins)
                    for t in range(2):
                        ins = dve.bn_aggr(mv[:, 2 * b + t, :], bnst[:, t, :])
                    link(ins)
                if phase == 2:
                    dve.tensor_scalar(v[:, 0:2], mv[:, 2 * b:2 * b + 2, 1], EPS, None, ALU.add)
                    link(dve.tensor_scalar(v[:, 2:4], mv[:, 2 * b:2 * b + 2, 1], 1.0 + EPS, EPS * EPS, ALU.mult, ALU.add))
                    rsqrt_seed(v, y, h)
                if 3 <= phase <= 5:
                    rsqrt_step(h, y, w, 4)
                if phase == 5:
                    for t in range(2):
                        n = 2 * b + t
                        ins = dve.tensor_scalar(yacc[:, n, :], x_sb[:, n, :], mv[:, n, 0:1], y[:, t:t + 1], ALU.subtract, ALU.mult)
                    if b:
                        dve.wait_ge(s["m7_pe"], m7["NT", b - 1] + 1)
                    for t in range(2):
                        n = 2 * b + t
                        ins = dve.tensor_scalar(nh[:, t, :], x_sb[:, n, :], mv[:, n, 0:1], y[:, 2 + t:3 + t], ALU.subtract, ALU.mult)
                    ins.then_inc(s["nh_ready"], 1)

            def affine(b, dst, bank_n, w, bias):
                for k in range(KT):
                    ins = dve.tensor_scalar(dst[:, k, :], bank[bank_n][:, 256 * k:256 * (k + 1)], cols_sb[:, w + k:w + k + 1],
                                            cols_sb[:, bias + k:bias + k + 1], ALU.mult, ALU.add)
                return ins

            def hidden_t(b):
                dve.wait_ge(s["m7_pe"], m7["NT", b] + 1)
                if b == 0:
                    dve.wait_ge(s["d_cols"], 16)
                else:
                    dve.wait_ge(s["h_ready"], b)
                ins = affine(b, hT, 7, B_L1W, B_L1B)
                ins.then_inc(s["m7_free"], 1)
                dve.wait_ge(s["m7_free"], m7["NT", b] + 1)
                dve.memset(small[:, 110:111], 0.0).then_inc(s["hT_ready"], 1)

            for p in range(NPX):
                b, k = divmod(p, XP)
                g, t, heads = piece(k)
                dve.wait_ge(s["s_pe"], p + 1)
                if p >= 2:
                    dve.wait_ge(s["s_exp"], p - 1)
                dve.tensor_reduce(nxm[:, p % 2, 0:len(heads)], S_B[p % 2][:, :].rearrange("p (h n) -> p h n", h=len(heads)),
                                  AX.X, ALU.max, negate=True).then_inc(s["s_max"], 1)
                if p >= 2 and not copied_by_act(p - 2):
                    pt_copy(dve, p - 2)
                if p == 0:
                    rsqrt_step(SM(124, 6), SM(56, 6), SM(130, 6), 6)
                if p == 1:
                    pack(0, 1)
                if k == 1 and b + 1 < B:
                    norm_q(b + 1)
                if k == 2 and b >= 2:
                    hidden_t(b - 2)
                if p >= 6 and p % 3 == 0:
                    norm_out((p - 6) // 3)
                if k == 5 and b + 1 < B:
                    pack(b + 1, 0)
                if k >= 6 and b:
                    residual(b - 1, k - 6)
                if k == 10 and b + 1 < B:
                    pack(b + 1, 1)
            for p in range(NPX - 2, NPX):
                if not copied_by_act(p):
                    pt_copy(dve, p)
            norm_out(NPX // 3 - 2)
            hidden_t(B - 2)
            norm_out(NPX // 3 - 1)

            def rope_cos(n, q, c, cols_):
                dve.wait_ge(s["chunk_f"], n + 1)
                col = C_RCOSK if c % 2 else C_RCOSQ
                dve.tensor_tensor(QT[:, c, cols_].rearrange("p (b t) -> p b t", b=2), qk_f[:, q, :].rearrange("p (b t) -> p b t", b=2),
                                  cst_sb[:, col:col + 256].unsqueeze(1).to_broadcast([P, 2, 256]), ALU.mult).then_inc(s["chunk_cos"], 1)

            def rope_add(n, q, c, cols_):
                dve.wait_ge(s["chunk_sw"], n + 1)
                dve.wait_ge(s["chunk_cos"], n + 1)
                dve.tensor_tensor(QT[:, c, cols_], QT[:, c, cols_], qk_sw[:, q, :], ALU.add).then_inc(s["rope_done"], 1)

            def v_out(m, b, p):
                dve.wait_ge(s["v_pe"], m + 1)
                bias = bv_sb[:, bass.ds(256 * p, 256)].unsqueeze(1).to_broadcast([P, 2, 256])
                dve.tensor_tensor(V[:, 2 * b:2 * b + 2, :], bank[6][:, :].rearrange("p (t n) -> p t n", t=2), bias, ALU.add).then_inc(s["v_ready"], 1)

            groups = (slice(0, 512), slice(512, 1024))
            dve.wait_ge(s["d_bv"], 16)
            dve.wait_ge(s["d_rope"], 16)
            residual(B - 1, 0)
            residual(B - 1, 1)
            rope_cos(0, 0, 0, groups[0])
            v_out(0, 0, 0)
            for phase in (2, 3, 4, 5):
                residual(B - 1, phase)
            rope_cos(1, 1, 1, groups[0])
            v_out(1, 1, 0)
            rope_add(0, 0, 0, groups[0])
            hidden_t(B - 1)
            rope_add(1, 1, 1, groups[0])
            rope_cos(2, 0, 2, groups[0])
            roped_low(dve, 0, 0, 0)
            roped_low(dve, 1, 1, 0)
            rope_add(2, 0, 2, groups[0])
            v_out(2, 2, 0)
            rope_cos(3, 1, 3, groups[0])
            roped_low(dve, 2, 2, 0)
            rope_add(3, 1, 3, groups[0])
            def second_norm(b, phase, batches=1):
                n = 2 * batches
                v, y, h, w = SM(112, n), SM(116, n), SM(120, n), SM(136, n)
                if phase == 0:
                    dve.wait_ge(s["b_yadd"], NU // 2 - B + b + batches)
                    for t in range(n):
                        ins = dve.bn_stats(bnst[:, t, :], yacc[:, 2 * b + t, :])
                    link(ins)
                    for t in range(n):
                        ins = dve.bn_aggr(mv[:, 2 * b + t, :], bnst[:, t, :])
                    link(ins)
                if phase == 1:
                    link(dve.tensor_scalar(v, mv[:, 2 * b:2 * b + n, 1], EPS, None, ALU.add))
                    rsqrt_seed(v, y, h)
                if 2 <= phase <= 4:
                    rsqrt_step(h, y, w, n)
                if phase == 5:
                    for t in range(n):
                        if b + t // 2 >= 2 and t % 2 == 0:
                            dve.wait_ge(s["c_tr"], b + t // 2 - 1)
                        ins = dve.tensor_scalar(second_nh[(b + t // 2) % 2][:, t % 2, :], yacc[:, 2 * b + t, :], mv[:, 2 * b + t, 0:1],
                                                y[:, t:t + 1], ALU.subtract, ALU.mult)
                        if t % 2:
                            ins.then_inc(s["c_nh"], 1)

            def second_t(b):
                dve.wait_ge(s["c_tr"], b + 1)
                affine(b, h2T[:, :, 256 * b:256 * (b + 1)], 4, B_L2W, B_L2B).then_inc(s["c_hT"], 1)

            def o_low(T, j):
                dve.wait_ge(s["b_oH"], T - 1)
                h = oH[:, ((j - 2) // 2) % 2, j % 2, :]
                dve.tensor_tensor(oL[:, ((j - 2) // 2) % 2, j % 2, :], bank[3][:, 0:256], h.bitcast(F32), ALU.subtract).then_inc(s["b_oL"], 1)

            def maxima(i, j):
                T, q = U * i + j, j % 2
                dve.wait_ge(s["b_s"], T + 1)
                if unit(i, j, 2):
                    dve.wait_ge(s["b_exp"], 2 * (T - 1))
                dve.memset(small[:, 111:112], 0.0)
                dve.tensor_tensor_reduce(sm[:, q, 0:P], S_B[q][:, 0:P], cst_sb[:, C_MASK + P:C_MASK + 256], 1.0, 3e38,
                                         ALU.add, ALU.min, nm[:, q, 0:1])
                dve.tensor_tensor_reduce(sm[:, q, P:3 * P], S_B[q][:, P:3 * P], cst_sb[:, C_MASK:C_MASK + 256], 1.0, 3e38,
                                         ALU.add, ALU.min, nm[:, q, 1:2]).then_inc(s["b_max"], 1)

            dve.wait_ge(s["h_ready"], B)
            maxima(0, 0)
            roped_low(dve, 3, 3, 0)
            for n in range(4, LEAD):
                rope_cos(n, n % 2, n % 4, groups[1])
            dve.wait_ge(s["yacc_init"], B)

            while_exp = {61: [(0, 0)], 62: [(0, 1), (0, 2)], 63: [(0, 3)]}
            extra = {63: [(0, 4), (0, 5)],
                     64: [(1, 0), (1, 1)], 65: [(0, -1), (1, 2), (1, 3), (1, 4), (1, 5)], 66: [(1, -1)]}

            def step(i, j):
                T = U * i + j
                q = j % 2
                if unit(i, j, 0) and not (isinstance(i, int) and T == 0):
                    maxima(i, j)
                if unit(i, j, -4):
                    rope_add(T + 4, q, j % 4, groups[(j + 4) // 4 % 2])
                last = isinstance(i, int) and i == NP
                if unit(i, j, 2) and last:
                    o_low(T, j)
                if last:
                    for b, phase in extra.get(T, []):
                        second_t(b) if phase < 0 else second_norm(b, phase)
                m = (j + 2) // 2
                if j % 2 == 0 and (not isinstance(i, int) or (2 < B * i + m < B * NP)):
                    v_out(B * i + m, m % B, i + m // B)
                if j % 2 == 1 and unit(i, j, 5):
                    m = (j - 5) // 2
                    dve.wait_ge(s["b_wo"], B * i + m + 1)
                    b = m % B
                    y = yacc[:, 2 * b:2 * b + 2, :].rearrange("p t n -> p (t n)")
                    dve.tensor_tensor(y, y, output_bank(B * i + m)[:, :], ALU.add).then_inc(s["b_yadd"], 1)
                if isinstance(i, int):
                    for b, phase in while_exp.get(T, []):
                        second_norm(b, phase)
                if unit(i, j, 0):
                    dve.wait_ge(s["b_exp"], 2 * (T + 1))
                    dve.reciprocal(rs[:, q, :], rs[:, q, :]).then_inc(s["b_recip"], 1)
                    dve.wait_ge(s["b_recip"], T + 1)
                    dve.tensor_scalar(PR[:, q, 0:P], PR[:, q, 0:P], rs[:, q, 0:1], None, ALU.mult)
                    dve.tensor_scalar(PR[:, q, P:3 * P], PR[:, q, P:3 * P], rs[:, q, 1:2], None, ALU.mult).then_inc(s["b_norm"], 1)
                if unit(i, j, -LEAD):
                    c, g = chunk_at(j)
                    rope_cos(T + LEAD, q, c, groups[g])
                if unit(i, j, 2) and not last:
                    o_low(T, j)
                for b, phase in extra.get(T, []) if isinstance(i, int) and not last else []:
                    second_t(b) if phase < 0 else second_norm(b, phase)

            steps(dve, step)

            for phase in range(6):
                second_norm(2, phase, 2)
            second_t(2)
            second_t(3)

            Gt = lambda a, n: gate[:, a:a + n]
            V3 = lambda a: gate[:, a:a + 32].rearrange("p (t e) -> p t e", e=E)
            dve.wait_ge(s["c_logit"], 1)
            link(dve.tensor_copy(Gt(0, 32), bank[5][:, 0:32]))
            link(dve.tensor_reduce(Gt(96, 8), V3(0), AX.X, ALU.max))
            dve.tensor_tensor(V3(32), V3(0), Gt(96, 8).unsqueeze(2).to_broadcast([P, NT, E]), ALU.subtract).then_inc(s["c_gmax"], 1)
            dve.wait_ge(s["c_gexp"], 1)
            link(dve.tensor_reduce(Gt(104, 8), V3(64), AX.X, ALU.add))
            link(dve.reciprocal(Gt(112, 8), Gt(104, 8)))
            link(dve.tensor_tensor(V3(64), V3(64), Gt(112, 8).unsqueeze(2).to_broadcast([P, NT, E]), ALU.mult))
            Q4 = lambda a: gate[:, a:a + 128].rearrange("p (t e f) -> p t e f", e=E, f=E)
            for e in range(E):
                pe_ = V3(64)[:, :, e:e + 1].to_broadcast([P, NT, E])
                dve.tensor_tensor(Q4(120)[:, :, e, :], V3(64), pe_, ALU.is_gt)
                ins = dve.tensor_tensor(Q4(248)[:, :, e, :], V3(64), pe_, ALU.is_equal)
            link(ins)
            tie = cst_sb[:, C_TIE:C_TIE + 16].unsqueeze(1).to_broadcast([P, NT, 16])
            q16 = gate[:, 248:376].rearrange("p (t f) -> p t f", t=NT)
            link(dve.tensor_tensor(q16, q16, tie, ALU.mult))
            link(dve.tensor_tensor(Gt(120, 128), Gt(120, 128), Gt(248, 128), ALU.add))
            rank = gate[:, 408:440]
            link(dve.tensor_reduce(rank, gate[:, 120:248].rearrange("p (n f) -> p n f", f=E), AX.X, ALU.add))
            first, second = gate[:, 120:152], gate[:, 152:184]
            dve.tensor_scalar(first, rank, 0.0, None, ALU.is_equal)
            link(dve.tensor_scalar(second, rank, 1.0, None, ALU.is_equal))
            dve.tensor_tensor(Gt(184, 32), first, Gt(64, 32), ALU.mult)
            link(dve.tensor_tensor(Gt(216, 32), second, Gt(64, 32), ALU.mult))
            dve.tensor_reduce(Gt(376, 8), V3(184), AX.X, ALU.add)
            link(dve.tensor_reduce(Gt(384, 8), V3(216), AX.X, ALU.add))
            dve.tensor_tensor(Gt(392, 8), Gt(384, 8), Gt(376, 8), ALU.subtract).then_inc(s["c_gdiff"], 1)
            dve.wait_ge(s["c_gexp"], 2)
            link(dve.tensor_scalar(Gt(248, 8), Gt(400, 8), 1.0, None, ALU.add))
            link(dve.reciprocal(Gt(256, 8), Gt(248, 8)))
            link(dve.tensor_tensor(Gt(264, 8), Gt(256, 8), Gt(400, 8), ALU.mult))
            dve.tensor_tensor(V3(120), V3(120), Gt(256, 8).unsqueeze(2).to_broadcast([P, NT, E]), ALU.mult)
            link(dve.tensor_tensor(V3(152), V3(152), Gt(264, 8).unsqueeze(2).to_broadcast([P, NT, E]), ALU.mult))
            dve.tensor_tensor(Gt(0, 32), Gt(120, 32), Gt(152, 32), ALU.add).then_inc(s["c_comb"], 1)
            dve.wait_ge(s["c_combT_pe"], 1)
            dve.tensor_copy(combT[:, 0:4, :].rearrange("p t n -> p (t n)"), bank[4][0:E, :])
            dve.tensor_copy(combT[:, 4:8, :].rearrange("p t n -> p (t n)"), bank[5][0:E, :]).then_inc(s["c_combT"], 1)
            for b in range(B):
                dve.wait_ge(s["c_be"], b + 1)
                y = yacc[:, 2 * b:2 * b + 2, :].rearrange("p t n -> p (t n)")
                dve.tensor_tensor(y, y, bank[4 + b % 2][:, :], ALU.add).then_inc(s["c_init"], 1)
            dve.wait_ge(s["c_init"], B)

            for m in range(2 * E):
                c, e = divmod(m, E)
                for hf in range(2):
                    b = 2 * c + hf
                    dve.wait_ge(s["c_exp_pe"], 2 * m + hf + 1)
                    if m:
                        dve.wait_ge(s["c_acc"], 2 * (m - 1) + hf + 1)
                    for t in range(2):
                        n = 2 * b + t
                        ins = dve.scalar_tensor_tensor(yacc[:, n, :], out_bank(m, hf)[:, 256 * t:256 * (t + 1)],
                                                       gate[:, 4 * n + e:4 * n + e + 1], yacc[:, n, :], ALU.mult, ALU.add)
                    ins.then_inc(s["c_acc"], 1)
                    if e == E - 1:
                        dve.wait_ge(s["c_acc"], 2 * m + hf + 1)
                        y = yacc[:, 2 * b:2 * b + 2, :].rearrange("p t n -> p (t n)")
                        xb = x_sb[:, 2 * b:2 * b + 2, :].rearrange("p t n -> p (t n)")
                        dve.scalar_tensor_tensor(y, y, small[:, 97:98], xb, ALU.mult, ALU.add).then_inc(s["c_fin"], 1)

        @block.tensor
        def _(pe):
            pe.wait_ge(s["bf_ready"], 1)
            pe.wait_ge(s["d_cst"], 16)
            pe.wait_ge(s["kpack_ready"], 1)

            def k_turn(b):
                if b:
                    pe.wait_ge(s["m7_free"], b)
                for g in range(XG):
                    for t in range(2):
                        ins = pe.transpose(bank_bf[1][:, (2 * g + t) * P:(2 * g + t + 1) * P],
                                           kpack[:, (2 * b + t) * XG + g, :, :].rearrange("p s d -> p (s d)"), ident_bf)
                ins.then_inc(s["m7_pe"], 1)

            def q_turn(b, X, t):
                n = m6["Q", b, X, t]
                pe.wait_ge(s["qpack_ready"], 2 * b + X + 1)
                if n:
                    pe.wait_ge(s["m6_free"], n)
                for h in range(8):
                    ins = pe.transpose(bank_bf[0][:, h * P:(h + 1) * P], qpack[:, X, t, h, :, :].rearrange("p s d -> p (s d)"), ident_bf)
                ins.then_inc(s["m6_pe"], 1)

            def out_turn(b):
                n = m6["OT", b]
                pe.wait_ge(s["o_done"], 2 * XG * (b + 1))
                pe.wait_ge(s["m6_free"], n)
                for k in range(KT):
                    for t in range(2):
                        ins = pe.transpose(bank[6][:, (2 * k + t) * P:(2 * k + t + 1) * P], on[:, t, k * P:(k + 1) * P], ident)
                ins.then_inc(s["m6_pe"], 1)

            def out_project(b):
                n = m7["PJ", b]
                pe.wait_ge(s["m6_free"], m6["OT", b] + 1)
                pe.wait_ge(s["m7_free"], n)
                if b == 0:
                    pe.wait_ge(s["d_wout"], 16)
                for t in range(2):
                    for k in range(KT):
                        ins = pe.matmul(bank[7][:, 256 * t:256 * (t + 1)], onT[:, k, t, :], w_out_sb[:, k, :], start=(k == 0), stop=(k == 1))
                ins.then_inc(s["m7_pe"], 1)

            def norm_turn(b):
                n = m7["NT", b]
                pe.wait_ge(s["nh_ready"], b + 1)
                pe.wait_ge(s["m7_free"], n)
                for k in range(KT):
                    for t in range(2):
                        ins = pe.transpose(bank[7][:, (2 * k + t) * P:(2 * k + t + 1) * P], nh[:, t, k * P:(k + 1) * P], ident)
                ins.then_inc(s["m7_pe"], 1)

            def x_scores(p):
                b, k = divmod(p, XP)
                g, t, heads = piece(k)
                width = P * (t + 1)
                pe.wait_ge(s["m6_free"], m6["Q", b, k // 6, 1] + 1)
                if k == 0:
                    pe.wait_ge(s["m7_free"], b + 1)
                if p >= 2:
                    pe.wait_ge(s["s_exp"], p - 1)
                for n, h in enumerate(heads):
                    pe.matmul(S_B[p % 2][:, n * width:(n + 1) * width], qT[:, h // 8, t, h % 8, :], kT[:, b, g, 0:width], start=True, stop=False)
                    ins = pe.matmul(S_B[p % 2][:, (n + 1) * width - P:(n + 1) * width], ident_bf, mask_bf, start=False, stop=True)
                ins.then_inc(s["s_pe"], 1)

            def x_turn(p):
                pe.wait_ge(s["s_exp"], p + 1)
                if p >= 2:
                    pe.wait_ge(s[copier(p - 2)[0]], copier(p - 2)[1])
                for n in range(4):
                    ins = pe.transpose(PT_B[p % 2][:, n * P:(n + 1) * P], PR[:, p % 2, n * P:(n + 1) * P], ident)
                ins.then_inc(s["pt_pe"], 1)

            def x_values(p):
                b, k = divmod(p, XP)
                g, t, heads = piece(k)
                m = p // 3
                pe.wait_ge(s[copier(p)[0]], copier(p)[1])
                if p == 0:
                    pe.wait_ge(s["va_ready"], 1 + B)
                if t == 0 and m:
                    pe.wait_ge(s["oT_ready"], m)
                c = P * t
                for n, h in enumerate(heads):
                    for kt in range(t + 1):
                        a = VZ + VP * (XG * (2 * b + kt) + g) - 32 * (h % 4)
                        ins = pe.matmul(bank[4][:, c:c + P], room[:, a:a + P], PTs[:, p % 2, (n * (t + 1) + kt) * P:(n * (t + 1) + kt + 1) * P],
                                        start=(h % 4 == 0 and kt == 0), stop=(h % 4 == 3 and kt == t))
                ins.then_inc(s["pv_pe"], 1)

            def o_turn(m):
                pe.wait_ge(s["oT_ready"], m + 1)
                if m:
                    pe.wait_ge(s["o_done"], 2 * m)
                for t in range(2):
                    ins = pe.transpose(bank[5][:, t * P:(t + 1) * P], oT[:, m % 2, t * P:(t + 1) * P], ident)
                ins.then_inc(s["o_pe"], 1)

            k_turn(0)
            q_turn(0, 0, 0)
            k_turn(1)
            q_turn(0, 0, 1)
            k_turn(2)
            k_turn(3)
            for p in range(NPX + 3):
                b, k = divmod(p, XP)
                if p < NPX:
                    x_scores(p)
                    if k in (2, 3):
                        q_turn(b, 1, k - 2)
                    if k == 5 and b:
                        out_turn(b - 1)
                    if k == 6 and b:
                        out_project(b - 1)
                    if k in (7, 9) and b + 1 < B:
                        q_turn(b + 1, 0, (k - 7) // 2)
                if 2 <= p < NPX + 2:
                    x_turn(p - 2)
                if k == 1 and b >= 2:
                    norm_turn(b - 2)
                if p >= 6 and p % 3 == 0:
                    o_turn((p - 6) // 3)
                if p >= 3:
                    x_values(p - 3)

            def three(outp, pairs):
                n = 3 * len(pairs)
                m = 0
                for (aH, aL), (bH, bL) in pairs:
                    for l, r in ((aH, bL), (aL, bH), (aH, bH)):
                        ins = pe.matmul(outp, l, r, start=(m == 0), stop=(m == n - 1))
                        m += 1
                return ins

            def project_qk(n, q, c, g, guard):
                if guard:
                    pe.wait_ge(s["chunk_f"], n - 1)
                cut = slice(512 * g, 512 * (g + 1))
                three(O_B[q][:, :], [((wqkH[:, c, k, :], wqkL[:, c, k, :]), (hH[:, k, cut], hL[:, k, cut])) for k in range(KT)]).then_inc(s["chunk_pe"], 1)

            def project_v(m, b, guard):
                if guard:
                    pe.wait_ge(s["v_ready"], m)
                for t in range(2):
                    cut = slice((2 * b + t) * P, (2 * b + t + 1) * P)
                    ins = three(bank[6][:, 256 * t:256 * (t + 1)], [((hH[:, k, cut], hL[:, k, cut]), (wvH[:, k, :], wvL[:, k, :])) for k in range(KT)])
                ins.then_inc(s["v_pe"], 1)

            pe.wait_ge(s["h_ready"], 2)
            pe.wait_ge(s["wqk_ready"], 4)
            pe.wait_ge(s["oT_ready"], NPX // 3)
            project_qk(0, 0, 0, 0, False)
            o_turn(NPX // 3 - 1)
            out_turn(B - 1)
            project_qk(1, 1, 1, 0, False)
            out_project(B - 1)
            pe.wait_ge(s["wv_ready"], 1)
            pe.wait_ge(s["m6_free"], len(M6))
            project_v(0, 0, False)
            project_qk(2, 0, 2, 0, True)
            project_v(1, 1, True)
            project_qk(3, 1, 3, 0, True)
            norm_turn(B - 1)
            def scores(i, j):
                T = U * i + j
                b, r = j // 2, j % 2
                pe.wait_ge(s["split_low"], U * i + 4 * (j // 4) + 2 * r + 2)
                if unit(i, j, 2):
                    pe.wait_ge(s["b_max"], T - 1)
                first = slice(256 * b, 256 * b + P)
                pe.matmul(S_B[j % 2][:, 0:P], QT[:, 2 * r, first], QT[:, 2 * r + 1, first], start=True, stop=True)
                three(S_B[j % 2][:, P:3 * P], [([q_split[:, m, r, b, :] for m in range(2)],
                                                [k_split[:, m, r, 256 * b:256 * (b + 1)] for m in range(2)])]).then_inc(s["b_s"], 1)

            pe.wait_ge(s["h_ready"], 3)
            project_v(2, 2, True)
            pe.wait_ge(s["m7_free"], len(M7))
            pe.wait_ge(s["h_ready"], B)
            project_qk(4, 0, 0, 1, True)
            scores(0, 0)
            project_qk(5, 1, 1, 1, True)

            def step(i, j):
                T = U * i + j
                q = j % 2
                early = isinstance(i, int) and (T == 0 or T > NU - LEAD)
                if unit(i, j, 0) and not early:
                    scores(i, j)
                if isinstance(i, int) and NU - LEAD <= T < NU - 1:
                    scores(*divmod(T + 1, U))
                if unit(i, j, -LEAD):
                    if 2 <= j < 6:
                        pe.wait_ge(s["wqk_ready"], 4 * (i + 1) + j - 2 + 1)
                    c, g = chunk_at(j)
                    project_qk(T + LEAD, q, c, g, True)
                if unit(i, j, 1):
                    pe.wait_ge(s["b_norm"], T)
                    if unit(i, j, 2):
                        pe.wait_ge(s["b_ptcopy"], T - 1)
                    for n in range(3):
                        ins = pe.transpose(bank[2][:, n * P:(n + 1) * P], PR[:, 1 - q, n * P:(n + 1) * P], ident)
                    ins.then_inc(s["b_pt"], 1)
                if unit(i, j, 2):
                    u = (j - 2) % U
                    b, r = u // 2, u % 2
                    pe.wait_ge(s["b_ptcopy"], T - 1)
                    pe.wait_ge(s["v_ready"], 4 * i + (j - 2) // 2 + 1)
                    if unit(i, j, 3):
                        pe.wait_ge(s["b_oL"], T - 2)
                    pe.matmul(bank[3][:, 0:256], V[:, 2 * b, r * HD:(r + 1) * HD], PTs[:, q, 0:256], start=True, stop=False)
                    pe.matmul(bank[3][:, P:256], V[:, 2 * b + 1, r * HD:(r + 1) * HD], PTs[:, q, 256:384], start=False, stop=True).then_inc(s["b_pv"], 1)
                if v_event(i, j):
                    m = (j + 3) // 2
                    pe.wait_ge(s["wv_ready"], i + m // B + 1)
                    project_v(B * i + m, m % B, True)
                if j % 2 == 0 and unit(i, j, 4):
                    mo = (j - 4) // 2
                    pe.wait_ge(s["b_oL"], 8 * i + 2 * mo + 2)
                    pe.wait_ge(s["wo_ready"], i + mo // 4 + 1)
                    if not (isinstance(i, int) and (i == 0 and mo == 0 or B * i + mo == NU // 2 - 1)):
                        pe.wait_ge(s["b_yadd"], 4 * i + mo)
                    for t in range(2):
                        ins = three(output_bank(B * i + mo)[:, 256 * t:256 * (t + 1)],
                                    [((oH[:, mo % 2, r, t * P:(t + 1) * P], oL[:, mo % 2, r, t * P:(t + 1) * P]), (woH[:, r, :], woL[:, r, :])) for r in range(2)])
                    ins.then_inc(s["b_wo"], 1)

            def second_turn(b):
                pe.wait_ge(s["c_nh"], b + 1)
                if b:
                    pe.wait_ge(s["c_hT"], b)
                for k in range(KT):
                    for t in range(2):
                        ins = pe.transpose(bank[4][:, (2 * k + t) * P:(2 * k + t + 1) * P], second_nh[b % 2][:, t, k * P:(k + 1) * P], ident)
                ins.then_inc(s["c_tr"], 1)

            def step_and_turns(i, j):
                step(i, j)
                if isinstance(i, int) and i == NP and j in (1, 3):
                    second_turn(j // 2)

            steps(pe, step_and_turns)

            def middle_part(n, first, size):
                c, m = divmod(n, NE)
                cut = slice(512 * c + first, 512 * c + first + size)
                return three(bank[n % 2][:, first:first + size],
                             [((we1H[:, k, m * P:(m + 1) * P], we1L[:, k, m * P:(m + 1) * P]), (hH[:, k, cut], hL[:, k, cut])) for k in range(KT)])

            def middle(n):
                if n >= 2:
                    pe.wait_ge(s["c_gelu"], n - 1)
                if n == NE:
                    pe.wait_ge(s["c_h"], B)
                middle_part(n, 0, 512).then_inc(s["c_mid"], 1)

            def expert_out(m):
                c, e = divmod(m, E)
                pe.wait_ge(s["c_gL"], 2 * m + 2)
                if m < 2:
                    pe.wait_ge(s["b_yadd"], NU // 2)
                for hf in range(2):
                    if m >= 2:
                        pe.wait_ge(s["c_acc"], 2 * (m - 2) + hf + 1)
                    for t in range(2):
                        cut = slice((2 * hf + t) * P, (2 * hf + t + 1) * P)
                        ins = three(out_bank(m, hf)[:, 256 * t:256 * (t + 1)],
                                    [((GH[:, m % 2, k, cut], GL[:, m % 2, k, cut]), (we2H[:, 2 * e + k, :], we2L[:, 2 * e + k, :])) for k in range(IT)])
                    ins.then_inc(s["c_exp_pe"], 1)

            pe.wait_ge(s["we_ready"], NP)
            for b in range(2):
                pe.wait_ge(s["c_h"], b + 1)
                for n in range(2):
                    ins = middle_part(n, 256 * b, 256)
                    if b:
                        ins.then_inc(s["c_mid"], 1)
            second_turn(2)
            middle(2)
            second_turn(3)
            middle(3)
            expert_out(0)
            pe.wait_ge(s["c_hT"], B)
            pe.wait_ge(s["d_small"], 32)
            for n in range(NT):
                for k in range(KT):
                    ins = pe.matmul(bank[5][:, E * n:E * (n + 1)], h2T[:, k, n * P:(n + 1) * P], w_gate_sb[:, k, :], start=(k == 0), stop=(k == 1))
            ins.then_inc(s["c_logit"], 1)
            expert_out(1)
            middle(4)
            middle(5)
            pe.wait_ge(s["c_comb"], 1)
            for n in range(NT):
                ins = pe.transpose(bank[4 + n // 4][0:E, (n % 4) * P:(n % 4 + 1) * P], gate[:, E * n:E * (n + 1)], ident)
            ins.then_inc(s["c_combT_pe"], 1)
            middle(6)
            pe.wait_ge(s["c_combT"], 1)
            for b in range(B):
                if b >= 2:
                    pe.wait_ge(s["c_init"], b - 1)
                for t in range(2):
                    ins = pe.matmul(bank[4 + b % 2][:, 256 * t:256 * (t + 1)], combT[:, 2 * b + t, :], be2_sb[:, :], start=True, stop=True)
                ins.then_inc(s["c_be"], 1)
            for n in range(7, 2 * NE):
                middle(n)
                if n % 2:
                    expert_out((n - 3) // 2)
            expert_out(2 * E - 1)


def constants():
    f = np.float32
    c = np.zeros((P, C_END), f)
    c[:, C_ID:C_ID + P] = np.eye(P, dtype=f)
    above = np.triu(np.ones((P, P), f), 1)
    c[:, C_MASK + P:C_MASK + 256] = above * f(BIG)

    def angles(width):
        inv = f(1.0) / f(10000.0) ** (np.arange(0, width, 2, dtype=f) / f(width))
        a = np.arange(S, dtype=f)[:, None] * inv[None, :].astype(f)
        return np.cos(a).astype(f), np.sin(a).astype(f)

    co, si = angles(XD)
    for t in range(2):
        c[:, C_XCOS + t * XD:C_XCOS + (t + 1) * XD] = np.concatenate([co, co], 1)[t * P:(t + 1) * P]
        c[:, C_XSIN + t * XD:C_XSIN + (t + 1) * XD] = np.concatenate([-si, si], 1)[t * P:(t + 1) * P]
    co, si = angles(HD)
    scale = f(-1.0 / np.sqrt(HD))
    cos_t, sin_t = np.concatenate([co, co], 1).T, np.concatenate([-si, si], 1).T
    c[:, C_RCOSQ:C_RCOSQ + 256] = cos_t * scale
    c[:, C_RSINQ:C_RSINQ + 256] = sin_t * scale
    c[:, C_RCOSK:C_RCOSK + 256] = cos_t
    c[:, C_RSINK:C_RSINK + 256] = sin_t
    c[:, C_TIE:C_TIE + 16] = np.tril(np.ones((E, E), f), -1).reshape(1, 16)
    return c


def kernel(**inputs):
    import concourse.bacc as bacc
    from concourse.bass_utils import run_bass_kernel_spmd

    a = {k: np.ascontiguousarray(v) for k, v in inputs.items()}
    w = {k[7:]: v for k, v in a.items() if k.startswith("L0_ffn_")}

    def kxn(m, n):
        return m.reshape(n, P, *m.shape[1:]).swapaxes(0, 1)

    def col(v):
        return v.reshape(-1, P).T

    def pairs(m):
        return m.reshape(KT, P, NP, 256).transpose(2, 1, 0, 3)

    c = constants()
    arrays = {
        "x": a["x"],
        "ctx": a["ctx_512"],
        "cst": c,
        "cols": np.concatenate([col(w["bq"]), col(w["bk"]), col(w["ln1_w"]), col(w["ln1_b"]), col(w["ln2_w"]),
                                col(w["ln2_b"]), col(w["be1"])], 1),
        "rows": np.concatenate([a["L0_xattn_q_norm_w"], a["L0_xattn_k_norm_w"], w["bo"], a["g_xattn"], a["g_ffn"]])[None],
        "bv": w["bv"][None],
        "wqkv": np.stack([pairs(w["wq"]), pairs(w["wk"]), pairs(w["wv"])], 2),
        "wo": w["wo"].reshape(NP, 2, P, D).swapaxes(1, 2),
        "w_out_t": kxn(a["L0_xattn_w_out"].T, KT),
        "w_gate": kxn(w["w_gate"], KT),
        "be2": w["be2"],
        "we": np.concatenate([kxn(w["we1"].transpose(1, 0, 2).reshape(D, E * I), KT).reshape(P, -1),
                              kxn(w["we2"].reshape(E * I, D), NE).reshape(P, -1)], 1).reshape(P, NP, WE_CUT).swapaxes(0, 1),
    }
    nc = bacc.Bacc("TRN2", target_bir_lowering=False, num_devices=1)
    args, arrays = [], {f"in_{k}": np.ascontiguousarray(v) for k, v in arrays.items()}
    for name, v in arrays.items():
        args.append(nc.dram_tensor(name, v.shape, mybir.dt.from_np(v.dtype), kind="ExternalInput").ap())
    args.append(nc.dram_tensor("out_y", (B, S, D), F32, kind="ExternalOutput").ap())
    build_kernel(nc, *args)
    r = run_bass_kernel_spmd(nc, [arrays], core_ids=[0])
    return r.results[0]["out_y"]
```
